# Optimizing a Trainium2 kernel written in Bass

```python
import numpy as np
import jax
import jax.numpy as jnp

def _softmax(x, axis=-1):
    return jax.nn.softmax(x, axis=axis)

def _gelu(x):
    return jax.nn.gelu(x, approximate=True)

def _silu(x):
    return jax.nn.silu(x)

def _sigmoid(x):
    return jax.nn.sigmoid(x)

def _layernorm(x, axis=-1, eps=1e-05):
    m = jnp.mean(x, axis=axis, keepdims=True)
    v = jnp.var(x, axis=axis, keepdims=True)
    return (x - m) / jnp.sqrt(v + eps)

def _scatter_add(tgt, idx, src, axis=0):
    return tgt.at[idx].add(src)

def _segment_sum(src, seg, n):
    return jax.ops.segment_sum(src, seg, n)
kernel_name = 'mk_pixart_seq_d4_seqx_r4_6093ad'

def setup_inputs(seed: int=0):
    np.random.seed(seed)
    _w = jnp.asarray

    def _rec_inputs():
        import jax
        import jax.numpy as jnp
        _rk = jax.random.key(seed)
        x = -0.0002928 + 1 * jax.random.normal(jax.random.fold_in(_rk, 1), (8, 256, 256), jnp.float32)
        _lenS = 256 - jax.random.randint(jax.random.fold_in(_rk, 7), (8,), 0, max(1, 256 // 4) + 1, jnp.int32)
        _lenS2 = 77 - jax.random.randint(jax.random.fold_in(_rk, 8), (8,), 0, max(1, 77 // 4) + 1, jnp.int32)
        cond_1024 = 0.000887014 + 1.03683 * jax.random.normal(jax.random.fold_in(_rk, 11), (8, 256), jnp.float32)
        _ctx_1024P = jax.random.normal(jax.random.fold_in(_rk, 12), (8, 16, 256), jnp.float32)
        _ctx_1024c = jax.random.dirichlet(jax.random.fold_in(_rk, 512), 0.3 * jnp.ones((16,), jnp.float32), (8, 77))
        _ctx_1024t = jnp.einsum('bsk,bkd->bsd', _ctx_1024c, _ctx_1024P)
        _ctx_1024t = _ctx_1024t * jax.lax.rsqrt(jnp.mean(jnp.square(_ctx_1024t)) + 1e-12) * 0.953939
        ctx_1024 = -0.00606593 + 0.997213 * (_ctx_1024t + 0.3 * jax.random.normal(jax.random.fold_in(_rk, 612), (8, 77, 256), jnp.float32))
        _validS = jnp.arange(256)[None, :] < _lenS[:, None]
        _validS2 = jnp.arange(77)[None, :] < _lenS2[:, None]
        _causal = jnp.tril(jnp.ones((256, 256), dtype=bool))
        mask_BxS2_bf1 = jnp.ones((8, 77), dtype=bool)
        mask_SxS_bk0 = jnp.logical_not(jnp.broadcast_to(_validS[0:1, :], (256, 256)))
        return (x, cond_1024, ctx_1024, mask_BxS2_bf1, mask_SxS_bk0)
    x, cond_1024, ctx_1024, mask_BxS2_bf1, mask_SxS_bk0 = _rec_inputs()

    def _L0_xcond_setup():
        import jax, jax.numpy as jnp
        import numpy as np
        B, N, D, H, LC = (2, 256, 256, 16, 77)
        HD = D // H
        BLOCK = 16
        ROPE_BASE = 10000.0
        EPS = 1e-05

        def _block_diff_mask(n, block_size):
            idx = np.arange(2 * n)
            q = idx[:, None]
            kv = idx[None, :]
            fq = q >= n
            fkv = kv >= n
            bq = np.where(fq, (q - n) // block_size, q // block_size)
            bkv = np.where(fkv, (kv - n) // block_size, kv // block_size)
            block_diagonal = (bq == bkv) & (fq == fkv)
            offset_block_causal = (bq > bkv) & fkv & ~fq
            block_causal = (bq >= bkv) & fq & fkv
            return jnp.asarray(block_diagonal | offset_block_causal | block_causal)

        def _rope_tables(n):
            inv_freq = 1.0 / ROPE_BASE ** (np.arange(0, HD, 2, dtype=np.float32) / HD)
            freqs = np.outer(np.arange(n, dtype=np.float32), inv_freq)
            emb = np.concatenate([freqs, freqs], axis=-1)
            cos = jnp.asarray(np.cos(emb), jnp.float32)[None, :, None, :]
            sin = jnp.asarray(np.sin(emb), jnp.float32)[None, :, None, :]
            return (cos, sin)

        def _ln(x, w):
            xf = x.astype(jnp.float32)
            mu = jnp.mean(xf, axis=-1, keepdims=True)
            var = jnp.mean(jnp.square(xf - mu), axis=-1, keepdims=True)
            y = (xf - mu) * jax.lax.rsqrt(var + EPS)
            return y * w[None, None, :]

        def _apply_rope(t, cos, sin):
            t1, t2 = jnp.split(t, 2, axis=-1)
            rot = jnp.concatenate([-t2, t1], axis=-1)
            return t * cos + rot * sin

        def _attn(q, k, v, mask):
            scale = 1.0 / np.sqrt(HD)
            s = jnp.einsum('bqhd,bkhd->bhqk', q, k) * scale
            s = jnp.where(mask, s, jnp.finfo(s.dtype).min)
            a = jax.nn.softmax(s, axis=-1)
            return jnp.einsum('bhqk,bkhd->bqhd', a, v)
        key = jax.random.key(seed)
        ks = jax.random.split(key, 16)
        w = lambda k, shp: jax.random.normal(k, shp, jnp.float32) * 0.02
        inp = {'x': jax.random.normal(ks[0], (B, 2 * N, D), jnp.float32), 'cond_global': jax.random.normal(ks[1], (B, D), jnp.float32), 'cond_tokens': jax.random.normal(ks[2], (B, LC, D), jnp.float32), 'adaLN_W': w(ks[3], (D, 9 * D)), 'adaLN_b': w(ks[4], (9 * D,)), 'norm1_w': jnp.ones((D,), jnp.float32), 'qkv_W': w(ks[5], (D, 3 * D)), 'attn_out_W': w(ks[6], (D, D)), 'normc_w': jnp.ones((D,), jnp.float32), 'cq_W': w(ks[7], (D, D)), 'ck_W': w(ks[8], (D, D)), 'cv_W': w(ks[9], (D, D)), 'co_W': w(ks[10], (D, D)), 'norm2_w': jnp.ones((D,), jnp.float32), 'mlp_W1': w(ks[11], (D, 4 * D)), 'mlp_b1': w(ks[12], (4 * D,)), 'mlp_W2': w(ks[13], (4 * D, D)), 'mlp_b2': w(ks[14], (D,)), 'cond_kv_mask': jnp.ones((B, LC), bool), 'attn_mask': _block_diff_mask(N, BLOCK)}
        return inp
    _L0_xcond_all = _L0_xcond_setup()
    _L0_xcond_in = {k: v for k, v in _L0_xcond_all.items() if k in ('adaLN_W', 'adaLN_b', 'norm1_w', 'qkv_W', 'attn_out_W', 'normc_w', 'cq_W', 'ck_W', 'cv_W', 'co_W', 'norm2_w', 'mlp_W1', 'mlp_b1', 'mlp_W2', 'mlp_b2')}
    del _L0_xcond_all

    def _L1_xcond_setup():
        import jax, jax.numpy as jnp
        import numpy as np
        C = 256
        H = 16
        D = C // H
        WIN = 128
        SHIFT = 64
        TOPK = 16
        HID = 1024
        EPS = 1e-06

        def _ln(x):
            x32 = x.astype(jnp.float32)
            m = x32.mean(-1, keepdims=True)
            v = jnp.mean((x32 - m) ** 2, axis=-1, keepdims=True)
            return ((x32 - m) * jax.lax.rsqrt(v + EPS)).astype(x.dtype)

        def _self_attn(h, w_qkv, b_qkv, w_so, b_so):
            B, L, _ = h.shape
            qkv = h @ w_qkv + b_qkv
            qkv = jnp.roll(qkv, -SHIFT, axis=1)
            nw = L // WIN
            qkv = qkv.reshape(B, nw, WIN, 3, H, D)
            q, k, v = (qkv[:, :, :, 0], qkv[:, :, :, 1], qkv[:, :, :, 2])
            scores = jnp.einsum('bnqhd,bnkhd->bnhqk', q, k) / jnp.sqrt(jnp.float32(D)).astype(h.dtype)
            attn = jax.nn.softmax(scores, axis=-1)
            o = jnp.einsum('bnhqk,bnkhd->bnqhd', attn, v).reshape(B, L, C)
            o = jnp.roll(o, SHIFT, axis=1)
            return o @ w_so + b_so

        def _topk_cross_attn(h, ctx, w_q, b_q, w_kv, b_kv, w_co, b_co):
            B, L, _ = h.shape
            Lc = ctx.shape[1]
            q = (h @ w_q + b_q).reshape(B, L, H, D)
            kv = (ctx @ w_kv + b_kv).reshape(B, Lc, 2, H, D)
            k, v = (kv[:, :, 0], kv[:, :, 1])
            scores = jnp.einsum('bqhd,bkhd->bhqk', q, k) / jnp.sqrt(jnp.float32(D)).astype(h.dtype)
            top_s, top_i = jax.lax.top_k(scores, TOPK)
            attn = jax.nn.softmax(top_s, axis=-1)
            v_bh = jnp.transpose(v, (0, 2, 1, 3))
            vg = jnp.take_along_axis(v_bh[:, :, None, :, :], top_i[..., None], axis=3)
            o = jnp.einsum('bhqk,bhqkd->bqhd', attn, vg).reshape(B, L, C)
            return o @ w_co + b_co

        def _swiglu(h, w_m1, b_m1, w_m2, b_m2):
            u = h @ w_m1 + b_m1
            a, b = (u[..., :HID], u[..., HID:])
            return jax.nn.silu(a) * b @ w_m2 + b_m2
        key = jax.random.key(seed)
        ks = jax.random.split(key, 24)
        s = 0.02
        inp = {'x': jax.random.normal(ks[0], (2, 1024, C), jnp.float32), 'mod': jax.random.normal(ks[1], (2, C), jnp.float32), 'context': jax.random.normal(ks[2], (2, 256, C), jnp.float32), 'w_ada': jax.random.normal(ks[3], (C, 9 * C), jnp.float32) * s, 'b_ada': jnp.zeros((9 * C,), jnp.float32), 'w_qkv': jax.random.normal(ks[4], (C, 3 * C), jnp.float32) * s, 'b_qkv': jnp.zeros((3 * C,), jnp.float32), 'w_so': jax.random.normal(ks[5], (C, C), jnp.float32) * s, 'b_so': jnp.zeros((C,), jnp.float32), 'w_q': jax.random.normal(ks[6], (C, C), jnp.float32) * s, 'b_q': jnp.zeros((C,), jnp.float32), 'w_kv': jax.random.normal(ks[7], (C, 2 * C), jnp.float32) * s, 'b_kv': jnp.zeros((2 * C,), jnp.float32), 'w_co': jax.random.normal(ks[8], (C, C), jnp.float32) * s, 'b_co': jnp.zeros((C,), jnp.float32), 'w_m1': jax.random.normal(ks[9], (C, 2 * HID), jnp.float32) * s, 'b_m1': jnp.zeros((2 * HID,), jnp.float32), 'w_m2': jax.random.normal(ks[10], (HID, C), jnp.float32) * s, 'b_m2': jnp.zeros((C,), jnp.float32)}
        return inp
    _L1_xcond_all = _L1_xcond_setup()
    _L1_xcond_in = {k: v for k, v in _L1_xcond_all.items() if k in ('w_ada', 'b_ada', 'w_qkv', 'b_qkv', 'w_so', 'b_so', 'w_q', 'b_q', 'w_kv', 'b_kv', 'w_co', 'b_co', 'w_m1', 'b_m1', 'w_m2', 'b_m2')}
    del _L1_xcond_all

    def _L2_xcond_setup():
        import jax, jax.numpy as jnp
        import numpy as np
        LN_EPS = 1e-06

        def _ln(x):
            mu = jnp.mean(x, axis=-1, keepdims=True)
            var = jnp.var(x, axis=-1, keepdims=True)
            return (x - mu) * jax.lax.rsqrt(var + LN_EPS)
        key = jax.random.key(seed)
        H, NH = (256, 16)
        B, N, S = (4, 256, 77)
        MLP = int(H * 4.0)
        ks = jax.random.split(key, 20)
        s = 1.0 / np.sqrt(H)
        return {'x': jax.random.normal(ks[0], (B, N, H), jnp.float32), 'c': jax.random.normal(ks[1], (B, H), jnp.float32), 'context': jax.random.normal(ks[2], (B, S, H), jnp.float32), 'W_mod': jax.random.normal(ks[3], (H, 6 * H), jnp.float32) * s, 'b_mod': jnp.zeros((6 * H,), jnp.float32), 'W_qkv': jax.random.normal(ks[4], (H, 3 * H), jnp.float32) * s, 'b_qkv': jnp.zeros((3 * H,), jnp.float32), 'W_proj': jax.random.normal(ks[5], (H, H), jnp.float32) * s, 'b_proj': jnp.zeros((H,), jnp.float32), 'W_qc': jax.random.normal(ks[6], (H, H), jnp.float32) * s, 'b_qc': jnp.zeros((H,), jnp.float32), 'W_kvc': jax.random.normal(ks[7], (H, 2 * H), jnp.float32) * s, 'b_kvc': jnp.zeros((2 * H,), jnp.float32), 'W_cproj': jax.random.normal(ks[8], (H, H), jnp.float32) * s, 'b_cproj': jnp.zeros((H,), jnp.float32), 'W_mlp1': jax.random.normal(ks[9], (H, MLP), jnp.float32) * s, 'b_mlp1': jnp.zeros((MLP,), jnp.float32), 'W_mlp2': jax.random.normal(ks[10], (MLP, H), jnp.float32) * (1.0 / np.sqrt(MLP)), 'b_mlp2': jnp.zeros((H,), jnp.float32)}
    _L2_xcond_all = _L2_xcond_setup()
    _L2_xcond_in = {k: v for k, v in _L2_xcond_all.items() if k in ('W_mod', 'b_mod', 'W_qkv', 'b_qkv', 'W_proj', 'b_proj', 'W_qc', 'b_qc', 'W_kvc', 'b_kvc', 'W_cproj', 'b_cproj', 'W_mlp1', 'b_mlp1', 'W_mlp2', 'b_mlp2')}
    del _L2_xcond_all

    def _L3_xcond_setup():
        import jax, jax.numpy as jnp
        import numpy as np
        H = 256
        RH = 2 * H
        E = 3
        B, T, P = (8, 512, 64)
        LN_EPS = 1e-05

        def _layer_norm(x, gamma, beta):
            mu = jnp.mean(x, axis=-1, keepdims=True)
            var = jnp.mean(jnp.square(x - mu), axis=-1, keepdims=True)
            return (x - mu) * jax.lax.rsqrt(var + LN_EPS) * gamma + beta
        key = jax.random.key(seed)
        ks = jax.random.split(key, 24)
        s = lambda fan_in: 1.0 / np.sqrt(fan_in)
        inp = {'mix_hidden_states': jax.random.normal(ks[0], (B, T, H), jnp.float32), 'global_anchor': jax.random.normal(ks[1], (B, H), jnp.float32), 'prototype_bank': jax.random.normal(ks[2], (B, P, H), jnp.float32), 'ln_gamma': jnp.ones((H,), jnp.float32), 'ln_beta': jnp.zeros((H,), jnp.float32), 'Wq': jax.random.normal(ks[3], (H, H), jnp.float32) * s(H), 'Wk': jax.random.normal(ks[4], (H, H), jnp.float32) * s(H), 'Wv': jax.random.normal(ks[5], (H, H), jnp.float32) * s(H), 'router_W': jax.random.normal(ks[6], (3 * H, E), jnp.float32) * s(3 * H), 'router_b': jnp.zeros((E,), jnp.float32), 'e_w1': jax.random.normal(ks[7], (E, 3 * H, RH), jnp.float32) * s(3 * H), 'e_b1': jnp.zeros((E, RH), jnp.float32), 'e_w2': jax.random.normal(ks[8], (E, RH, H), jnp.float32) * s(RH), 'e_b2': jnp.zeros((E, H), jnp.float32), 'gate_w1': jax.random.normal(ks[9], (3 * H, H), jnp.float32) * s(3 * H), 'gate_b1': jnp.zeros((H,), jnp.float32), 'gate_w2': jax.random.normal(ks[10], (H, H), jnp.float32) * s(H), 'gate_b2': jnp.zeros((H,), jnp.float32), 'out_w': jax.random.normal(ks[11], (H, H), jnp.float32) * s(H), 'out_b': jnp.zeros((H,), jnp.float32)}
        return inp
    _L3_xcond_all = _L3_xcond_setup()
    _L3_xcond_in = {k: v for k, v in _L3_xcond_all.items() if k in ('ln_gamma', 'ln_beta', 'Wq', 'Wk', 'Wv', 'router_W', 'router_b', 'e_w1', 'e_b1', 'e_w2', 'e_b2', 'gate_w1', 'gate_b1', 'gate_w2', 'gate_b2', 'out_w', 'out_b')}
    del _L3_xcond_all
    return {'x': x, 'cond_1024': cond_1024, 'ctx_1024': ctx_1024, 'mask_BxS2_bf1': mask_BxS2_bf1, 'mask_SxS_bk0': mask_SxS_bk0, 'L0_xcond_adaLN_W': _L0_xcond_in['adaLN_W'], 'L0_xcond_adaLN_b': _L0_xcond_in['adaLN_b'], 'L0_xcond_norm1_w': _L0_xcond_in['norm1_w'], 'L0_xcond_qkv_W': _L0_xcond_in['qkv_W'], 'L0_xcond_attn_out_W': _L0_xcond_in['attn_out_W'], 'L0_xcond_normc_w': _L0_xcond_in['normc_w'], 'L0_xcond_cq_W': _L0_xcond_in['cq_W'], 'L0_xcond_ck_W': _L0_xcond_in['ck_W'], 'L0_xcond_cv_W': _L0_xcond_in['cv_W'], 'L0_xcond_co_W': _L0_xcond_in['co_W'], 'L0_xcond_norm2_w': _L0_xcond_in['norm2_w'], 'L0_xcond_mlp_W1': _L0_xcond_in['mlp_W1'], 'L0_xcond_mlp_b1': _L0_xcond_in['mlp_b1'], 'L0_xcond_mlp_W2': _L0_xcond_in['mlp_W2'], 'L0_xcond_mlp_b2': _L0_xcond_in['mlp_b2'], 'L1_xcond_w_ada': _L1_xcond_in['w_ada'], 'L1_xcond_b_ada': _L1_xcond_in['b_ada'], 'L1_xcond_w_qkv': _L1_xcond_in['w_qkv'], 'L1_xcond_b_qkv': _L1_xcond_in['b_qkv'], 'L1_xcond_w_so': _L1_xcond_in['w_so'], 'L1_xcond_b_so': _L1_xcond_in['b_so'], 'L1_xcond_w_q': _L1_xcond_in['w_q'], 'L1_xcond_b_q': _L1_xcond_in['b_q'], 'L1_xcond_w_kv': _L1_xcond_in['w_kv'], 'L1_xcond_b_kv': _L1_xcond_in['b_kv'], 'L1_xcond_w_co': _L1_xcond_in['w_co'], 'L1_xcond_b_co': _L1_xcond_in['b_co'], 'L1_xcond_w_m1': _L1_xcond_in['w_m1'], 'L1_xcond_b_m1': _L1_xcond_in['b_m1'], 'L1_xcond_w_m2': _L1_xcond_in['w_m2'], 'L1_xcond_b_m2': _L1_xcond_in['b_m2'], 'L2_xcond_W_mod': _L2_xcond_in['W_mod'], 'L2_xcond_b_mod': _L2_xcond_in['b_mod'], 'L2_xcond_W_qkv': _L2_xcond_in['W_qkv'], 'L2_xcond_b_qkv': _L2_xcond_in['b_qkv'], 'L2_xcond_W_proj': _L2_xcond_in['W_proj'], 'L2_xcond_b_proj': _L2_xcond_in['b_proj'], 'L2_xcond_W_qc': _L2_xcond_in['W_qc'], 'L2_xcond_b_qc': _L2_xcond_in['b_qc'], 'L2_xcond_W_kvc': _L2_xcond_in['W_kvc'], 'L2_xcond_b_kvc': _L2_xcond_in['b_kvc'], 'L2_xcond_W_cproj': _L2_xcond_in['W_cproj'], 'L2_xcond_b_cproj': _L2_xcond_in['b_cproj'], 'L2_xcond_W_mlp1': _L2_xcond_in['W_mlp1'], 'L2_xcond_b_mlp1': _L2_xcond_in['b_mlp1'], 'L2_xcond_W_mlp2': _L2_xcond_in['W_mlp2'], 'L2_xcond_b_mlp2': _L2_xcond_in['b_mlp2'], 'L3_xcond_ln_gamma': _L3_xcond_in['ln_gamma'], 'L3_xcond_ln_beta': _L3_xcond_in['ln_beta'], 'L3_xcond_Wq': _L3_xcond_in['Wq'], 'L3_xcond_Wk': _L3_xcond_in['Wk'], 'L3_xcond_Wv': _L3_xcond_in['Wv'], 'L3_xcond_router_W': _L3_xcond_in['router_W'], 'L3_xcond_router_b': _L3_xcond_in['router_b'], 'L3_xcond_e_w1': _L3_xcond_in['e_w1'], 'L3_xcond_e_b1': _L3_xcond_in['e_b1'], 'L3_xcond_e_w2': _L3_xcond_in['e_w2'], 'L3_xcond_e_b2': _L3_xcond_in['e_b2'], 'L3_xcond_gate_w1': _L3_xcond_in['gate_w1'], 'L3_xcond_gate_b1': _L3_xcond_in['gate_b1'], 'L3_xcond_gate_w2': _L3_xcond_in['gate_w2'], 'L3_xcond_gate_b2': _L3_xcond_in['gate_b2'], 'L3_xcond_out_w': _L3_xcond_in['out_w'], 'L3_xcond_out_b': _L3_xcond_in['out_b']}

def reference(x, cond_1024, ctx_1024, mask_BxS2_bf1, mask_SxS_bk0, L0_xcond_adaLN_W, L0_xcond_adaLN_b, L0_xcond_norm1_w, L0_xcond_qkv_W, L0_xcond_attn_out_W, L0_xcond_normc_w, L0_xcond_cq_W, L0_xcond_ck_W, L0_xcond_cv_W, L0_xcond_co_W, L0_xcond_norm2_w, L0_xcond_mlp_W1, L0_xcond_mlp_b1, L0_xcond_mlp_W2, L0_xcond_mlp_b2, L1_xcond_w_ada, L1_xcond_b_ada, L1_xcond_w_qkv, L1_xcond_b_qkv, L1_xcond_w_so, L1_xcond_b_so, L1_xcond_w_q, L1_xcond_b_q, L1_xcond_w_kv, L1_xcond_b_kv, L1_xcond_w_co, L1_xcond_b_co, L1_xcond_w_m1, L1_xcond_b_m1, L1_xcond_w_m2, L1_xcond_b_m2, L2_xcond_W_mod, L2_xcond_b_mod, L2_xcond_W_qkv, L2_xcond_b_qkv, L2_xcond_W_proj, L2_xcond_b_proj, L2_xcond_W_qc, L2_xcond_b_qc, L2_xcond_W_kvc, L2_xcond_b_kvc, L2_xcond_W_cproj, L2_xcond_b_cproj, L2_xcond_W_mlp1, L2_xcond_b_mlp1, L2_xcond_W_mlp2, L2_xcond_b_mlp2, L3_xcond_ln_gamma, L3_xcond_ln_beta, L3_xcond_Wq, L3_xcond_Wk, L3_xcond_Wv, L3_xcond_router_W, L3_xcond_router_b, L3_xcond_e_w1, L3_xcond_e_b1, L3_xcond_e_w2, L3_xcond_e_b2, L3_xcond_gate_w1, L3_xcond_gate_b1, L3_xcond_gate_w2, L3_xcond_gate_b2, L3_xcond_out_w, L3_xcond_out_b):
    import jax
    import jax.numpy as jnp

    def _L0_xcond_ref(x, cond_global, cond_tokens, adaLN_W, adaLN_b, norm1_w, qkv_W, attn_out_W, normc_w, cq_W, ck_W, cv_W, co_W, norm2_w, mlp_W1, mlp_b1, mlp_W2, mlp_b2, cond_kv_mask, attn_mask):
        import jax, jax.numpy as jnp
        import numpy as np
        B, N, D, H, LC = (2, 256, 256, 16, 77)
        HD = D // H
        BLOCK = 16
        ROPE_BASE = 10000.0
        EPS = 1e-05

        def _block_diff_mask(n, block_size):
            idx = np.arange(2 * n)
            q = idx[:, None]
            kv = idx[None, :]
            fq = q >= n
            fkv = kv >= n
            bq = np.where(fq, (q - n) // block_size, q // block_size)
            bkv = np.where(fkv, (kv - n) // block_size, kv // block_size)
            block_diagonal = (bq == bkv) & (fq == fkv)
            offset_block_causal = (bq > bkv) & fkv & ~fq
            block_causal = (bq >= bkv) & fq & fkv
            return jnp.asarray(block_diagonal | offset_block_causal | block_causal)

        def _rope_tables(n):
            inv_freq = 1.0 / ROPE_BASE ** (np.arange(0, HD, 2, dtype=np.float32) / HD)
            freqs = np.outer(np.arange(n, dtype=np.float32), inv_freq)
            emb = np.concatenate([freqs, freqs], axis=-1)
            cos = jnp.asarray(np.cos(emb), jnp.float32)[None, :, None, :]
            sin = jnp.asarray(np.sin(emb), jnp.float32)[None, :, None, :]
            return (cos, sin)

        def _ln(x, w):
            xf = x.astype(jnp.float32)
            mu = jnp.mean(xf, axis=-1, keepdims=True)
            var = jnp.mean(jnp.square(xf - mu), axis=-1, keepdims=True)
            y = (xf - mu) * jax.lax.rsqrt(var + EPS)
            return y * w[None, None, :]

        def _apply_rope(t, cos, sin):
            t1, t2 = jnp.split(t, 2, axis=-1)
            rot = jnp.concatenate([-t2, t1], axis=-1)
            return t * cos + rot * sin

        def _attn(q, k, v, mask):
            scale = 1.0 / np.sqrt(HD)
            s = jnp.einsum('bqhd,bkhd->bhqk', q, k) * scale
            s = jnp.where(mask, s, jnp.finfo(s.dtype).min)
            a = jax.nn.softmax(s, axis=-1)
            return jnp.einsum('bhqk,bkhd->bqhd', a, v)
        b, s, d = x.shape
        n = s // 2
        mod = (cond_global @ adaLN_W + adaLN_b)[:, None, :]
        sh_msa, sc_msa, g_msa, sh_x, sc_x, g_x, sh_mlp, sc_mlp, g_mlp = jnp.split(mod, 9, axis=-1)
        x_norm = _ln(x, norm1_w) * (1 + sc_msa) + sh_msa
        cos, sin = _rope_tables(n)

        def qkv(h):
            t = (h @ qkv_W).reshape(b, n, 3, H, HD)
            q, k, v = (t[:, :, 0], t[:, :, 1], t[:, :, 2])
            return (_apply_rope(q, cos, sin), _apply_rope(k, cos, sin), v)
        q1, k1, v1 = qkv(x_norm[:, :n])
        q2, k2, v2 = qkv(x_norm[:, n:])
        q = jnp.concatenate([q1, q2], axis=1)
        k = jnp.concatenate([k1, k2], axis=1)
        v = jnp.concatenate([v1, v2], axis=1)
        self_out = _attn(q, k, v, attn_mask[None, None]).reshape(b, s, d) @ attn_out_W
        x = x + g_msa * self_out
        xc = _ln(x, normc_w) * (1 + sc_x) + sh_x
        qc = (xc @ cq_W).reshape(b, s, H, HD)
        kc = (cond_tokens @ ck_W).reshape(b, LC, H, HD)
        vc = (cond_tokens @ cv_W).reshape(b, LC, H, HD)
        cross = _attn(qc, kc, vc, cond_kv_mask[:, None, None, :]).reshape(b, s, d) @ co_W
        x = x + g_x * cross
        xm = _ln(x, norm2_w) * (1 + sc_mlp) + sh_mlp
        h = jax.nn.gelu(xm @ mlp_W1 + mlp_b1, approximate=True)
        mlp_out = h @ mlp_W2 + mlp_b2
        return x + g_mlp * mlp_out

    def _L1_xcond_ref(x, mod, context, w_ada, b_ada, w_qkv, b_qkv, w_so, b_so, w_q, b_q, w_kv, b_kv, w_co, b_co, w_m1, b_m1, w_m2, b_m2):
        import jax, jax.numpy as jnp
        import numpy as np
        C = 256
        H = 16
        D = C // H
        WIN = 128
        SHIFT = 64
        TOPK = 16
        HID = 1024
        EPS = 1e-06

        def _ln(x):
            x32 = x.astype(jnp.float32)
            m = x32.mean(-1, keepdims=True)
            v = jnp.mean((x32 - m) ** 2, axis=-1, keepdims=True)
            return ((x32 - m) * jax.lax.rsqrt(v + EPS)).astype(x.dtype)

        def _self_attn(h, w_qkv, b_qkv, w_so, b_so):
            B, L, _ = h.shape
            qkv = h @ w_qkv + b_qkv
            qkv = jnp.roll(qkv, -SHIFT, axis=1)
            nw = L // WIN
            qkv = qkv.reshape(B, nw, WIN, 3, H, D)
            q, k, v = (qkv[:, :, :, 0], qkv[:, :, :, 1], qkv[:, :, :, 2])
            scores = jnp.einsum('bnqhd,bnkhd->bnhqk', q, k) / jnp.sqrt(jnp.float32(D)).astype(h.dtype)
            attn = jax.nn.softmax(scores, axis=-1)
            o = jnp.einsum('bnhqk,bnkhd->bnqhd', attn, v).reshape(B, L, C)
            o = jnp.roll(o, SHIFT, axis=1)
            return o @ w_so + b_so

        def _topk_cross_attn(h, ctx, w_q, b_q, w_kv, b_kv, w_co, b_co):
            B, L, _ = h.shape
            Lc = ctx.shape[1]
            q = (h @ w_q + b_q).reshape(B, L, H, D)
            kv = (ctx @ w_kv + b_kv).reshape(B, Lc, 2, H, D)
            k, v = (kv[:, :, 0], kv[:, :, 1])
            scores = jnp.einsum('bqhd,bkhd->bhqk', q, k) / jnp.sqrt(jnp.float32(D)).astype(h.dtype)
            top_s, top_i = jax.lax.top_k(scores, TOPK)
            attn = jax.nn.softmax(top_s, axis=-1)
            v_bh = jnp.transpose(v, (0, 2, 1, 3))
            vg = jnp.take_along_axis(v_bh[:, :, None, :, :], top_i[..., None], axis=3)
            o = jnp.einsum('bhqk,bhqkd->bqhd', attn, vg).reshape(B, L, C)
            return o @ w_co + b_co

        def _swiglu(h, w_m1, b_m1, w_m2, b_m2):
            u = h @ w_m1 + b_m1
            a, b = (u[..., :HID], u[..., HID:])
            return jax.nn.silu(a) * b @ w_m2 + b_m2
        m = jax.nn.silu(mod) @ w_ada + b_ada
        sh_msa, sc_msa, g_msa, sh_mca, sc_mca, g_mca, sh_mlp, sc_mlp, g_mlp = [m[:, i * C:(i + 1) * C][:, None, :] for i in range(9)]
        h = _ln(x) * (1 + sc_msa) + sh_msa
        h = _self_attn(h, w_qkv, b_qkv, w_so, b_so)
        x = x + h * g_msa
        h = _ln(x) * (1 + sc_mca) + sh_mca
        h = _topk_cross_attn(h, context, w_q, b_q, w_kv, b_kv, w_co, b_co)
        x = x + h * g_mca
        h = _ln(x) * (1 + sc_mlp) + sh_mlp
        h = _swiglu(h, w_m1, b_m1, w_m2, b_m2)
        x = x + h * g_mlp
        return x

    def _L2_xcond_ref(x, c, context, W_mod, b_mod, W_qkv, b_qkv, W_proj, b_proj, W_qc, b_qc, W_kvc, b_kvc, W_cproj, b_cproj, W_mlp1, b_mlp1, W_mlp2, b_mlp2):
        import jax, jax.numpy as jnp
        import numpy as np
        LN_EPS = 1e-06

        def _ln(x):
            mu = jnp.mean(x, axis=-1, keepdims=True)
            var = jnp.var(x, axis=-1, keepdims=True)
            return (x - mu) * jax.lax.rsqrt(var + LN_EPS)
        B, N, H = x.shape
        NH = 16
        hd = H // NH
        scale = hd ** (-0.5)
        c_proj = jax.nn.silu(c) @ W_mod + b_mod
        shift_a, scale_a, gate_a, shift_m, scale_m, gate_m = jnp.split(c_proj, 6, axis=-1)

        def modulate(t, shift, sc):
            return t * (1 + sc[:, None]) + shift[:, None]
        x_norm = modulate(_ln(x), shift_a, scale_a)
        qkv = x_norm @ W_qkv + b_qkv
        q, k, v = jnp.split(qkv, 3, axis=-1)
        q = q.reshape(B, N, NH, hd).transpose(0, 2, 1, 3)
        k = k.reshape(B, N, NH, hd).transpose(0, 2, 1, 3)
        v = v.reshape(B, N, NH, hd).transpose(0, 2, 1, 3)
        attn_w = jax.nn.softmax(jnp.einsum('bhqd,bhkd->bhqk', q, k) * scale, axis=-1)
        attn_out = jnp.einsum('bhqk,bhkd->bhqd', attn_w, v)
        attn_out = attn_out.transpose(0, 2, 1, 3).reshape(B, N, H)
        attn_out = attn_out @ W_proj + b_proj
        x = x + gate_a[:, None] * attn_out
        S = context.shape[1]
        q_c = _ln(x) @ W_qc + b_qc
        kv_c = _ln(context) @ W_kvc + b_kvc
        k_c, v_c = jnp.split(kv_c, 2, axis=-1)
        q_c = q_c.reshape(B, N, NH, hd).transpose(0, 2, 1, 3)
        k_c = k_c.reshape(B, S, NH, hd).transpose(0, 2, 1, 3)
        v_c = v_c.reshape(B, S, NH, hd).transpose(0, 2, 1, 3)
        c_attn_w = jax.nn.softmax(jnp.einsum('bhqd,bhsd->bhqs', q_c, k_c) * scale, axis=-1)
        c_attn_out = jnp.einsum('bhqs,bhsd->bhqd', c_attn_w, v_c)
        c_attn_out = c_attn_out.transpose(0, 2, 1, 3).reshape(B, N, H)
        c_attn_out = c_attn_out @ W_cproj + b_cproj
        x = x + c_attn_out
        x_norm2 = modulate(_ln(x), shift_m, scale_m)
        h = jax.nn.gelu(x_norm2 @ W_mlp1 + b_mlp1)
        h = h @ W_mlp2 + b_mlp2
        x = x + gate_m[:, None] * h
        return x

    def _L3_xcond_ref(mix_hidden_states, global_anchor, prototype_bank, ln_gamma, ln_beta, Wq, Wk, Wv, router_W, router_b, e_w1, e_b1, e_w2, e_b2, gate_w1, gate_b1, gate_w2, gate_b2, out_w, out_b):
        import jax, jax.numpy as jnp
        import numpy as np
        H = 256
        RH = 2 * H
        E = 3
        B, T, P = (8, 512, 64)
        LN_EPS = 1e-05

        def _layer_norm(x, gamma, beta):
            mu = jnp.mean(x, axis=-1, keepdims=True)
            var = jnp.mean(jnp.square(x - mu), axis=-1, keepdims=True)
            return (x - mu) * jax.lax.rsqrt(var + LN_EPS) * gamma + beta
        x = mix_hidden_states
        nx = _layer_norm(x, ln_gamma, ln_beta)
        q = nx @ Wq
        k = prototype_bank @ Wk
        v = prototype_bank @ Wv
        scores = jnp.einsum('bth,bph->btp', q, k) * H ** (-0.5)
        weights = jax.nn.softmax(scores, axis=-1)
        evidence = jnp.einsum('btp,bph->bth', weights, v)
        anchor = jnp.broadcast_to(global_anchor[:, None, :], nx.shape)
        combined = jnp.concatenate([nx, evidence, anchor], axis=-1)
        router_logits = combined @ router_W + router_b
        router_probs = jax.nn.softmax(router_logits, axis=-1)
        h = jax.nn.silu(jnp.einsum('btc,ecr->bter', combined, e_w1) + e_b1)
        expert_out = jnp.einsum('bter,erh->bteh', h, e_w2) + e_b2
        routed = jnp.sum(expert_out * router_probs[..., None], axis=-2)
        g = jax.nn.sigmoid(jax.nn.silu(combined @ gate_w1 + gate_b1) @ gate_w2 + gate_b2)
        refined_delta = g * (routed @ out_w + out_b)
        return x + refined_delta
    x = _L0_xcond_ref(x, cond_1024, ctx_1024, L0_xcond_adaLN_W, L0_xcond_adaLN_b, L0_xcond_norm1_w, L0_xcond_qkv_W, L0_xcond_attn_out_W, L0_xcond_normc_w, L0_xcond_cq_W, L0_xcond_ck_W, L0_xcond_cv_W, L0_xcond_co_W, L0_xcond_norm2_w, L0_xcond_mlp_W1, L0_xcond_mlp_b1, L0_xcond_mlp_W2, L0_xcond_mlp_b2, mask_BxS2_bf1, mask_SxS_bk0)
    x = _L1_xcond_ref(x, cond_1024, ctx_1024, L1_xcond_w_ada, L1_xcond_b_ada, L1_xcond_w_qkv, L1_xcond_b_qkv, L1_xcond_w_so, L1_xcond_b_so, L1_xcond_w_q, L1_xcond_b_q, L1_xcond_w_kv, L1_xcond_b_kv, L1_xcond_w_co, L1_xcond_b_co, L1_xcond_w_m1, L1_xcond_b_m1, L1_xcond_w_m2, L1_xcond_b_m2)
    x = _L2_xcond_ref(x, cond_1024, ctx_1024, L2_xcond_W_mod, L2_xcond_b_mod, L2_xcond_W_qkv, L2_xcond_b_qkv, L2_xcond_W_proj, L2_xcond_b_proj, L2_xcond_W_qc, L2_xcond_b_qc, L2_xcond_W_kvc, L2_xcond_b_kvc, L2_xcond_W_cproj, L2_xcond_b_cproj, L2_xcond_W_mlp1, L2_xcond_b_mlp1, L2_xcond_W_mlp2, L2_xcond_b_mlp2)
    x = _L3_xcond_ref(x, cond_1024, ctx_1024, L3_xcond_ln_gamma, L3_xcond_ln_beta, L3_xcond_Wq, L3_xcond_Wk, L3_xcond_Wv, L3_xcond_router_W, L3_xcond_router_b, L3_xcond_e_w1, L3_xcond_e_b1, L3_xcond_e_w2, L3_xcond_e_b2, L3_xcond_gate_w1, L3_xcond_gate_b1, L3_xcond_gate_w2, L3_xcond_gate_b2, L3_xcond_out_w, L3_xcond_out_b)
    return x

_drawn_inputs = setup_inputs


def setup_inputs(seed=0):
    import zlib

    import numpy as np

    out = dict(_drawn_inputs(seed))
    spreads = {'L0_xcond_norm1_w': (1.0, 0.6),
     'L0_xcond_normc_w': (1.0, 0.6),
     'L0_xcond_norm2_w': (1.0, 0.6),
     'L1_xcond_b_ada': (0.0, 0.447),
     'L1_xcond_b_qkv': (0.0, 0.8),
     'L1_xcond_b_so': (0.0, 0.38),
     'L1_xcond_b_q': (0.0, 0.8),
     'L1_xcond_b_kv': (0.0, 0.8),
     'L1_xcond_b_co': (0.0, 0.363),
     'L1_xcond_b_m1': (0.0, 0.8),
     'L1_xcond_b_m2': (0.0, 2.0),
     'L2_xcond_b_mod': (0.0, 0.721),
     'L2_xcond_b_qkv': (0.0, 0.8),
     'L2_xcond_b_proj': (0.0, 0.8),
     'L2_xcond_b_qc': (0.0, 2.0),
     'L2_xcond_b_kvc': (0.0, 0.8),
     'L2_xcond_b_cproj': (0.0, 0.8),
     'L2_xcond_b_mlp1': (0.0, 0.8),
     'L2_xcond_b_mlp2': (0.0, 0.8),
     'L3_xcond_ln_gamma': (1.0, 0.6),
     'L3_xcond_ln_beta': (0.0, 2.0),
     'L3_xcond_router_b': (0.0, 2.0),
     'L3_xcond_e_b1': (0.0, 2.0),
     'L3_xcond_e_b2': (0.0, 2.0),
     'L3_xcond_gate_b1': (0.0, 2.0),
     'L3_xcond_gate_b2': (0.0, 2.0),
     'L3_xcond_out_b': (0.0, 0.8)}
    factors = {'L0_xcond_adaLN_b': 8.0,
     'L0_xcond_qkv_W': 4.167,
     'L0_xcond_attn_out_W': 4.338,
     'L0_xcond_cq_W': 8.0,
     'L0_xcond_ck_W': 8.0,
     'L0_xcond_cv_W': 3.227,
     'L0_xcond_co_W': 3.252,
     'L0_xcond_mlp_b1': 8.0,
     'L0_xcond_mlp_b2': 8.0,
     'L1_xcond_w_qkv': 8.0,
     'L1_xcond_w_so': 6.007,
     'L1_xcond_w_q': 8.0,
     'L1_xcond_w_kv': 4.005,
     'L1_xcond_w_co': 3.469,
     'L1_xcond_w_m1': 7.236,
     'L1_xcond_w_m2': 7.221,
     'L2_xcond_W_qc': 4.45,
     'L3_xcond_Wq': 8.0,
     'L3_xcond_Wk': 8.0,
     'L3_xcond_Wv': 7.31,
     'L3_xcond_router_W': 4.944,
     'L3_xcond_e_w1': 2.959,
     'L3_xcond_gate_w1': 8.0,
     'L3_xcond_gate_w2': 7.456}
    for name, (base, spread) in spreads.items():
        noise = np.random.default_rng([zlib.crc32(name.encode()), seed]).standard_normal(out[name].shape)
        drawn = base * np.exp(spread * noise) if base else spread * noise
        out[name] = jnp.asarray(drawn.astype(out[name].dtype))
    for name, factor in factors.items():
        out[name] = (out[name] * factor).astype(out[name].dtype)
    return out
```

```python
from contextlib import ExitStack

import concourse.bass as bass
from concourse import mybir

ALU = mybir.AluOpType
ACT = mybir.ActivationFunctionType
F32 = mybir.dt.float32
U8 = mybir.dt.uint8
I32 = mybir.dt.int32
AX_X = mybir.AxisListType.X

P = 128
B, S, D = 8, 256, 256
SC = 77
SCP = 96
H, HD = 16, 16
CT = D // P
QT = S // P
HPT = P // HD
PAIR = 2
TURNS = B // PAIR
HID = 4 * D
HT_N = HID // P
E_N, RH = 3, 512
M3 = E_N * RH // P + CT
NEG = -3.4028234663852886e38
TAKEN = -3.0e38
SCALE = HD ** -0.5
SCALE3 = D ** -0.5
EPS = (1e-5, 1e-6, 1e-6, 1e-5)
SHIFT = 64
W_EVEN, W_ODD = 8192, 12288

SELF = {0: (2, 2), 1: (4, 1), 2: (2, 2)}
CROSS = (4, 1)


def groups(hg):
    return QT * H // hg


class Mark:

    def __init__(self, sem, per):
        self.sem, self.per, self.credit = sem, per, max(per)

    def base(self, l):
        return self.credit + TURNS * sum(self.per[:l])

    def of(self, l, i, k):
        return i * self.per[l] + (self.base(l) + k)

    def before(self, l, i, k):
        return i * self.per[l] + (self.base(l) - self.per[l] + k)


def projection_uses(l):
    both = lambda *names: [(n, j, o) for j in range(PAIR) for n, o in names]
    if l < 3:
        uses = both(("T0", "A"))
        uses += both(("Q", "A"), ("K", "A" if l == 0 else "V"), ("V0", "V"))
        uses += both(("VC", "A"))
        uses += both(("O", "V")) + both(("T1", "A")) + both(("QC", "A"))
        uses += both(("OC", "V")) + both(("T2", "A"))
        n, o = (HT_N, "V") if l == 1 else (HT_N // 2, "A")
        uses += both(*[(f"M{m}", o) for m in range(n)]) + both(("MO", "V"))
    else:
        uses = both(("T0", "A"), ("VC", "A"))
        uses += both(("Q", "A")) + both(("S", "A")) + both(("PT", "A"))
        uses += both(("EV", "A")) + both(("RL", "A")) + both(("RT", "V"))
        uses += both(*[(f"M{m}", "A") for m in range(M3 // 2)])
        uses += both(*[(f"E{e}", "V") for e in range(E_N)])
        uses += both(("GO", "V")) + both(("RR", "A")) + both(("OUT", "V"))
    return uses


USES = [projection_uses(l) for l in range(4)]
INDEX = [{(n, j): k for k, (n, j, _) in enumerate(u)} for u in USES]
ORDER = [[sum(x[2] == u[k][2] for x in u[:k + 1]) for k in range(len(u))] for u in USES]
COUNT = {o: [sum(x[2] == o for x in u) for u in USES] for o in "AV"}
NSELF = [PAIR * groups(SELF[l][0]) for l in range(3)]
NCROSS = PAIR * groups(CROSS[0])
NG = [n + NCROSS for n in NSELF] + [0]
NLN = (3, 3, 3, 1)

VECTORS = [("L0_xcond_norm1_w", 2), ("L0_xcond_normc_w", 2), ("L0_xcond_norm2_w", 2), ("L0_xcond_mlp_b1", 8),
           ("L1_xcond_b_qkv", 6), ("L1_xcond_b_q", 2), ("L1_xcond_b_kv", 4), ("L1_xcond_b_m1", 16),
           ("L2_xcond_b_qkv", 6), ("L2_xcond_b_qc", 2), ("L2_xcond_b_kvc", 4), ("L2_xcond_b_mlp1", 8),
           ("L3_xcond_ln_gamma", 2), ("L3_xcond_ln_beta", 2), ("L3_xcond_e_b1", 12), ("L3_xcond_gate_b1", 2)]
ROW, NROW = {}, 0
for _n, _k in VECTORS:
    ROW[_n] = NROW
    NROW += _k

NPRE = [(9 * D + 511) // 512, (9 * D + 511) // 512, (6 * D + 511) // 512]
ROWS_IN = [sum(NPRE[:l + 1]) for l in range(3)]
PRE_MODS = 1 + ROWS_IN[2] + 3
PRE_RAW = PRE_MODS + 3
PRE_ALL = PRE_RAW + 3
KEY_BANKS = CT * ((B * SC + 511) // 512)
KEYS_IN = [PRE_ALL - ROWS_IN[2] + (l + 1) * KEY_BANKS for l in range(4)]
PRE_LOADS = 2 + len(VECTORS) + 3 + 6

DVE_LINKS = (170, 296, 36, 32)


def mod_rows(KM, l):
    n = (0, 9 * D, 18 * D, 24 * D)
    return KM[0:B].rearrange("p j c h s -> p (j c h s)")[:, n[l]:n[l + 1]]


def padded(VP, j, t, n):
    return VP[0:n, j, t].rearrange("p h e (u d) -> p h (e u) d", d=HD)[:, :, 0:4:3, :]


def V3(VP, j):
    return VP[0:SCP, j, 0].rearrange("p h e w -> p (h e w)")[:, 0:D]


LINKS = {}
PRE_DVE_VAR = 2 * B + 1
PRE_DVE_CTX = PRE_DVE_VAR + 4 + B


def build(nc, a, out):
    A = lambda l, n: a[f"L{l}_xcond_{n}"]
    with ExitStack() as ctx:
        def sb(name, shape, dt=F32):
            return ctx.enter_context(nc.sbuf_tensor(name, shape, dt))

        def sem(name):
            return ctx.enter_context(nc.semaphore(name))

        X = sb("X", [P, B, QT, D])
        w_even = sb("w_even", [P, W_EVEN])
        w_odd = sb("w_odd", [P, W_ODD])
        KM = sb("KM", [P, PAIR, CT, HPT, S])
        probs = sb("probs", [P, 4, 512])
        probsT = sb("probsT", [P, 4, 512])
        xh = sb("xh", [P, PAIR, QT, D])
        oT = xh
        hT = sb("hT", [P, PAIR, CT, S])
        qT = sb("qT", [P, PAIR, CT, S])
        kT = sb("kT", [P, PAIR, CT, S])
        VP = sb("VP", [P, PAIR, QT, HPT, 2, 32])
        gates = sb("gates", [P, PAIR, 3, D])
        brow = sb("brow", [P, 5, D])
        ctxT = sb("ctxT", [P, CT, B * SC])
        ctxnT = sb("ctxnT", [P, CT, B * SC])
        kcT = sb("kcT", [P, CT, B * SC])
        cs = sb("cs", [P, PAIR, CT, SCP])
        mods = sb("mods", [P, 3, 12, B])
        cols = sb("cols", [P, PAIR, 12])
        vec = sb("vec", [P, NROW])
        bq = sb("bq", [P, 2, 4])
        ident = sb("ident", [P, P])
        onesP = sb("onesP", [P, 2, 32])
        onesC = sb("onesC", [SCP, 2, 32])
        cosT = sb("cosT", [P, P])
        sinT = sb("sinT", [P, P])
        maskS = sb("maskS", [P, QT, S])
        maskC = sb("maskC", [P, B, SC])
        maskCj = sb("maskCj", [P, PAIR, SC])
        maskSw = sb("maskSw", [P, QT * S // 4], I32)
        maskCw = sb("maskCw", [P, B * SC // 4], I32)
        maskSb = maskSw[:, :].bitcast(U8).rearrange("p (t k) -> p t k", t=QT)
        maskCb = maskCw[:, :].bitcast(U8).rearrange("p (b k) -> p b k", b=B)
        cT = sb("cT", [P, CT, B])
        scT = sb("scT", [P, CT, B])
        crow = xh[0:B, 0, 0, :]
        srow = xh[0:B, 0, 1, :]
        nmax = sb("nmax", [P, 4, 4])
        top1 = sb("top1", [P, 4, 8])
        top2 = sb("top2", [P, 4, 8])
        left1 = maskS[:, :, :].rearrange("p t k -> p (t k)")[:, 0:4 * SC].rearrange("p (h k) -> p h k", h=4)
        left2 = maskC[:, :, :].rearrange("p (n h) k -> p n h k", n=2)
        rden = sb("rden", [P, CT * S])
        stats = sb("stats", [P, PAIR, QT, 6])
        mv = sb("mv", [P, PAIR, QT, 2])
        ve = sb("ve", [P, PAIR, QT])
        rstd = sb("rstd", [P, PAIR, QT])
        mhalf = sb("mhalf", [P, 8])
        anchor = gates[:, 0, 1, 0:M3 * B].rearrange("p (m b) -> p m b", b=B)
        anc = sb("anc", [P, PAIR, M3])
        ranchor = sb("ranchor", [E_N, B + 1])
        ranc = sb("ranc", [E_N, PAIR])
        rb = sb("rb", [E_N, 1])
        logT = gates[0:E_N, :, 0, :]
        rp = sb("rp", [P, PAIR, QT, E_N])
        small = sb("small", [P, PAIR, QT, 2])
        stage = probs[:, :, :].rearrange("p a b -> p (a b)")
        scratch = nc.dram_tensor("gate_rows", [3, B, 3 * D], F32, kind="Internal").ap()

        bank = [ctx.enter_context(nc.psum_tensor(f"bank{n}", [P, 512], F32)) for n in range(8)]
        pj, ps, pt, po, pn = bank[0:2], bank[2:4], bank[4:6], bank[6], bank[7]

        s_in = sem("inputs_landed")
        s_ada = [sem(f"ada_landed{l}") for l in range(3)]
        s_w = [sem(f"weights_landed{l}") for l in range(4)]
        s_brow = sem("bias_rows_landed")
        s_const = sem("constants_made")
        s_mask = sem("masks_made")
        s_phase = sem("engine_done_with_layer")
        s_pre_full = sem("prelude_bank_full")
        s_pre_empty = sem("prelude_bank_emptied_by_scalar")
        s_rows = sem("modulation_rows_bank_emptied_by_vector")
        s_pre_dve = sem("prelude_vector_step")
        s_pre_act = sem("prelude_scalar_step")
        s_pre_pool = sem("prelude_pool_step")
        s_gates_out = sem("gate_rows_stored")
        s_out = sem("outputs_stored")
        s_held = [sem("tensor_held"), sem("vector_held")]
        vector_engine = [None]
        credited = []

        def mark(name, per):
            m = Mark(sem(name), tuple(per))
            credited.append(m)
            return m

        full = mark("projection_bank_full", [len(u) for u in USES])
        emptied = {"A": mark("bank_emptied_by_scalar", COUNT["A"]), "V": mark("bank_emptied_by_vector", COUNT["V"])}
        var_ready = mark("variance_ready", [2 * n for n in NLN])
        rstd_ready = mark("rstd_ready", [2 * n for n in NLN])
        xh_ready = mark("tokens_normalised", [2 * n for n in NLN])
        rope_ready = mark("rope_done", [2, 0, 0, 0])
        scored = mark("scores_ready", NG)
        maxed = mark("max_ready", NG)
        exped = mark("exp_ready", NG)
        chosen = mark("topk_applied", [0, NCROSS, 0, 0])
        turned = mark("probs_transposed", NG)
        copied = [mark(f"probsT_copied_{n}", [g // 2 for g in NG]) for n in ("scalar", "vector")]
        summed = mark("values_summed", NG)
        normed = mark("heads_normalised", [4, 4, 4, 0])
        added = mark("residual_added", [6, 6, 6, 2])
        picked = mark("batch_columns_copied", [2, 2, 2, 2])
        gates_in = [mark(f"gates_landed{j}", [16, 16, 16, 0]) for j in range(PAIR)]
        keys_in = [mark(f"masked_keys_landed{j}", [256, 256, 256, 0]) for j in range(PAIR)]
        act3 = mark("layer3_scalar_step", [0, 0, 0, 4])
        silu_done = mark("silu_ready", [0, PAIR * HT_N, 0, 0])
        dve3 = mark("layer3_vector_step", [0, 0, 0, 4])
        dve_own = mark("vector_own_step", DVE_LINKS)

        def region(buf, at, *shape):
            n = 1
            for s in shape:
                n *= s
            v = buf[:, at:at + n]
            if len(shape) == 2:
                v = v.rearrange("p (k n) -> p k n", n=shape[1])
            elif len(shape) == 3:
                v = v.rearrange("p (e k n) -> p e k n", k=shape[1], n=shape[2])
            return v

        def lay(buf, items):
            got, at = {}, 0
            for name, *shape in items:
                n = 1
                for s in shape:
                    n *= s
                got[name] = region(buf, at, *shape)
                at += n
            assert at <= buf.shape[1], (at, buf.shape)
            return got

        common = lambda kv, m1: [("qkv", CT, 3 * D), ("so", CT, D), ("cq", CT, D), *kv, ("co", CT, D), ("m1", CT, m1), ("m2", HT_N, D)]
        W = [lay(w_even, common([("ck", CT, D), ("cv", CT, D)], HID)),
             lay(w_odd, common([("ckv", CT, 2 * D)], 2 * HID)),
             lay(w_even, common([("ckv", CT, 2 * D)], HID)),
             lay(w_odd, [("e1", E_N, 4, RH), ("e2", E_N, 4, D), ("wq", CT, D), ("ck", CT, D), ("cv", CT, D), ("g1", 4, D), ("g2", CT, D)])]
        W3 = lay(w_even, [("out", CT, D), ("e1a", E_N, CT, RH), ("g1a", CT, D), ("r", 4, E_N), ("ra", CT, E_N)])
        ADA_N = (9 * D, 9 * D, 6 * D)
        WA = lay(w_odd, [("0", CT, ADA_N[0]), ("1", CT, ADA_N[1]), ("2", CT, ADA_N[2])])
        for l in (1, 2):
            W[l]["ck"], W[l]["cv"] = W[l]["ckv"][:, :, 0:D], W[l]["ckv"][:, :, D:2 * D]
        kp = lambda w: w.rearrange("(k p) n -> p k n", p=P)
        LOADS = [
            [("qkv", "qkv_W"), ("so", "attn_out_W"), ("cq", "cq_W"), ("ck", "ck_W"), ("cv", "cv_W"), ("co", "co_W"), ("m1", "mlp_W1"), ("m2", "mlp_W2")],
            [("qkv", "w_qkv"), ("so", "w_so"), ("cq", "w_q"), ("ckv", "w_kv"), ("co", "w_co"), ("m1", "w_m1"), ("m2", "w_m2")],
            [("qkv", "W_qkv"), ("so", "W_proj"), ("cq", "W_qc"), ("ckv", "W_kvc"), ("co", "W_cproj"), ("m1", "W_mlp1"), ("m2", "W_mlp2")],
        ]
        LOADED = [16 * len(x) for x in LOADS] + [16 * 18]
        BROWS = [["mlp_b2"], ["b_so", "b_co", "b_m2"], ["b_proj", "b_cproj", "b_mlp2"], ["e_b2", "gate_b2", "out_b"]]
        BROW_AT = [{2: 0}, {0: 0, 1: 1, 2: 2}, {0: 0, 1: 1, 2: 2}]
        BROW_N = [16 * len(x) for x in BROWS]
        VC = lambda l, name: ROW[f"L{l}_xcond_{name}"]
        BK = {1: VC(1, "b_qkv") + 2, 2: VC(2, "b_qkv") + 2}
        BV = {(1, 0): VC(1, "b_qkv") + 4, (2, 0): VC(2, "b_qkv") + 4, (1, 1): VC(1, "b_kv") + 2, (2, 1): VC(2, "b_kvc") + 2}
        BKC = {1: VC(1, "b_kv"), 2: VC(2, "b_kvc")}
        B1 = {0: VC(0, "mlp_b1"), 1: VC(1, "b_m1"), 2: VC(2, "b_mlp1")}
        MOD = {0: [(0, 1, 2), (3, 4, 5), (6, 7, 8)], 1: [(0, 1, 2), (3, 4, 5), (6, 7, 8)], 2: [(0, 1, 2), None, (3, 4, 5)]}

        def wait_full(eng, l, i, name, j):
            eng.wait_ge(full.sem, full.of(l, i, INDEX[l][name, j] + 1))

        def wait_taken(eng, l, i, name, j):
            k = INDEX[l][name, j]
            m = emptied[USES[l][k][2]]
            eng.wait_ge(m.sem, m.of(l, i, ORDER[l][k]))

        def wait_free(eng, l, i, name, j, *needs):
            k = INDEX[l][name, j]
            last = k - 2 if k >= 2 else max(x for x in range(len(USES[l])) if x % 2 == k % 2)
            owner = USES[l][last][2]
            least = {owner: ORDER[l][last] - (0 if k >= 2 else emptied[owner].per[l])}
            for n in needs:
                x = INDEX[l][n, j]
                owner = USES[l][x][2]
                least[owner] = max(ORDER[l][x], least.get(owner, ORDER[l][x]))
            for owner, k_ in least.items():
                eng.wait_ge(emptied[owner].sem, emptied[owner].of(l, i, k_))
            return pj[k % 2]

        def bank_of(l, name, j):
            return pj[INDEX[l][name, j] % 2]

        def wait_group(eng, m, l, i, n, start=0):
            if n >= start:
                eng.wait_ge(m.sem, m.of(l, i, n - start + 1))
            else:
                eng.wait_ge(m.sem, m.before(l, i, m.per[l] + n - start + 1))

        def wait_copied(eng, l, i, n):
            m = copied[n % 2]
            if n >= 0:
                eng.wait_ge(m.sem, m.of(l, i, n // 2 + 1))
            else:
                eng.wait_ge(m.sem, m.before(l, i, m.per[l] + (n // 2) + 1))

        def hold(eng):
            eng.sem_inc(s_held[eng is vector_engine[0]], 1)

        def shape(l, cross):
            hg, kts = CROSS if cross else SELF[l]
            width = SCP if cross else kts * P
            return hg, kts, width, (SCP if cross else P), (NSELF[l] if cross else 0)

        def parts(l, cross, g):
            hg = shape(l, cross)[0]
            per = H // hg
            return g // (QT * per), g // per % QT, g % per * hg

        def layer_done(eng, l):
            eng.drain().then_inc(s_phase, 1)
            eng.wait_ge(s_phase, 5 * (l + 1))

        def hidden(j, l):
            if l == 3:
                return KM[:, j].rearrange("p c h s -> p (c h) s")
            buf = probs if j == 0 else probsT
            return buf[:, :, :].rearrange("p a (b s) -> p (a b) s", s=S)

        block = ctx.enter_context(nc.Block())

        @block.sync
        def _(sp):
            sp.dma_start(crow, a["cond_1024"]).then_inc(s_in, 16)
            ctx_tok = stage[0:SC, 0:B * D].rearrange("p (b d) -> p b d", b=B)
            sp.dma_start(ctx_tok, a["ctx_1024"].rearrange("b s d -> s b d")).then_inc(s_in, 16)
            vst = hT[:, 0, 0, 0:P]
            for n, k in VECTORS:
                r = ROW[n]
                v = a[n]
                if len(v.shape) == 2:
                    v = v.rearrange("e n -> (e n)")
                sp.dma_start(vst[r:r + k, :], v.rearrange("(k p) -> k p", p=P)).then_inc(s_in, 16)
            for l, n in enumerate(("adaLN_b", "b_ada", "b_mod")):
                sp.dma_start(mod_rows(KM, l), A(l, n).rearrange("(o n) -> o n", o=1).to_broadcast([B, ADA_N[l]])).then_inc(s_in, 16)
            for l, n in enumerate(("adaLN_W", "w_ada", "W_mod")):
                sp.dma_start(WA[str(l)], kp(A(l, n))).then_inc(s_ada[l], 16)
                if l == 0:
                    sp.dma_start(X[:, :, :, :].rearrange("p b t d -> p (b t) d"), a["x"].rearrange("b (t p) d -> p (b t) d", p=P)).then_inc(s_in, 16)
                    sp.dma_start(maskSw[:, :].rearrange("p (t k) -> p t k", t=QT), a["mask_SxS_bk0"].rearrange("(t p k) -> p t k", p=P, t=QT)).then_inc(s_in, 16)
                    sp.dma_start(maskCw[:, :], a["mask_BxS2_bf1"].rearrange("(o k) -> o k", o=1).to_broadcast([P, B * SC // 4])).then_inc(s_in, 16)
                    sp.dma_start(cosT[:, :], a["rope_cos"]).then_inc(s_in, 16)
                    sp.dma_start(sinT[:, :], a["rope_sin"]).then_inc(s_in, 16)
                    sp.dma_start(rb[:, :], A(3, "router_b").rearrange("(e o) -> e o", o=1)).then_inc(s_in, 16)
            for name, src in LOADS[0]:
                sp.dma_start(W[0][name], kp(A(0, src))).then_inc(s_w[0], 16)
            for l in range(3):
                sp.wait_ge(s_rows, ROWS_IN[l])
                for n, m in enumerate(MOD[l]):
                    g = (m or MOD[l][0])[2]
                    sp.dma_start(scratch[l, :, n * D:(n + 1) * D], mod_rows(KM, l)[:, g * D:(g + 1) * D]).then_inc(s_gates_out, 16)
            sp.wait_ge(s_gates_out, 16 * 9)
            sp.drain().then_inc(s_phase, 1)
            sp.wait_ge(s_phase, 5)
            for l in range(4):
                r = 0
                for n in BROWS[l]:
                    v = A(l, n)
                    if n == "e_b2":
                        sp.dma_start(brow[:, 0:E_N, :], v.rearrange("(o e) n -> o e n", o=1).to_broadcast([P, E_N, D])).then_inc(s_brow, 16)
                        r += E_N
                    else:
                        sp.dma_start(brow[:, r, :], v.rearrange("(o n) -> o n", o=1).to_broadcast([P, D])).then_inc(s_brow, 16)
                        r += 1
                if l == 3:
                    for e in range(E_N):
                        sp.dma_start(W3["e1a"][:, e], A(3, "e_w1")[e, 4 * P:6 * P, :].rearrange("(k p) n -> p k n", p=P)).then_inc(s_w[3], 16)
                    sp.dma_start(W3["g1a"], kp(A(3, "gate_w1")[4 * P:6 * P, :])).then_inc(s_w[3], 16)
                    sp.dma_start(W3["r"], kp(A(3, "router_W")[0:4 * P, :])).then_inc(s_w[3], 16)
                    sp.dma_start(W3["ra"], kp(A(3, "router_W")[4 * P:6 * P, :])).then_inc(s_w[3], 16)
                    sp.dma_start(W3["out"], kp(A(3, "out_w"))).then_inc(s_w[3], 16)
                elif l == 2:
                    for n, src in (("ck", "Wk"), ("cv", "Wv"), ("wq", "Wq"), ("g2", "gate_w2")):
                        sp.dma_start(W[3][n], kp(A(3, src))).then_inc(s_w[3], 16)
                    sp.dma_start(W[3]["g1"], kp(A(3, "gate_w1")[0:4 * P, :])).then_inc(s_w[3], 16)
                    for e in range(E_N):
                        sp.dma_start(W[3]["e1"][:, e], kp(A(3, "e_w1")[e, 0:4 * P, :])).then_inc(s_w[3], 16)
                        sp.dma_start(W[3]["e2"][:, e], kp(A(3, "e_w2")[e])).then_inc(s_w[3], 16)
                else:
                    for name, src in LOADS[l + 1]:
                        sp.dma_start(W[l + 1][name], kp(A(l + 1, src))).then_inc(s_w[l + 1], 16)
                if l == 3:
                    with sp.Fori(0, TURNS) as i:
                        for j in range(PAIR):
                            sp.wait_ge(added.sem, added.of(3, i, j + 1))
                            sp.dma_start(out[bass.ds(i * PAIR + j, 1)].rearrange("o (t p) d -> p (o t) d", p=P),
                                         X[:, bass.ds(i * PAIR + j, 1)].rearrange("p o t d -> p (o t) d")).then_inc(s_out, 16)
                    sp.wait_ge(s_out, 16 * B)
                else:
                    sp.wait_ge(s_pre_empty, KEYS_IN[l])
                    with sp.Fori(0, TURNS) as i:
                        for j in range(PAIR):
                            sp.wait_ge(added.sem, added.before(l, i, 5 + j))
                            sp.dma_start(gates[:, j].rearrange("p g d -> p (g d)"),
                                         scratch[l, bass.ds(i * PAIR + j, 1), :].to_broadcast([P, 3 * D])).then_inc(gates_in[j].sem, 16)
                        for j in range(PAIR):
                            if l == 0:
                                sp.wait_ge(rope_ready.sem, rope_ready.of(l, i, j + 1))
                            else:
                                wait_taken(sp, l, i, "K", j)
                            for h in range(HPT):
                                sp.dma_start(KM[HD * h:HD * (h + 1), j, :, h, :], kT[HD * h:HD * (h + 1), j, :, :]).then_inc(keys_in[j].sem, 16)
                        for j in range(PAIR):
                            wait_group(sp, scored, l, i, (j + 1) * NSELF[l] // 2 - 1)
                            for h in range(HPT):
                                sp.dma_start(KM[HD * h:HD * (h + 1), j, :, h, 0:SC],
                                             kcT[HD * h:HD * (h + 1), :, bass.ds((i * PAIR + j) * SC, SC)]).then_inc(keys_in[j].sem, 16)
                if l < 3:
                    layer_done(sp, l + 1)

        @block.gpsimd
        def _(pool):
            for m in credited:
                pool.sem_inc(m.sem, m.credit)
            nc.gpsimd.memset(ident[:, :], 0.0).then_inc(s_pre_pool, 1)
            nc.gpsimd.memset(onesP[:, :, :], 0.0).then_inc(s_pre_pool, 1)
            nc.gpsimd.memset(onesC[:, :, :], 0.0).then_inc(s_pre_pool, 1)
            pool.wait_ge(s_pre_pool, 3)
            nc.gpsimd.affine_select(out=ident[:, :], in_=ident[:, :], compare_op=ALU.not_equal, fill=1.0,
                                    base=0, pattern=[[-1, P]], channel_multiplier=1).then_inc(s_const, 1)
            for e in range(2):
                nc.gpsimd.memset(onesP[:, e, 16 * e:16 * e + 16], 1.0).then_inc(s_const, 1)
            nc.gpsimd.memset(mods[:, :, :, :].rearrange("p l c b -> p (l c b)"), 0.0).then_inc(s_const, 1)
            nc.gpsimd.memset(cs[:, :, :, :].rearrange("p j c k -> p (j c k)"), 0.0).then_inc(s_pre_pool, 1)
            for e in range(2):
                nc.gpsimd.memset(onesC[0:SC, e, 16 * e:16 * e + 16], 1.0).then_inc(s_pre_pool, 1)
            nc.gpsimd.memset(mhalf[:, :], -0.5).then_inc(s_pre_pool, 1)
            nc.gpsimd.memset(VP[:, :].rearrange("p j t h e w -> p (j t h e w)"), 0.0).then_inc(s_const, 1)
            pool.wait_ge(s_pre_pool, 7)
            pool.wait_ge(s_pre_dve, PRE_DVE_VAR)
            nc.gpsimd.tensor_tensor(rden[0:SC, 16:24], rden[0:SC, 8:16], mhalf[0:SC, :], ALU.pow).then_inc(s_pre_pool, 1)
            pool.wait_ge(s_pre_full, PRE_MODS)
            pool.wait_ge(s_gates_out, 16 * 9)
            for j in range(PAIR):
                nc.gpsimd.memset(KM[:, j].rearrange("p c h s -> p (c h s)"), 0.0).then_inc(s_const, 1)
            pool.drain().then_inc(s_phase, 1)
            pool.wait_ge(s_phase, 5)
            for l in range(4):
                pool.wait_ge(s_pre_empty, KEYS_IN[l] + (l == 3))
                if l == 3:
                    pool.wait_ge(s_mask, 1)
                with pool.Fori(0, TURNS) as i:
                    src = ctxnT if l == 2 else ctxT
                    for j in range(PAIR):
                        b = i * PAIR + j
                        if l < 3:
                            last = emptied["A"]
                            k = INDEX[l]["T2", j]
                            pool.wait_ge(last.sem, last.before(l, i, ORDER[l][k]))
                            if l == 0:
                                nc.gpsimd.tensor_copy(maskCj[:, j, :], maskC[:, bass.ds(b, 1), :].rearrange("p o k -> p (o k)"))
                            nc.gpsimd.tensor_copy(cols[:, j, :], mods[:, l, :, bass.ds(b, 1)].rearrange("p c o -> p (c o)"))
                        else:
                            pool.wait_ge(added.sem, added.before(l, i, j + 1))
                            nc.gpsimd.tensor_copy(anc[:, j, :], anchor[:, :, bass.ds(b, 1)].rearrange("p c o -> p (c o)"))
                            nc.gpsimd.tensor_copy(ranc[:, j:j + 1], ranchor[:, bass.ds(b, 1)])
                            nc.gpsimd.tensor_copy(kT[:, j, :, 0:SC], kcT[:, :, bass.ds(b * SC, SC)])
                        nc.gpsimd.tensor_copy(cs[:, j, :, 0:SC], src[:, :, bass.ds(b * SC, SC)]).then_inc(picked.sem, 1)
                    for n in range(NLN[l]):
                        for j in range(PAIR):
                            pool.wait_ge(var_ready.sem, var_ready.of(l, i, 2 * n + j + 1))
                            nc.gpsimd.tensor_tensor(rstd[:, j, :], ve[:, j, :], mhalf[:, 0:QT], ALU.pow).then_inc(rstd_ready.sem, 1)
                if l < 3:
                    layer_done(pool, l + 1)

        @block.tensor
        def _(pe):
            uses = [0]

            def pre_bank():
                u = uses[0]
                uses[0] += 1
                if 1 <= u - 2 <= ROWS_IN[2]:
                    pe.wait_ge(s_rows, u - 2)
                elif u >= 2:
                    pe.wait_ge(s_pre_empty, max(1, u - 1 - ROWS_IN[2]))
                return pj[u % 2]

            def mm(dst, pairs):
                for n, (x, y) in enumerate(pairs):
                    last = nc.tensor.matmul(dst, x, y, start=(n == 0), stop=(n == len(pairs) - 1))
                return last

            pe.wait_ge(s_in, 16 * PRE_LOADS)
            pe.wait_ge(s_const, 4)
            b_ = pre_bank()
            for c in range(CT):
                nc.tensor.transpose(b_[:, c * B:(c + 1) * B], crow[:, c * P:(c + 1) * P], ident[0:B, 0:B])
            pe.wait_ge(s_pre_act, 1)
            for c in range(CT):
                nc.tensor.transpose(b_[:, (2 + c) * B:(3 + c) * B], srow[:, c * P:(c + 1) * P], ident[0:B, 0:B])
            nc.tensor.transpose(b_[:, P:P + NROW], hT[0:NROW, 0, 0, 0:P], ident[0:NROW, 0:NROW]).then_inc(s_pre_full, 1)
            pe.wait_ge(s_pre_empty, 1)
            for l in range(3):
                pe.wait_ge(s_ada[l], 16)
                cc = cT if l == 0 else scT
                for n in range(0, ADA_N[l], 512):
                    w = min(512, ADA_N[l] - n)
                    b_ = pre_bank()
                    mm(b_[0:B, 0:w], [(cc[:, k, :], WA[str(l)][:, k, n:n + w]) for k in range(CT)]).then_inc(s_pre_full, 1)
            for l in range(3):
                pe.wait_ge(s_rows, ROWS_IN[l])
                b_ = pre_bank()
                rows = mod_rows(KM, l)
                at = 0
                for m in MOD[l]:
                    if m is None:
                        continue
                    for chunk in m[0:2]:
                        for c in range(CT):
                            last = nc.tensor.transpose(b_[:, at:at + B], rows[:, chunk * D + c * P:chunk * D + (c + 1) * P], ident[0:B, 0:B])
                            at += B
                last.then_inc(s_pre_full, 1)
            for norm in range(2):
                ctx_tok = stage[0:SC, 0:B * D].rearrange("p (b d) -> p b d", b=B)
                if norm:
                    pe.wait_ge(s_pre_dve, PRE_DVE_CTX)
                for b0 in range(0, B, 3):
                    b_ = pre_bank()
                    for b in range(b0, min(b0 + 3, B)):
                        for c in range(CT):
                            at = (c * 3 + b - b0) * SC
                            last = nc.tensor.transpose(b_[:, at:at + SC], ctx_tok[:, b, c * P:(c + 1) * P], ident[0:SC, 0:SC])
                    last.then_inc(s_pre_full, 1)
            pe.drain().then_inc(s_phase, 1)
            pe.wait_ge(s_phase, 5)

            def context_keys(l):
                src = ctxnT if l == 2 else ctxT
                for c in range(CT):
                    for n in range(0, B * SC, 512):
                        w = min(512, B * SC - n)
                        b_ = pre_bank()
                        mm(b_[:, 0:w], [(W[l]["ck"][:, k, c * P:(c + 1) * P], src[:, k, n:n + w]) for k in range(CT)]).then_inc(s_pre_full, 1)

            def to_channels(l, i, j, n):
                pe.wait_ge(xh_ready.sem, xh_ready.of(l, i, 2 * n + j + 1))
                b_ = wait_free(pe, l, i, f"T{n}", j)
                for t in range(QT):
                    for c in range(CT):
                        last = nc.tensor.transpose(b_[:, c * S + t * P:c * S + (t + 1) * P], xh[:, j, t, c * P:(c + 1) * P], ident[:, :])
                last.then_inc(full.sem, 1)

            def channels_out(l, i, name, j, w, at, rhs, *needs, ks=CT):
                b_ = wait_free(pe, l, i, name, j, *needs)
                for c in range(2):
                    last = mm(b_[:, c * S:(c + 1) * S], [(w[:, k, at + c * P:at + (c + 1) * P], rhs(k)) for k in range(ks)])
                last.then_inc(full.sem, 1)

            def tokens_out(l, i, name, j, w, at, lhs, *needs, ks=CT):
                b_ = wait_free(pe, l, i, name, j, *needs)
                for t in range(QT):
                    last = mm(b_[:, t * D:(t + 1) * D], [(lhs(k)[:, t * P:(t + 1) * P], w[:, k, at:at + D]) for k in range(ks)])
                last.then_inc(full.sem, 1)

            def attention(l, i, cross):
                hg, kts, width, kp_, first = shape(l, cross)
                total = PAIR * groups(hg)
                swap = l == 1 and cross
                for step in range(total + 3):
                    if step < total:
                        n = first + step
                        j, qt, h0 = parts(l, cross, step)
                        if step % (total // 2) == 0:
                            if l == 0 and not cross:
                                pe.wait_ge(rope_ready.sem, rope_ready.of(l, i, j + 1))
                            else:
                                wait_taken(pe, l, i, "QC" if cross else "Q", j)
                            pe.wait_ge(keys_in[j].sem, keys_in[j].of(l, i, 256 if cross else 128))
                        wait_group(pe, exped, l, i, n - 2)
                        for x in range(hg):
                            h = h0 + x
                            keys = KM[:, j, h // HPT, h % HPT, 0:SCP] if cross else (
                                KM[:, j, h // HPT, h % HPT, qt * P:(qt + 1) * P] if kts == 1 else KM[:, j, h // HPT, h % HPT, :])
                            last = nc.tensor.matmul(ps[n % 2][:, x * width:(x + 1) * width], qT[:, j, h // HPT, qt * P:(qt + 1) * P], keys, start=True, stop=True)
                        last.then_inc(scored.sem, 1)
                    if 0 <= step - 2 < total:
                        n = first + step - 2
                        if swap:
                            pe.wait_ge(chosen.sem, chosen.of(l, i, step - 1))
                        else:
                            wait_group(pe, exped, l, i, n)
                        wait_copied(pe, l, i, n - 2)
                        for x in range(hg):
                            for k in range(kts):
                                at = (x * kts + k) * P
                                keys_ = SC if cross else P
                                last = nc.tensor.transpose(pt[n % 2][0:keys_, at:at + P], probs[:, n % 4, x * width + k * P:x * width + k * P + keys_], ident[:, :])
                        last.then_inc(turned.sem, 1)
                    if 0 <= step - 3 < total:
                        n = first + step - 3
                        j, qt, h0 = parts(l, cross, step - 3)
                        if (step - 3) % (total // 2) == 0:
                            k = 2 * cross + j
                            if k:
                                pe.wait_ge(normed.sem, normed.of(l, i, k))
                            else:
                                pe.wait_ge(normed.sem, normed.before(l, i, 4))
                            wait_taken(pe, l, i, "VC" if cross else "V0", j)
                        wait_copied(pe, l, i, n)
                        for x in range(0, hg, 2):
                            h = h0 + x
                            quad, c = h % HPT // 2, h // HPT
                            at = slice(c * S + qt * P, c * S + (qt + 1) * P)
                            for dst in (po, pn):
                                for e in range(2):
                                    for k in range(kts):
                                        kt = qt if (kts == 1 and not cross) else k
                                        lhs = VP[0:kp_, j, kt, h // 2, e, :] if dst is po else (onesC if cross else onesP)[0:kp_, e, :]
                                        col = ((x + e) * kts + k) * P
                                        last = nc.tensor.matmul(dst[32 * quad:32 * quad + 32, at], lhs, probsT[0:kp_, n % 4, col:col + P],
                                                                start=(e == 0 and k == 0), stop=(e == 1 and k == kts - 1))
                        last.then_inc(summed.sem, 1)

            for l in range(3):
                w = W[l]
                pe.wait_ge(s_w[l], LOADED[l])
                context_keys(l)
                with pe.Fori(0, TURNS) as i:
                    for j in range(PAIR):
                        to_channels(l, i, j, 0)
                    for j in range(PAIR):
                        x = lambda k: hT[:, j, k, :]
                        channels_out(l, i, "Q", j, w["qkv"], 0, x, "T0")
                        channels_out(l, i, "K", j, w["qkv"], D, x)
                        tokens_out(l, i, "V0", j, w["qkv"], 2 * D, x)
                    attention(l, i, 0)
                    for j in range(PAIR):
                        pe.wait_ge(picked.sem, picked.of(l, i, j + 1))
                        b_ = wait_free(pe, l, i, "VC", j)
                        mm(b_[0:SCP, 0:D], [(cs[:, j, k, :], w["cv"][:, k, :]) for k in range(CT)]).then_inc(full.sem, 1)
                    for j in range(PAIR):
                        pe.wait_ge(normed.sem, normed.of(l, i, j + 1))
                        tokens_out(l, i, "O", j, w["so"], 0, lambda k: oT[:, j, k, :])
                    for j in range(PAIR):
                        to_channels(l, i, j, 1)
                    for j in range(PAIR):
                        channels_out(l, i, "QC", j, w["cq"], 0, lambda k: hT[:, j, k, :], "T1")
                    attention(l, i, 1)
                    for j in range(PAIR):
                        pe.wait_ge(normed.sem, normed.of(l, i, 3 + j))
                        tokens_out(l, i, "OC", j, w["co"], 0, lambda k: oT[:, j, k, :])
                    for j in range(PAIR):
                        to_channels(l, i, j, 2)
                    for j in range(PAIR):
                        if l == 1:
                            for m in range(HT_N):
                                b_ = wait_free(pe, l, i, f"M{m}", j, "T2")
                                for half in range(2):
                                    at = half * HID + m * P
                                    last = mm(b_[:, half * S:(half + 1) * S], [(w["m1"][:, k, at:at + P], hT[:, j, k, :]) for k in range(CT)])
                                last.then_inc(full.sem, 1)
                        else:
                            for m in range(HT_N // 2):
                                channels_out(l, i, f"M{m}", j, w["m1"], 2 * m * P, lambda k: hT[:, j, k, :], "T2")
                    for j in range(PAIR):
                        hid = hidden(j, l)
                        tokens_out(l, i, "MO", j, w["m2"], 0, lambda k: hid[:, k, :],
                                   f"M{HT_N - 1 if l == 1 else HT_N // 2 - 1}", ks=HT_N)
                layer_done(pe, l + 1)

            l, w = 3, W[3]
            pe.wait_ge(s_w[3], LOADED[3])
            context_keys(3)
            b_ = pre_bank()
            for m in range(M3):
                for k in range(CT):
                    lhs = W3["e1a"][:, m // 4, k, m % 4 * P:(m % 4 + 1) * P] if m < 4 * E_N else W3["g1a"][:, k, (m - 4 * E_N) * P:(m - 4 * E_N + 1) * P]
                    last = nc.tensor.matmul(b_[:, m * B:(m + 1) * B], lhs, cT[:, k, :], start=(k == 0), stop=(k == CT - 1))
            mm(b_[0:E_N, M3 * B:(M3 + 1) * B], [(W3["ra"][:, k, :], cT[:, k, :]) for k in range(CT)]).then_inc(s_pre_full, 1)
            with pe.Fori(0, TURNS) as i:
                for j in range(PAIR):
                    to_channels(l, i, j, 0)
                    pe.wait_ge(picked.sem, picked.of(l, i, j + 1))
                    b_ = wait_free(pe, l, i, "VC", j)
                    mm(b_[0:SCP, 0:D], [(cs[:, j, k, :], w["cv"][:, k, :]) for k in range(CT)]).then_inc(full.sem, 1)
                for j in range(PAIR):
                    channels_out(l, i, "Q", j, w["wq"], 0, lambda k: hT[:, j, k, :], "T0")
                for j in range(PAIR):
                    b_ = wait_free(pe, l, i, "S", j, "Q")
                    for t in range(QT):
                        last = mm(b_[:, t * SC:(t + 1) * SC], [(qT[:, j, k, t * P:(t + 1) * P], kT[:, j, k, 0:SC]) for k in range(CT)])
                    last.then_inc(full.sem, 1)
                for j in range(PAIR):
                    pe.wait_ge(dve3.sem, dve3.of(l, i, 3 + j))
                    b_ = wait_free(pe, l, i, "PT", j)
                    for t in range(QT):
                        last = nc.tensor.transpose(b_[0:SC, t * P:(t + 1) * P], probs[:, j, t * SC:(t + 1) * SC], ident[:, :])
                    last.then_inc(full.sem, 1)
                for j in range(PAIR):
                    b_ = wait_free(pe, l, i, "EV", j, "PT", "VC")
                    for c in range(CT):
                        last = nc.tensor.matmul(b_[:, c * S:(c + 1) * S], V3(VP, j)[:, c * P:(c + 1) * P], probsT[0:SCP, j, 0:S], start=True, stop=True)
                    last.then_inc(full.sem, 1)
                comb = lambda j: (lambda k: hT[:, j, k, :] if k < CT else qT[:, j, k - CT, :])
                for j in range(PAIR):
                    b_ = wait_free(pe, l, i, "RL", j, "EV")
                    mm(b_[0:E_N, 0:S], [(W3["r"][:, k, :], comb(j)(k)) for k in range(4)]).then_inc(full.sem, 1)
                for j in range(PAIR):
                    b_ = wait_free(pe, l, i, "RT", j, "RL")
                    hold(pe)
                    for t in range(QT):
                        last = nc.tensor.transpose(b_[:, t * E_N:(t + 1) * E_N], logT[:, j, t * P:(t + 1) * P], ident[0:E_N, 0:E_N])
                    last.then_inc(full.sem, 1)
                for j in range(PAIR):
                    for m in range(M3 // 2):
                        ws, at = (w["e1"][:, m // 2], m % 2 * 2 * P) if m < 2 * E_N else (w["g1"], 0)
                        channels_out(l, i, f"M{m}", j, ws, at, comb(j), ks=4)
                for j in range(PAIR):
                    hid = hidden(j, l)
                    for e in range(E_N):
                        tokens_out(l, i, f"E{e}", j, w["e2"][:, e], 0, lambda k: hid[:, 4 * e + k, :], f"M{M3 // 2 - 1}", ks=4)
                for j in range(PAIR):
                    hid = hidden(j, l)
                    tokens_out(l, i, "GO", j, w["g2"], 0, lambda k: hid[:, 4 * E_N + k, :])
                for j in range(PAIR):
                    b_ = wait_free(pe, l, i, "RR", j, f"E{E_N - 1}")
                    for t in range(QT):
                        for c in range(CT):
                            last = nc.tensor.transpose(b_[:, c * S + t * P:c * S + (t + 1) * P], xh[:, j, t, c * P:(c + 1) * P], ident[:, :])
                    last.then_inc(full.sem, 1)
                for j in range(PAIR):
                    tokens_out(l, i, "OUT", j, W3["out"], 0, lambda k: hT[:, j, k, :], "RR")

        @block.scalar
        def _(act):
            uses = [0]

            def pre_bank():
                u = uses[0]
                uses[0] += 1
                act.wait_ge(s_pre_full, u + 1)
                return pj[u % 2]

            ident_ = lambda o, x, **kw: nc.scalar.activation(o, x, ACT.Identity, **kw)
            copy_ = lambda o, x: nc.scalar.activation(o, x, ACT.Copy)
            act.wait_ge(s_in, 16 * PRE_LOADS)
            nc.scalar.activation(srow, crow, ACT.Silu).then_inc(s_pre_act, 1)
            b_ = pre_bank()
            copy_(cT[:, :, :].rearrange("p c b -> p (c b)"), b_[:, 0:CT * B])
            copy_(scT[:, :, :].rearrange("p c b -> p (c b)"), b_[:, CT * B:2 * CT * B])
            for n, c in enumerate((VC(1, "b_qkv"), VC(1, "b_q"), VC(2, "b_qkv"), VC(2, "b_qc"))):
                nc.scalar.activation(bq[:, n // 2, n % 2 * 2:n % 2 * 2 + 2], b_[:, P + c:P + c + 2], ACT.Copy, scale=SCALE)
            copy_(vec[:, :], b_[:, P:P + NROW]).then_inc(s_pre_empty, 1)
            uses[0] += sum(NPRE)
            for l in range(3):
                b_ = pre_bank()
                at = 0
                for n, m in enumerate(MOD[l]):
                    if m is None:
                        continue
                    for what in range(2):
                        o = mods[:, l, 4 * n + 2 * what:4 * n + 2 * what + 2, :]
                        src = b_[:, at:at + CT * B].rearrange("p (c b) -> p c b", c=CT)
                        if what == 0:
                            last = copy_(o, src)
                        elif l > 0:
                            last = ident_(o, src, bias=1.0)
                        else:
                            for c in range(CT):
                                wc = vec[:, 2 * n + c:2 * n + c + 1]
                                last = ident_(o[:, c, :], src[:, c, :], bias=wc, scale=wc)
                        at += CT * B
                last.then_inc(s_pre_empty, 1)
            for dst in (ctxT, ctxnT):
                for b0 in range(0, B, 3):
                    nb = min(3, B - b0)
                    b_ = pre_bank()
                    for c in range(CT):
                        last = copy_(dst[:, c, b0 * SC:(b0 + nb) * SC], b_[:, c * 3 * SC:(c * 3 + nb) * SC])
                    last.then_inc(s_pre_empty, 1)
            act.drain().then_inc(s_phase, 1)
            act.wait_ge(s_phase, 5)

            def context_keys(l):
                for c in range(CT):
                    for n in range(0, B * SC, 512):
                        w = min(512, B * SC - n)
                        b_ = pre_bank()
                        o = kcT[:, c, n:n + w]
                        if l in BKC:
                            last = ident_(o, b_[:, 0:w], bias=vec[:, BKC[l] + c:BKC[l] + c + 1])
                        else:
                            last = copy_(o, b_[:, 0:w])
                        last.then_inc(s_pre_empty, 1)

            def channels(l, i, j, n):
                wait_full(act, l, i, f"T{n}", j)
                b_ = bank_of(l, f"T{n}", j)
                for c in range(CT):
                    if l == 3:
                        sc, bi = vec[:, VC(3, "ln_gamma") + c:][:, 0:1], vec[:, VC(3, "ln_beta") + c:][:, 0:1]
                    else:
                        sc, bi = cols[:, j, 4 * n + 2 + c:4 * n + 3 + c], cols[:, j, 4 * n + c:4 * n + c + 1]
                    if l == 2 and n == 1:
                        last = copy_(hT[:, j, c, :], b_[:, c * S:(c + 1) * S])
                    elif l == 1 and n == 0:
                        ident_(hT[:, j, c, 0:S - SHIFT], b_[:, c * S + SHIFT:(c + 1) * S], bias=bi, scale=sc)
                        last = ident_(hT[:, j, c, S - SHIFT:S], b_[:, c * S:c * S + SHIFT], bias=bi, scale=sc)
                    else:
                        last = ident_(hT[:, j, c, :], b_[:, c * S:(c + 1) * S], bias=bi, scale=sc)
                last.then_inc(emptied["A"].sem, 1)

            def queries(l, i, j, cross):
                name = "QC" if cross else "Q"
                wait_full(act, l, i, name, j)
                b_ = bank_of(l, name, j)
                scale = SCALE3 if l == 3 else SCALE
                if l in (1, 2):
                    for c in range(CT):
                        bias = bq[:, l - 1, 2 * cross + c:2 * cross + c + 1]
                        last = ident_(qT[:, j, c, :], b_[:, c * S:(c + 1) * S], bias=bias, scale=scale)
                else:
                    last = nc.scalar.activation(qT[:, j].rearrange("p c s -> p (c s)"), b_[:, :], ACT.Copy, scale=scale)
                last.then_inc(emptied["A"].sem, 1)

            def attention(l, i, cross):
                hg, kts, width, kp_, first = shape(l, cross)
                total = PAIR * groups(hg)
                for step in range(total + 2):
                    if step < total:
                        n = first + step
                        wait_group(act, maxed, l, i, n)
                        wait_group(act, turned, l, i, n - 4)
                        keys_ = SC if cross else width
                        for x in range(hg):
                            last = nc.scalar.activation(probs[:, n % 4, x * width:x * width + keys_], ps[n % 2][:, x * width:x * width + keys_],
                                                        ACT.Exp, bias=nmax[:, n % 4, x:x + 1])
                        last.then_inc(exped.sem, 1)
                    if 0 <= step - 2 < total and step % 2 == 0:
                        n = first + step - 2
                        wait_group(act, turned, l, i, n)
                        wait_group(act, summed, l, i, n - 4)
                        copy_(probsT[0:kp_, n % 4, :], pt[n % 2][0:kp_, :]).then_inc(copied[0].sem, 1)

            def values(l, i, j):
                wait_full(act, l, i, "VC", j)
                b_ = bank_of(l, "VC", j)
                if l == 3:
                    last = copy_(V3(VP, j), b_[0:SCP, 0:D])
                else:
                    last = copy_(padded(VP, j, 0, SCP), b_[0:SCP, 0:D].rearrange("p (h e d) -> p h e d", e=2, d=HD))
                last.then_inc(emptied["A"].sem, 1)

            for l in range(3):
                context_keys(l)
                with act.Fori(0, TURNS) as i:
                    for j in range(PAIR):
                        act.wait_ge(picked.sem, picked.of(l, i, j + 1))
                        channels(l, i, j, 0)
                    for j in range(PAIR):
                        queries(l, i, j, 0)
                        if l == 0:
                            wait_full(act, l, i, "K", j)
                            copy_(kT[:, j].rearrange("p c s -> p (c s)"), bank_of(l, "K", j)[:, :]).then_inc(emptied["A"].sem, 1)
                    attention(l, i, 0)
                    for j in range(PAIR):
                        values(l, i, j)
                    for j in range(PAIR):
                        channels(l, i, j, 1)
                    for j in range(PAIR):
                        queries(l, i, j, 1)
                    attention(l, i, 1)
                    for j in range(PAIR):
                        channels(l, i, j, 2)
                    for j in range(PAIR):
                        hid = hidden(j, l)
                        for m in range(HT_N if l == 1 else HT_N // 2):
                            wait_full(act, l, i, f"M{m}", j)
                            b_ = bank_of(l, f"M{m}", j)
                            if l == 1:
                                nc.scalar.activation(hid[:, m, :], b_[:, 0:S], ACT.Silu, bias=vec[:, B1[l] + m:B1[l] + m + 1]).then_inc(silu_done.sem, 1)
                            else:
                                for x in range(2):
                                    k = 2 * m + x
                                    last = nc.scalar.activation(hid[:, k, :], b_[:, x * S:(x + 1) * S], ACT.Gelu_apprx_tanh, bias=vec[:, B1[l] + k:B1[l] + k + 1])
                                last.then_inc(emptied["A"].sem, 1)
                layer_done(act, l + 1)

            l = 3
            context_keys(3)
            b_ = pre_bank()
            copy_(anchor[:, :, :].rearrange("p m b -> p (m b)"), b_[:, 0:M3 * B])
            nc.scalar.activation(ranchor[:, 0:B], b_[0:E_N, M3 * B:(M3 + 1) * B], ACT.Identity, bias=rb[:, 0:1]).then_inc(s_pre_empty, 1)
            with act.Fori(0, TURNS) as i:
                for j in range(PAIR):
                    channels(l, i, j, 0)
                    values(l, i, j)
                for j in range(PAIR):
                    queries(l, i, j, 0)
                for j in range(PAIR):
                    act.wait_ge(dve3.sem, dve3.of(l, i, 1 + j))
                    b_ = bank_of(l, "S", j)
                    for t in range(QT):
                        last = nc.scalar.activation(probs[:, j, t * SC:(t + 1) * SC], b_[:, t * SC:(t + 1) * SC], ACT.Exp,
                                                    bias=nmax[:, j, t:t + 1], accum_out=small[:, j, t, 0:1])
                    last.then_inc(emptied["A"].sem, 1)
                for j in range(PAIR):
                    wait_full(act, l, i, "PT", j)
                    copy_(probsT[0:SCP, j, 0:S], bank_of(l, "PT", j)[0:SCP, 0:S]).then_inc(emptied["A"].sem, 1)
                for j in range(PAIR):
                    wait_full(act, l, i, "EV", j)
                    copy_(qT[:, j].rearrange("p c s -> p (c s)"), bank_of(l, "EV", j)[:, :]).then_inc(emptied["A"].sem, 1)
                for j in range(PAIR):
                    act.wait_ge(picked.sem, picked.of(l, i, j + 1))
                    wait_full(act, l, i, "RL", j)
                    ident_(logT[:, j, :], bank_of(l, "RL", j)[0:E_N, 0:S], bias=ranc[:, j:j + 1]).then_inc(emptied["A"].sem, 1)
                for j in range(PAIR):
                    wait_taken(act, l, i, "RT", j)
                    for t in range(QT):
                        last = nc.scalar.activation(rp[:, j, t, :], rp[:, j, t, :], ACT.Exp, accum_out=small[:, j, t, 1:2])
                    last.then_inc(act3.sem, 1)
                for j in range(PAIR):
                    hid = hidden(j, l)
                    for m in range(M3 // 2):
                        wait_full(act, l, i, f"M{m}", j)
                        b_ = bank_of(l, f"M{m}", j)
                        for x in range(2):
                            k = 2 * m + x
                            last = nc.scalar.activation(hid[:, k, :], b_[:, x * S:(x + 1) * S], ACT.Silu, bias=anc[:, j, k:k + 1])
                        last.then_inc(emptied["A"].sem, 1)
                for j in range(PAIR):
                    wait_taken(act, l, i, "GO", j)
                    g = kT[:, j].rearrange("p c s -> p (c s)")
                    nc.scalar.activation(g, g, ACT.Tanh, scale=0.5).then_inc(act3.sem, 1)
                for j in range(PAIR):
                    wait_full(act, l, i, "RR", j)
                    copy_(hT[:, j].rearrange("p c s -> p (c s)"), bank_of(l, "RR", j)[:, :]).then_inc(emptied["A"].sem, 1)

        @block.vector
        def _(dve):
            vector_engine[0] = dve
            links = [0]
            where = [None, None]

            def link(ins):
                links[0] += 1
                ins.then_inc(dve_own.sem, 1)

            def settle():
                l, i = where
                dve.wait_ge(dve_own.sem, dve_own.of(l, i, links[0]))

            uses = [1]
            pre = [0]

            def pre_link(ins, wait=True):
                pre[0] += 1
                ins.then_inc(s_pre_dve, 1)
                if wait:
                    dve.wait_ge(s_pre_dve, pre[0])

            dve.wait_ge(s_in, 16 * PRE_LOADS)
            ctx_tok = stage[0:SC, 0:B * D].rearrange("p (b d) -> p b d", b=B)
            st = rden[0:SC, 32:32 + 6 * B].rearrange("p (b s) -> p b s", b=B)
            mvc = rden[0:SC, 128:128 + 2 * B].rearrange("p (b s) -> p b s", b=B)
            for b in range(B):
                pre_link(nc.vector.bn_stats(st[:, b, :], ctx_tok[:, b, :]), b == B - 1)
            for b in range(B):
                pre_link(nc.vector.bn_aggr(mvc[:, b, :], st[:, b, :]), b == B - 1)
            pre_link(nc.vector.tensor_scalar(rden[0:SC, 8:16], mvc[:, :, 1], EPS[2], None, ALU.add))
            assert pre[0] == PRE_DVE_VAR, pre[0]
            for m, mb in ((maskS, maskSb), (maskC, maskCb)):
                pre_link(nc.vector.tensor_copy(m[:, :, :], mb[:, :, :]))
                pre_link(nc.vector.tensor_scalar(m[:, :, :], m[:, :, :], 1.0, -NEG, ALU.subtract, ALU.mult))
            for l in range(3):
                for n in range(0, ADA_N[l], 512):
                    w = min(512, ADA_N[l] - n)
                    dve.wait_ge(s_pre_full, uses[0] + 1)
                    b_ = pj[uses[0] % 2]
                    uses[0] += 1
                    r = mod_rows(KM, l)[:, n:n + w]
                    nc.vector.tensor_tensor(r, b_[0:B, 0:w], r, ALU.add).then_inc(s_rows, 1)
            dve.wait_ge(s_pre_full, PRE_RAW)
            dve.wait_ge(s_pre_pool, 8)
            for b in range(B):
                pre_link(nc.vector.tensor_scalar(ctx_tok[:, b, :], ctx_tok[:, b, :], mvc[:, b, 0:1], rden[0:SC, 16 + b:17 + b], ALU.subtract, ALU.mult), False)
            assert pre[0] == PRE_DVE_CTX, pre[0]
            dve.drain().then_inc(s_phase, 1)
            dve.wait_ge(s_phase, 5)

            def statistics(l, i, j, n):
                b = i * PAIR + j
                hold(dve)
                for t in range(QT):
                    link(nc.vector.bn_stats(stats[:, j, t, :], X[:, bass.ds(b, 1), t, :].rearrange("p o d -> p (o d)")))
                settle()
                hold(dve)
                for t in range(QT):
                    link(nc.vector.bn_aggr(mv[:, j, t, :], stats[:, j, t, :]))
                settle()
                nc.vector.tensor_scalar(ve[:, j, :], mv[:, j, :, 1], EPS[l], None, ALU.add).then_inc(var_ready.sem, 1)

            def normalise(l, i, j, n):
                b = i * PAIR + j
                dve.wait_ge(rstd_ready.sem, rstd_ready.of(l, i, 2 * n + j + 1))
                for t in range(QT):
                    last = nc.vector.tensor_scalar(xh[:, j, t, :], X[:, bass.ds(b, 1), t, :].rearrange("p o d -> p (o d)"),
                                                   mv[:, j, t, 0:1], rstd[:, j, t:t + 1], ALU.subtract, ALU.mult)
                last.then_inc(xh_ready.sem, 1)

            def residual(l, i, j, n, name):
                b = i * PAIR + j
                wait_full(dve, l, i, name, j)
                b_ = bank_of(l, name, j)[:, :].rearrange("p (t d) -> p t d", t=QT)
                u = kT[:, j].rearrange("p c s -> p (c s)").rearrange("p (t d) -> p t d", t=QT)
                gate = not (l == 2 and n == 1)
                x = X[:, bass.ds(b, 1)].rearrange("p o t d -> p (o t) d")
                row = BROW_AT[l].get(n)
                g = gates[:, j, n, :].unsqueeze(1).to_broadcast([P, QT, D])
                if n == 0:
                    dve.wait_ge(gates_in[j].sem, gates_in[j].of(l, i, 16))
                if row is not None:
                    bb = brow[:, row, :].unsqueeze(1).to_broadcast([P, QT, D])
                    nc.vector.tensor_tensor(u, b_, bb, ALU.add).then_inc(emptied["V"].sem, 1)
                    wait_taken(dve, l, i, name, j)
                    if gate:
                        link(nc.vector.tensor_tensor(u, u, g, ALU.mult))
                        settle()
                else:
                    nc.vector.tensor_tensor(u, b_, g, ALU.mult).then_inc(emptied["V"].sem, 1)
                    wait_taken(dve, l, i, name, j)
                nc.vector.tensor_tensor(x, x, u, ALU.add).then_inc(added.sem, 1)
                dve.wait_ge(added.sem, added.of(l, i, 2 * n + j + 1))

            def rope(l, i, j):
                wait_taken(dve, l, i, "Q", j)
                wait_taken(dve, l, i, "K", j)
                hold(dve)
                swap = stage[:, j * 1024:(j + 1) * 1024]
                n = swap.shape[1] // P // 2
                c, s = (m[:, :].unsqueeze(1).to_broadcast([P, n, P]) for m in (cosT, sinT))
                for x, raw in enumerate((qT, kT)):
                    r = raw[:, j].rearrange("p c s -> p (c s)")
                    link(nc.vector.stream_shuffle(swap[:, x * 512:(x + 1) * 512], r, [p ^ (HD // 2) for p in range(32)]))
                settle()
                for x, raw in enumerate((qT, kT)):
                    r = raw[:, j].rearrange("p c s -> p (c s)").rearrange("p (n w) -> p n w", w=P)
                    w = swap[:, x * 512:(x + 1) * 512].rearrange("p (n w) -> p n w", w=P)
                    link(nc.vector.tensor_tensor(r, r, c, ALU.mult))
                    link(nc.vector.tensor_tensor(w, w, s, ALU.mult))
                settle()
                for x, raw in enumerate((qT, kT)):
                    r = raw[:, j].rearrange("p c s -> p (c s)")
                    last = nc.vector.tensor_tensor(r, r, swap[:, x * 512:(x + 1) * 512], ALU.add)
                last.then_inc(rope_ready.sem, 1)

            def keys(l, i, j):
                wait_full(dve, l, i, "K", j)
                b_ = bank_of(l, "K", j)
                for c in range(CT):
                    last = nc.vector.tensor_scalar(kT[:, j, c, :], b_[:, c * S:(c + 1) * S], vec[:, BK[l] + c:BK[l] + c + 1], None, ALU.add)
                last.then_inc(emptied["V"].sem, 1)

            def values(l, i, j):
                wait_full(dve, l, i, "V0", j)
                b_ = bank_of(l, "V0", j)
                for t in range(QT):
                    last = nc.vector.tensor_copy(padded(VP, j, t, P), b_[:, t * D:(t + 1) * D].rearrange("p (h e d) -> p h e d", e=2, d=HD))
                last.then_inc(emptied["V"].sem, 1)

            def heads_out(l, i, j, cross):
                first = shape(l, cross)[4]
                half = groups(shape(l, cross)[0])
                wait_group(dve, summed, l, i, first + (j + 1) * half - 1)
                link(nc.vector.reciprocal(rden[:, :], pn[:, :]))
                settle()
                o = oT[:, j].rearrange("p c s -> p (c s)")
                bias = BV.get((l, cross))
                if l == 1 and not cross:
                    ov = o.rearrange("p (c s) -> p c s", c=CT)
                    pv = po[:, :].rearrange("p (c s) -> p c s", c=CT)
                    rv = rden[:, :].rearrange("p (c s) -> p c s", c=CT)
                    link(nc.vector.tensor_tensor(ov[:, :, SHIFT:S], pv[:, :, 0:S - SHIFT], rv[:, :, 0:S - SHIFT], ALU.mult))
                    last = nc.vector.tensor_tensor(ov[:, :, 0:SHIFT], pv[:, :, S - SHIFT:S], rv[:, :, S - SHIFT:S], ALU.mult)
                else:
                    last = nc.vector.tensor_tensor(o, po[:, :], rden[:, :], ALU.mult)
                if bias is None:
                    last.then_inc(normed.sem, 1)
                    return
                link(last)
                settle()
                for c in range(CT):
                    last = nc.vector.tensor_scalar(oT[:, j, c, :], oT[:, j, c, :], vec[:, bias + c:bias + c + 1], None, ALU.add)
                last.then_inc(normed.sem, 1)

            def maxima(l, i, cross, step):
                hg, kts, width, kp_, first = shape(l, cross)
                n = first + step
                j, qt, _ = parts(l, cross, step)
                wait_group(dve, scored, l, i, n)
                wait_group(dve, exped, l, i, n - 4)
                keys_ = SC if cross else width
                sc = ps[n % 2][:, 0:hg * width].rearrange("p (h k) -> p h k", h=hg)[:, :, 0:keys_]
                if l == 0:
                    hold(dve)
                    for x in range(hg):
                        m = maskCj[:, j, :] if cross else maskS[:, qt, :]
                        link(nc.vector.tensor_tensor_reduce(sc[:, x, :], sc[:, x, :], m, 1.0, NEG, ALU.add, ALU.max, top1[:, n % 4, x:x + 1]))
                    settle()
                    nc.vector.tensor_scalar(nmax[:, n % 4, 0:hg], top1[:, n % 4, 0:hg], -1.0, None, ALU.mult).then_inc(maxed.sem, 1)
                elif l == 1 and cross:
                    hold(dve)
                    for x in range(hg):
                        link(nc.vector.max(top1[:, x, :], sc[:, x, :]))
                    settle()
                    hold(dve)
                    for x in range(hg):
                        link(nc.vector.match_replace(left1[:, x, :], top1[:, x, :], sc[:, x, :], TAKEN))
                    nc.vector.tensor_scalar(nmax[:, n % 4, 0:hg], top1[:, :, 0], -1.0, None, ALU.mult).then_inc(maxed.sem, 1)
                    settle()
                    hold(dve)
                    for x in range(hg):
                        link(nc.vector.max(top2[:, x, :], left1[:, x, :]))
                    settle()
                    hold(dve)
                    for x in range(hg):
                        link(nc.vector.match_replace(left2[:, n % 2, x, :], top2[:, x, :], left1[:, x, :], TAKEN))
                else:
                    nc.vector.tensor_reduce(nmax[:, n % 4, 0:hg], sc, AX_X, ALU.max, negate=True).then_inc(maxed.sem, 1)

            def attention(l, i, cross):
                hg, kts, width, kp_, first = shape(l, cross)
                total = PAIR * groups(hg)
                half = total // 2
                for step in range(total + 4):
                    if step in (half + 3, total + 3):
                        heads_out(l, i, step // half - 1, cross)
                    if step < total:
                        maxima(l, i, cross, step)
                    if l == 1 and cross and 0 <= step - 1 < total:
                        n = first + step - 1
                        wait_group(dve, exped, l, i, n)
                        settle()
                        p = probs[:, n % 4, 0:hg * width].rearrange("p (h k) -> p h k", h=hg)[:, :, 0:SC]
                        nc.vector.scalar_tensor_tensor(p, left2[:, n % 2], TAKEN, p, ALU.is_equal, ALU.mult).then_inc(chosen.sem, 1)
                    if 0 <= step - 2 < total and step % 2 == 1:
                        n = first + step - 2
                        wait_group(dve, turned, l, i, n)
                        wait_group(dve, summed, l, i, n - 4)
                        nc.vector.tensor_copy(probsT[0:kp_, n % 4, :], pt[n % 2][0:kp_, :]).then_inc(copied[1].sem, 1)

            for l in range(3):
                with dve.Fori(0, TURNS) as i:
                    links[0] = 0
                    where[:] = [l, i]
                    for j in range(PAIR):
                        statistics(l, i, j, 0)
                    for j in range(PAIR):
                        normalise(l, i, j, 0)
                    for j in range(PAIR):
                        if l > 0:
                            keys(l, i, j)
                        values(l, i, j)
                        if l == 0:
                            rope(l, i, j)
                    attention(l, i, 0)
                    if l > 0:
                        dve.wait_ge(s_brow, sum(BROW_N[:l + 1]))
                    for j in range(PAIR):
                        residual(l, i, j, 0, "O")
                        statistics(l, i, j, 1)
                    for j in range(PAIR):
                        normalise(l, i, j, 1)
                    attention(l, i, 1)
                    for j in range(PAIR):
                        residual(l, i, j, 1, "OC")
                        statistics(l, i, j, 2)
                    for j in range(PAIR):
                        normalise(l, i, j, 2)
                    if l == 1:
                        for j in range(PAIR):
                            hid = hidden(j, l)
                            for m in range(HT_N):
                                k = j * HT_N + m + 1
                                dve.wait_ge(silu_done.sem, silu_done.of(l, i, k))
                                b_ = bank_of(l, f"M{m}", j)
                                c = B1[l] + HT_N + m
                                nc.vector.scalar_tensor_tensor(hid[:, m, :], b_[:, S:2 * S], vec[:, c:c + 1], hid[:, m, :], ALU.add, ALU.mult).then_inc(emptied["V"].sem, 1)
                    if l == 0:
                        dve.wait_ge(s_brow, BROW_N[0])
                    for j in range(PAIR):
                        residual(l, i, j, 2, "MO")
                    LINKS[l] = links[0]
                layer_done(dve, l + 1)

            l = 3
            dve.wait_ge(s_brow, sum(BROW_N))
            dve.wait_ge(s_pre_empty, KEYS_IN[3] + 1)
            bh = vec[:, VC(3, "e_b1"):VC(3, "e_b1") + M3].unsqueeze(2).to_broadcast([P, M3, B])
            nc.vector.tensor_tensor(anchor[:, :, :], anchor[:, :, :], bh, ALU.add).then_inc(s_mask, 1)
            with dve.Fori(0, TURNS) as i:
                links[0] = 0
                where[:] = [l, i]
                for j in range(PAIR):
                    statistics(l, i, j, 0)
                for j in range(PAIR):
                    normalise(l, i, j, 0)
                for j in range(PAIR):
                    wait_full(dve, l, i, "S", j)
                    sc = bank_of(l, "S", j)[:, 0:QT * SC].rearrange("p (t k) -> p t k", t=QT)
                    nc.vector.tensor_reduce(nmax[:, j, 0:QT], sc, AX_X, ALU.max, negate=True).then_inc(dve3.sem, 1)
                for j in range(PAIR):
                    wait_taken(dve, l, i, "S", j)
                    link(nc.vector.reciprocal(small[:, j, :, 0], small[:, j, :, 0]))
                    settle()
                    for t in range(QT):
                        p = probs[:, j, t * SC:(t + 1) * SC]
                        last = nc.vector.tensor_scalar(p, p, small[:, j, t, 0:1], None, ALU.mult)
                    last.then_inc(dve3.sem, 1)
                for j in range(PAIR):
                    wait_full(dve, l, i, "RT", j)
                    b_ = bank_of(l, "RT", j)[:, 0:QT * E_N].rearrange("p (t e) -> p t e", t=QT)
                    link(nc.vector.tensor_reduce(nmax[:, 2 + j, 0:QT], b_, AX_X, ALU.max))
                    settle()
                    nc.vector.tensor_tensor(rp[:, j, :, :], b_, nmax[:, 2 + j, 0:QT].unsqueeze(2).to_broadcast([P, QT, E_N]), ALU.subtract).then_inc(emptied["V"].sem, 1)
                for j in range(PAIR):
                    act3_k = 1 + j
                    dve.wait_ge(act3.sem, act3.of(l, i, act3_k))
                    link(nc.vector.reciprocal(small[:, j, :, 1], small[:, j, :, 1]))
                    settle()
                    link(nc.vector.tensor_tensor(rp[:, j, :, :], rp[:, j, :, :], small[:, j, :, 1:2].to_broadcast([P, QT, E_N]), ALU.mult))
                    settle()
                    for t in range(QT):
                        link(nc.vector.tensor_scalar(xh[:, j, t, :], brow[:, 0, :], rp[:, j, t, 0:1], None, ALU.mult))
                    for e in range(1, E_N):
                        settle()
                        for t in range(QT):
                            link(nc.vector.scalar_tensor_tensor(xh[:, j, t, :], brow[:, e, :], rp[:, j, t, e:e + 1], xh[:, j, t, :], ALU.mult, ALU.add))
                settle()
                for j in range(PAIR):
                    for e in range(E_N):
                        wait_full(dve, l, i, f"E{e}", j)
                        b_ = bank_of(l, f"E{e}", j)
                        for t in range(QT):
                            last = nc.vector.scalar_tensor_tensor(xh[:, j, t, :], b_[:, t * D:(t + 1) * D], rp[:, j, t, e:e + 1], xh[:, j, t, :], ALU.mult, ALU.add)
                        last.then_inc(emptied["V"].sem, 1)
                        wait_taken(dve, l, i, f"E{e}", j)
                for j in range(PAIR):
                    wait_full(dve, l, i, "GO", j)
                    g = kT[:, j].rearrange("p c s -> p (c s)").rearrange("p (t d) -> p t d", t=QT)
                    b_ = bank_of(l, "GO", j)[:, :].rearrange("p (t d) -> p t d", t=QT)
                    nc.vector.tensor_tensor(g, b_, brow[:, 3, :].unsqueeze(1).to_broadcast([P, QT, D]), ALU.add).then_inc(emptied["V"].sem, 1)
                for j in range(PAIR):
                    b = i * PAIR + j
                    g = kT[:, j].rearrange("p c s -> p (c s)").rearrange("p (t d) -> p t d", t=QT)
                    u = probs[:, j, :].rearrange("p (t d) -> p t d", t=QT)
                    dve.wait_ge(act3.sem, act3.of(l, i, 3 + j))
                    link(nc.vector.tensor_scalar(g, g, 1.0, 0.5, ALU.add, ALU.mult))
                    wait_full(dve, l, i, "OUT", j)
                    b_ = bank_of(l, "OUT", j)[:, :].rearrange("p (t d) -> p t d", t=QT)
                    nc.vector.tensor_tensor(u, b_, brow[:, 4, :].unsqueeze(1).to_broadcast([P, QT, D]), ALU.add).then_inc(emptied["V"].sem, 1)
                    settle()
                    wait_taken(dve, l, i, "OUT", j)
                    link(nc.vector.tensor_tensor(u, u, g, ALU.mult))
                    settle()
                    x = X[:, bass.ds(b, 1)].rearrange("p o t d -> p (o t) d")
                    nc.vector.tensor_tensor(x, x, u, ALU.add).then_inc(added.sem, 1)
                LINKS[3] = links[0]
        assert tuple(LINKS[l] for l in range(4)) == DVE_LINKS, LINKS


def kernel(**inputs):
    import numpy as np
    import concourse.bacc as bacc
    from concourse.bass_utils import run_bass_kernel_spmd as run

    nc = bacc.Bacc("TRN2", target_bir_lowering=False, num_devices=1)
    arrays = {}
    for name, x in inputs.items():
        x = np.ascontiguousarray(x)
        arrays[name] = x.reshape(-1).view(np.int32) if x.dtype == np.bool_ else x
    inv = 1.0 / 10000.0 ** (np.arange(0, HD, 2, dtype=np.float32) / HD)
    freqs = np.outer(np.arange(P, dtype=np.float32), inv)
    emb = np.concatenate([freqs, freqs], axis=-1)
    sign = np.where(np.arange(HD) < HD // 2, -1.0, 1.0).astype(np.float32)
    arrays["rope_cos"] = np.ascontiguousarray(np.tile(np.cos(emb).astype(np.float32).T, (HPT, 1)))
    arrays["rope_sin"] = np.ascontiguousarray(np.tile((np.sin(emb).astype(np.float32) * sign).T, (HPT, 1)))
    aps = {n: nc.dram_tensor(f"in_{n}", x.shape, mybir.dt.from_np(x.dtype), kind="ExternalInput").ap() for n, x in arrays.items()}
    out = nc.dram_tensor("out", (B, S, D), F32, kind="ExternalOutput").ap()
    build(nc, aps, out)
    r = run(nc, [{f"in_{n}": x for n, x in arrays.items()}], core_ids=[0])
    return r.results[0]["out"]
```

```python
from contextlib import ExitStack

import concourse.bass as bass
from concourse import mybir

ALU = mybir.AluOpType
ACT = mybir.ActivationFunctionType
F32 = mybir.dt.float32
U8 = mybir.dt.uint8
I32 = mybir.dt.int32
AX_X = mybir.AxisListType.X

P = 128
B, S, D = 8, 256, 256
SC = 77
SCP = 96
H, HD = 16, 16
CT = D // P
QT = S // P
HPT = P // HD
PAIR = 2
TURNS = B // PAIR
HID = 4 * D
HT_N = HID // P
E_N, RH = 3, 512
M3 = E_N * RH // P + CT
NEG = -3.4028234663852886e38
TAKEN = -3.0e38
SCALE = HD ** -0.5
SCALE3 = D ** -0.5
EPS = (1e-5, 1e-6, 1e-6, 1e-5)
SHIFT = 64
W_EVEN, W_ODD = 8192, 12288

SELF = {0: (2, 2), 1: (4, 1), 2: (2, 2)}
CROSS = (4, 1)


def groups(hg):
    return QT * H // hg


class Mark:

    def __init__(self, sem, per):
        self.sem, self.per, self.credit = sem, per, max(per)

    def base(self, l):
        return self.credit + TURNS * sum(self.per[:l])

    def of(self, l, i, k):
        return i * self.per[l] + (self.base(l) + k)

    def before(self, l, i, k):
        return i * self.per[l] + (self.base(l) - self.per[l] + k)


SUM_LAG = 4
VALUES_AT, OUT_AT, TURN_AT, QUERY_AT = SUM_LAG - 1, SUM_LAG, 6, 7
RES_LAG, NORM_LAG = 0, 1


def ends(l):
    a, c = NSELF[l] // 2, NCROSS // 2
    return [a, 2 * a, 2 * a + c, 2 * a + 2 * c]


def between(l):
    e = ends(l)
    at = {}
    for j in range(PAIR):
        for d, name in ((VALUES_AT, "VC"), (OUT_AT, "O"), (TURN_AT, "T1"), (QUERY_AT, "QC")):
            at.setdefault(e[j] + d, []).append((name, j))
    for d, name in ((OUT_AT, "OC"), (TURN_AT, "T2")):
        at.setdefault(e[2] + d, []).append((name, 0))
    return at


def tail(l):
    m = [f"M{x}" for x in range(HT_N if l == 1 else HT_N // 2)]
    first = [(x, 0) for x in m]
    if l == 1:
        first[5:5] = [("T2", 1)]
    else:
        first[4:4] = [("T2", 1)]
    first[1:1] = [("OC", 1)]
    return first + [("MO", 0)] + [(x, 1) for x in m] + [("MO", 1)]


def projection_uses(l):
    both = lambda *names: [(n, j, o) for j in range(PAIR) for n, o in names]
    if l < 3:
        uses = both(("T0", "A"))
        uses += both(("K", "A" if l == 0 else "V"), ("Q", "A"), ("V0", "V"))
        owner = {"VC": "A", "O": "V", "T1": "A", "QC": "A", "OC": "V", "T2": "A", "MO": "V"}
        rest = [x for step in sorted(between(l)) for x in between(l)[step]] + tail(l)
        uses += [(n, j, owner.get(n, "V" if l == 1 else "A")) for n, j in rest]
    else:
        uses = both(("T0", "A"), ("VC", "A"))
        uses += both(("Q", "A")) + both(("S", "A")) + both(("PT", "A"))
        uses += both(("EV", "A")) + both(("RL", "A")) + both(("RT", "V"))
        uses += both(*[(f"M{m}", "A") for m in range(M3 // 2)])
        uses += both(*[(f"E{e}", "V") for e in range(E_N)])
        uses += both(("GO", "V")) + both(("RR", "A")) + both(("OUT", "V"))
    return uses


NSELF = [PAIR * groups(SELF[l][0]) for l in range(3)]
NCROSS = PAIR * groups(CROSS[0])
NG = [n + NCROSS for n in NSELF] + [0]
USES = [projection_uses(l) for l in range(4)]
INDEX = [{(n, j): k for k, (n, j, _) in enumerate(u)} for u in USES]
ORDER = [[sum(x[2] == u[k][2] for x in u[:k + 1]) for k in range(len(u))] for u in USES]
COUNT = {o: [sum(x[2] == o for x in u) for u in USES] for o in "AV"}
NLN = (3, 3, 3, 1)



def by_vector(l, n):
    return n % 2 == 1 and not (l == 1 and n >= NSELF[l])


VECTORS = [("L0_xcond_norm1_w", 2), ("L0_xcond_normc_w", 2), ("L0_xcond_norm2_w", 2), ("L0_xcond_mlp_b1", 8),
           ("L1_xcond_b_qkv", 6), ("L1_xcond_b_q", 2), ("L1_xcond_b_kv", 4), ("L1_xcond_b_m1", 16),
           ("L2_xcond_b_qkv", 6), ("L2_xcond_b_qc", 2), ("L2_xcond_b_kvc", 4), ("L2_xcond_b_mlp1", 8),
           ("L3_xcond_ln_gamma", 2), ("L3_xcond_ln_beta", 2), ("L3_xcond_e_b1", 12), ("L3_xcond_gate_b1", 2)]
ROW, NROW = {}, 0
for _n, _k in VECTORS:
    ROW[_n] = NROW
    NROW += _k

NPRE = [(9 * D + 511) // 512, (9 * D + 511) // 512, (6 * D + 511) // 512]
ROWS_IN = [sum(NPRE[:l + 1]) for l in range(3)]
PRE_MODS = 1 + ROWS_IN[2] + 3
PRE_RAW = PRE_MODS + 3
PRE_ALL = PRE_RAW + 3
KEY_BANKS = CT * ((B * SC + 511) // 512)
KEYS_IN = [PRE_ALL - ROWS_IN[2] + (l + 1) * KEY_BANKS for l in range(4)]
PRE_LOADS = 2 + len(VECTORS) + 3 + 6

FIRST = 8
DVE_LINKS = (170, 296, 36, 32)


def mod_rows(KM, l):
    n = (0, 9 * D, 18 * D, 24 * D)
    return KM[0:B].rearrange("p j c h s -> p (j c h s)")[:, n[l]:n[l + 1]]


def padded(VP, j, t, n):
    return VP[0:n, j, t].rearrange("p h e (u d) -> p h (e u) d", d=HD)[:, :, 0:4:3, :]


def V3(VP, j):
    return VP[0:SCP, j, 0].rearrange("p h e w -> p (h e w)")[:, 0:D]


LINKS = {}
PRE_DVE_VAR = 2 * B + 1
PRE_DVE_CTX = PRE_DVE_VAR + 4 + B


def build(nc, a, out):
    A = lambda l, n: a[f"L{l}_xcond_{n}"]
    with ExitStack() as ctx:
        def sb(name, shape, dt=F32):
            return ctx.enter_context(nc.sbuf_tensor(name, shape, dt))

        def sem(name):
            return ctx.enter_context(nc.semaphore(name))

        X = sb("X", [P, B, QT, D])
        w_even = sb("w_even", [P, W_EVEN])
        w_odd = sb("w_odd", [P, W_ODD])
        KM = sb("KM", [P, PAIR, CT, HPT, S])
        probs = sb("probs", [P, 4, 512])
        probsT = sb("probsT", [P, 4, 512])
        xh = sb("xh", [P, PAIR, QT, D])
        oT = xh
        hT = sb("hT", [P, PAIR, CT, S])
        qT = sb("qT", [P, PAIR, CT, S])
        kT = sb("kT", [P, PAIR, CT, S])
        VP = sb("VP", [P, PAIR, QT, HPT, 2, 32])
        gates = sb("gates", [P, PAIR, 3, D])
        brow = sb("brow", [P, 5, D])
        ctxT = sb("ctxT", [P, CT, B * SC])
        ctxnT = sb("ctxnT", [P, CT, B * SC])
        kcT = sb("kcT", [P, CT, B * SC])
        cs = sb("cs", [P, PAIR, CT, SCP])
        mods = sb("mods", [P, 3, 12, B])
        cols = sb("cols", [P, PAIR, 12])
        vec = sb("vec", [P, NROW])
        bq = sb("bq", [P, 2, 4])
        ident = sb("ident", [P, P])
        cosT = sb("cosT", [P, P])
        sinT = sb("sinT", [P, P])
        maskS = sb("maskS", [P, QT, S])
        maskC = sb("maskC", [P, B, SC])
        maskCj = sb("maskCj", [P, PAIR, SC])
        maskSw = sb("maskSw", [P, QT * S // 4], I32)
        maskCw = sb("maskCw", [P, B * SC // 4], I32)
        maskSb = maskSw[:, :].bitcast(U8).rearrange("p (t k) -> p t k", t=QT)
        maskCb = maskCw[:, :].bitcast(U8).rearrange("p (b k) -> p b k", b=B)
        cT = sb("cT", [P, CT, B])
        scT = sb("scT", [P, CT, B])
        crow = xh[0:B, 0, 0, :]
        srow = xh[0:B, 0, 1, :]
        nmax = sb("nmax", [P, 4, 4])
        top1 = sb("top1", [P, 4, 8])
        top2 = sb("top2", [P, 4, 8])
        left1 = maskS[:, :, :].rearrange("p t k -> p (t k)")[:, 0:4 * SC].rearrange("p (h k) -> p h k", h=4)
        left2 = maskC[:, :, :].rearrange("p (n h) k -> p n h k", n=2)
        rden = sb("rden", [P, CT * S])
        sums = sb("sums", [P, PAIR, QT, H])
        rsum = sb("rsum", [P, QT, H])
        stats = sb("stats", [P, PAIR, QT, 6])
        mv = sb("mv", [P, PAIR, QT, 2])
        ve = sb("ve", [P, PAIR, QT])
        rstd = sb("rstd", [P, PAIR, QT])
        mhalf = sb("mhalf", [P, 8])
        anchor = gates[:, 0, 1, 0:M3 * B].rearrange("p (m b) -> p m b", b=B)
        anc = sb("anc", [P, PAIR, M3])
        ranchor = sb("ranchor", [E_N, B + 1])
        ranc = sb("ranc", [E_N, PAIR])
        rb = sb("rb", [E_N, 1])
        logT = gates[0:E_N, :, 0, :]
        rp = sb("rp", [P, PAIR, QT, E_N])
        small = sb("small", [P, PAIR, QT, 2])
        stage = probs[:, :, :].rearrange("p a b -> p (a b)")
        scratch = nc.dram_tensor("gate_rows", [3, B, 3 * D], F32, kind="Internal").ap()

        bank = [ctx.enter_context(nc.psum_tensor(f"bank{n}", [P, 512], F32)) for n in range(8)]
        pj, ps, pt, po, pn = bank[0:2], bank[2:4], bank[4:6], bank[6], bank[7]

        s_in = sem("inputs_landed")
        s_ada = [sem(f"ada_landed{l}") for l in range(3)]
        s_w = [sem(f"weights_landed{l}") for l in range(4)]
        s_brow = sem("bias_rows_landed")
        s_const = sem("constants_made")
        s_mask = sem("masks_made")
        s_phase = sem("engine_done_with_layer")
        s_pre_full = sem("prelude_bank_full")
        s_pre_empty = sem("prelude_bank_emptied_by_scalar")
        s_rows = sem("modulation_rows_bank_emptied_by_vector")
        s_pre_dve = sem("prelude_vector_step")
        s_pre_act = sem("prelude_scalar_step")
        s_pre_pool = sem("prelude_pool_step")
        s_gates_out = sem("gate_rows_stored")
        s_out = sem("outputs_stored")
        s_held = [sem("tensor_held"), sem("vector_held")]
        vector_engine = [None]
        credited = []

        def mark(name, per):
            m = Mark(sem(name), tuple(per))
            credited.append(m)
            return m

        full = mark("projection_bank_full", [len(u) for u in USES])
        emptied = {"A": mark("bank_emptied_by_scalar", COUNT["A"]), "V": mark("bank_emptied_by_vector", COUNT["V"])}
        var_ready = mark("variance_ready", [2 * n for n in NLN])
        rstd_ready = mark("rstd_ready", [2 * n for n in NLN])
        xh_ready = mark("tokens_normalised", [2 * n for n in NLN])
        rope_ready = mark("rope_done", [4, 0, 0, 0])
        scored = mark("scores_ready", NG)
        maxed = mark("max_ready", NG)
        exped = mark("exp_ready", NG)
        chosen = mark("topk_applied", [0, NCROSS, 0, 0])
        turned = mark("probs_transposed", NG)
        copied = [mark(f"probsT_copied_{n}", [sum(by_vector(l, g) == (n == "vector") for g in range(NG[l])) for l in range(4)]) for n in ("scalar", "vector")]
        sums_turned = mark("denominators_transposed", [4, 4, 4, 0])
        sums_copied = mark("denominators_copied", [4, 4, 4, 0])
        spread = mark("denominators_spread", [4, 4, 4, 0])
        summed = mark("values_summed", NG)
        normed = mark("heads_normalised", [4, 4, 4, 0])
        added = mark("residual_added", [6, 6, 6, 2])
        picked = mark("batch_columns_copied", [2, 2, 2, 2])
        gates_in = [mark(f"gates_landed{j}", [16, 16, 16, 0]) for j in range(PAIR)]
        keys_in = [mark(f"masked_keys_landed{j}", [256, 256, 256, 0]) for j in range(PAIR)]
        act3 = mark("layer3_scalar_step", [0, 0, 0, 4])
        silu_done = mark("silu_ready", [0, PAIR * HT_N, 0, 0])
        dve3 = mark("layer3_vector_step", [0, 0, 0, 4])
        dve_own = mark("vector_own_step", DVE_LINKS)

        def region(buf, at, *shape):
            n = 1
            for s in shape:
                n *= s
            v = buf[:, at:at + n]
            if len(shape) == 2:
                v = v.rearrange("p (k n) -> p k n", n=shape[1])
            elif len(shape) == 3:
                v = v.rearrange("p (e k n) -> p e k n", k=shape[1], n=shape[2])
            return v

        def lay(buf, items):
            got, at = {}, 0
            for name, *shape in items:
                n = 1
                for s in shape:
                    n *= s
                got[name] = region(buf, at, *shape)
                at += n
            assert at <= buf.shape[1], (at, buf.shape)
            return got

        common = lambda kv, m1: [("qkv", CT, 3 * D), ("so", CT, D), ("cq", CT, D), *kv, ("co", CT, D), ("m1", CT, m1), ("m2", HT_N, D)]
        W = [lay(w_even, common([("ck", CT, D), ("cv", CT, D)], HID)),
             lay(w_odd, common([("ckv", CT, 2 * D)], 2 * HID)),
             lay(w_even, common([("ckv", CT, 2 * D)], HID)),
             lay(w_odd, [("e1", E_N, 4, RH), ("e2", E_N, 4, D), ("wq", CT, D), ("ck", CT, D), ("cv", CT, D), ("g1", 4, D), ("g2", CT, D)])]
        W3 = lay(w_even, [("out", CT, D), ("e1a", E_N, CT, RH), ("g1a", CT, D), ("r", 4, E_N), ("ra", CT, E_N)])
        ADA_N = (9 * D, 9 * D, 6 * D)
        WA = lay(w_odd, [("0", CT, ADA_N[0]), ("1", CT, ADA_N[1]), ("2", CT, ADA_N[2])])
        for l in (1, 2):
            W[l]["ck"], W[l]["cv"] = W[l]["ckv"][:, :, 0:D], W[l]["ckv"][:, :, D:2 * D]
        kp = lambda w: w.rearrange("(k p) n -> p k n", p=P)
        LOADS = [
            [("qkv", "qkv_W"), ("so", "attn_out_W"), ("cq", "cq_W"), ("ck", "ck_W"), ("cv", "cv_W"), ("co", "co_W"), ("m1", "mlp_W1"), ("m2", "mlp_W2")],
            [("qkv", "w_qkv"), ("so", "w_so"), ("cq", "w_q"), ("ckv", "w_kv"), ("co", "w_co"), ("m1", "w_m1"), ("m2", "w_m2")],
            [("qkv", "W_qkv"), ("so", "W_proj"), ("cq", "W_qc"), ("ckv", "W_kvc"), ("co", "W_cproj"), ("m1", "W_mlp1"), ("m2", "W_mlp2")],
        ]
        LOADED = [16 * len(x) for x in LOADS] + [16 * 18]
        BROWS = [["mlp_b2"], ["b_so", "b_co", "b_m2"], ["b_proj", "b_cproj", "b_mlp2"], ["e_b2", "gate_b2", "out_b"]]
        BROW_AT = [{2: 0}, {0: 0, 1: 1, 2: 2}, {0: 0, 1: 1, 2: 2}]
        BROW_N = [16 * len(x) for x in BROWS]
        VC = lambda l, name: ROW[f"L{l}_xcond_{name}"]
        BK = {1: VC(1, "b_qkv") + 2, 2: VC(2, "b_qkv") + 2}
        BV = {(1, 0): VC(1, "b_qkv") + 4, (2, 0): VC(2, "b_qkv") + 4, (1, 1): VC(1, "b_kv") + 2, (2, 1): VC(2, "b_kvc") + 2}
        BKC = {1: VC(1, "b_kv"), 2: VC(2, "b_kvc")}
        B1 = {0: VC(0, "mlp_b1"), 1: VC(1, "b_m1"), 2: VC(2, "b_mlp1")}
        MOD = {0: [(0, 1, 2), (3, 4, 5), (6, 7, 8)], 1: [(0, 1, 2), (3, 4, 5), (6, 7, 8)], 2: [(0, 1, 2), None, (3, 4, 5)]}

        def wait_full(eng, l, i, name, j):
            eng.wait_ge(full.sem, full.of(l, i, INDEX[l][name, j] + 1))

        def wait_taken(eng, l, i, name, j):
            k = INDEX[l][name, j]
            m = emptied[USES[l][k][2]]
            eng.wait_ge(m.sem, m.of(l, i, ORDER[l][k]))

        def wait_free(eng, l, i, name, j, *needs):
            k = INDEX[l][name, j]
            last = k - 2 if k >= 2 else max(x for x in range(len(USES[l])) if x % 2 == k % 2)
            owner = USES[l][last][2]
            least = {owner: ORDER[l][last] - (0 if k >= 2 else emptied[owner].per[l])}
            for n in needs:
                x = INDEX[l][n, j]
                owner = USES[l][x][2]
                least[owner] = max(ORDER[l][x], least.get(owner, ORDER[l][x]))
            for owner, k_ in least.items():
                eng.wait_ge(emptied[owner].sem, emptied[owner].of(l, i, k_))
            return pj[k % 2]

        def bank_of(l, name, j):
            return pj[INDEX[l][name, j] % 2]

        def wait_group(eng, m, l, i, n, start=0):
            if n >= start:
                eng.wait_ge(m.sem, m.of(l, i, n - start + 1))
            else:
                eng.wait_ge(m.sem, m.before(l, i, m.per[l] + n - start + 1))

        def wait_copied(eng, l, i, n):
            g = n % NG[l]
            m = copied[by_vector(l, g)]
            k = sum(by_vector(l, x) == by_vector(l, g) for x in range(g + 1))
            eng.wait_ge(m.sem, m.of(l, i, k) if n >= 0 else m.before(l, i, k))

        def hold(eng):
            eng.sem_inc(s_held[eng is vector_engine[0]], 1)

        def parts(l, n):
            cross = n >= NSELF[l]
            hg, kts = CROSS if cross else SELF[l]
            g, per = n - NSELF[l] * cross, H // hg
            return cross, g // (QT * per), g // per % QT, g % per * hg, hg, kts, SCP if cross else kts * P, SCP if cross else P

        def layer_done(eng, l):
            eng.drain().then_inc(s_phase, 1)
            eng.wait_ge(s_phase, 5 * (l + 1))

        def hidden(j, l):
            if l == 3:
                return KM[:, j].rearrange("p c h s -> p (c h) s")
            buf = probs if j == 0 else probsT
            return buf[:, :, :].rearrange("p a (b s) -> p (a b) s", s=S)

        block = ctx.enter_context(nc.Block())

        @block.sync
        def _(sp):
            sp.dma_start(crow, a["cond_1024"]).then_inc(s_in, 16)
            ctx_tok = stage[0:SC, 0:B * D].rearrange("p (b d) -> p b d", b=B)
            sp.dma_start(ctx_tok, a["ctx_1024"].rearrange("b s d -> s b d")).then_inc(s_in, 16)
            vst = hT[:, 0, 0, 0:P]
            for n, k in VECTORS:
                r = ROW[n]
                v = a[n]
                if len(v.shape) == 2:
                    v = v.rearrange("e n -> (e n)")
                sp.dma_start(vst[r:r + k, :], v.rearrange("(k p) -> k p", p=P)).then_inc(s_in, 16)
            for l, n in enumerate(("adaLN_b", "b_ada", "b_mod")):
                sp.dma_start(mod_rows(KM, l), A(l, n).rearrange("(o n) -> o n", o=1).to_broadcast([B, ADA_N[l]])).then_inc(s_in, 16)
            for l, n in enumerate(("adaLN_W", "w_ada", "W_mod")):
                sp.dma_start(WA[str(l)], kp(A(l, n))).then_inc(s_ada[l], 16)
                if l == 0:
                    sp.dma_start(X[:, :, :, :].rearrange("p b t d -> p (b t) d"), a["x"].rearrange("b (t p) d -> p (b t) d", p=P)).then_inc(s_in, 16)
                    sp.dma_start(maskSw[:, :].rearrange("p (t k) -> p t k", t=QT), a["mask_SxS_bk0"].rearrange("(t p k) -> p t k", p=P, t=QT)).then_inc(s_in, 16)
                    sp.dma_start(maskCw[:, :], a["mask_BxS2_bf1"].rearrange("(o k) -> o k", o=1).to_broadcast([P, B * SC // 4])).then_inc(s_in, 16)
                    sp.dma_start(cosT[:, :], a["rope_cos"]).then_inc(s_in, 16)
                    sp.dma_start(sinT[:, :], a["rope_sin"]).then_inc(s_in, 16)
                    sp.dma_start(rb[:, :], A(3, "router_b").rearrange("(e o) -> e o", o=1)).then_inc(s_in, 16)
            for name, src in LOADS[0]:
                sp.dma_start(W[0][name], kp(A(0, src))).then_inc(s_w[0], 16)
            for l in range(3):
                sp.wait_ge(s_rows, ROWS_IN[l])
                for n, m in enumerate(MOD[l]):
                    g = (m or MOD[l][0])[2]
                    sp.dma_start(scratch[l, :, n * D:(n + 1) * D], mod_rows(KM, l)[:, g * D:(g + 1) * D]).then_inc(s_gates_out, 16)
            sp.wait_ge(s_gates_out, 16 * 9)
            sp.drain().then_inc(s_phase, 1)
            sp.wait_ge(s_phase, 5)
            for l in range(4):
                r = 0
                for n in BROWS[l]:
                    v = A(l, n)
                    if n == "e_b2":
                        sp.dma_start(brow[:, 0:E_N, :], v.rearrange("(o e) n -> o e n", o=1).to_broadcast([P, E_N, D])).then_inc(s_brow, 16)
                        r += E_N
                    else:
                        sp.dma_start(brow[:, r, :], v.rearrange("(o n) -> o n", o=1).to_broadcast([P, D])).then_inc(s_brow, 16)
                        r += 1
                if l == 3:
                    for e in range(E_N):
                        sp.dma_start(W3["e1a"][:, e], A(3, "e_w1")[e, 4 * P:6 * P, :].rearrange("(k p) n -> p k n", p=P)).then_inc(s_w[3], 16)
                    sp.dma_start(W3["g1a"], kp(A(3, "gate_w1")[4 * P:6 * P, :])).then_inc(s_w[3], 16)
                    sp.dma_start(W3["r"], kp(A(3, "router_W")[0:4 * P, :])).then_inc(s_w[3], 16)
                    sp.dma_start(W3["ra"], kp(A(3, "router_W")[4 * P:6 * P, :])).then_inc(s_w[3], 16)
                    sp.dma_start(W3["out"], kp(A(3, "out_w"))).then_inc(s_w[3], 16)
                elif l == 2:
                    for n, src in (("ck", "Wk"), ("cv", "Wv"), ("wq", "Wq"), ("g2", "gate_w2")):
                        sp.dma_start(W[3][n], kp(A(3, src))).then_inc(s_w[3], 16)
                    sp.dma_start(W[3]["g1"], kp(A(3, "gate_w1")[0:4 * P, :])).then_inc(s_w[3], 16)
                    for e in range(E_N):
                        sp.dma_start(W[3]["e1"][:, e], kp(A(3, "e_w1")[e, 0:4 * P, :])).then_inc(s_w[3], 16)
                        sp.dma_start(W[3]["e2"][:, e], kp(A(3, "e_w2")[e])).then_inc(s_w[3], 16)
                else:
                    for name, src in LOADS[l + 1]:
                        sp.dma_start(W[l + 1][name], kp(A(l + 1, src))).then_inc(s_w[l + 1], 16)
                if l == 3:
                    with sp.Fori(0, TURNS) as i:
                        for j in range(PAIR):
                            sp.wait_ge(added.sem, added.of(3, i, j + 1))
                            sp.dma_start(out[bass.ds(i * PAIR + j, 1)].rearrange("o (t p) d -> p (o t) d", p=P),
                                         X[:, bass.ds(i * PAIR + j, 1)].rearrange("p o t d -> p (o t) d")).then_inc(s_out, 16)
                    sp.wait_ge(s_out, 16 * B)
                else:
                    sp.wait_ge(s_pre_empty, KEYS_IN[l])
                    with sp.Fori(0, TURNS) as i:
                        for j in range(PAIR):
                            sp.wait_ge(added.sem, added.before(l, i, 5 + j))
                            sp.dma_start(gates[:, j].rearrange("p g d -> p (g d)"),
                                         scratch[l, bass.ds(i * PAIR + j, 1), :].to_broadcast([P, 3 * D])).then_inc(gates_in[j].sem, 16)
                        for j in range(PAIR):
                            if l == 0:
                                sp.wait_ge(rope_ready.sem, rope_ready.of(l, i, 2 * j + 1))
                            else:
                                wait_taken(sp, l, i, "K", j)
                            for h in range(HPT):
                                sp.dma_start(KM[HD * h:HD * (h + 1), j, :, h, :], kT[HD * h:HD * (h + 1), j, :, :]).then_inc(keys_in[j].sem, 16)
                        for j in range(PAIR):
                            wait_group(sp, scored, l, i, (j + 1) * NSELF[l] // 2 - 1)
                            for h in range(HPT):
                                sp.dma_start(KM[HD * h:HD * (h + 1), j, :, h, 0:SC],
                                             kcT[HD * h:HD * (h + 1), :, bass.ds((i * PAIR + j) * SC, SC)]).then_inc(keys_in[j].sem, 16)
                if l < 3:
                    layer_done(sp, l + 1)

        @block.gpsimd
        def _(pool):
            for m in credited:
                pool.sem_inc(m.sem, m.credit)
            nc.gpsimd.memset(ident[:, :], 0.0).then_inc(s_pre_pool, 1)
            pool.wait_ge(s_pre_pool, 1)
            nc.gpsimd.affine_select(out=ident[:, :], in_=ident[:, :], compare_op=ALU.not_equal, fill=1.0,
                                    base=0, pattern=[[-1, P]], channel_multiplier=1).then_inc(s_const, 1)
            nc.gpsimd.memset(mods[:, :, :, :].rearrange("p l c b -> p (l c b)"), 0.0).then_inc(s_const, 1)
            nc.gpsimd.memset(cs[:, :, :, :].rearrange("p j c k -> p (j c k)"), 0.0).then_inc(s_pre_pool, 1)
            nc.gpsimd.memset(mhalf[:, :], -0.5).then_inc(s_pre_pool, 1)
            nc.gpsimd.memset(VP[:, :].rearrange("p j t h e w -> p (j t h e w)"), 0.0).then_inc(s_const, 1)
            pool.wait_ge(s_pre_pool, 3)
            pool.wait_ge(s_pre_dve, PRE_DVE_VAR)
            nc.gpsimd.tensor_tensor(rden[0:SC, 16:24], rden[0:SC, 8:16], mhalf[0:SC, :], ALU.pow).then_inc(s_pre_pool, 1)
            pool.wait_ge(s_pre_full, PRE_MODS)
            pool.wait_ge(s_gates_out, 16 * 9)
            for j in range(PAIR):
                nc.gpsimd.memset(KM[:, j].rearrange("p c h s -> p (c h s)"), 0.0).then_inc(s_const, 1)
            pool.drain().then_inc(s_phase, 1)
            pool.wait_ge(s_phase, 5)
            def inverse(l, i, k):
                pool.wait_ge(var_ready.sem, var_ready.of(l, i, k + 1))
                nc.gpsimd.tensor_tensor(rstd[:, k % 2, :], ve[:, k % 2, :], mhalf[:, 0:QT], ALU.pow).then_inc(rstd_ready.sem, 1)

            def pick(l, i, j):
                b = i * PAIR + j
                if l < 3:
                    last = emptied["A"]
                    k = INDEX[l]["T2", j]
                    pool.wait_ge(last.sem, last.before(l, i, ORDER[l][k]))
                    if l == 0:
                        nc.gpsimd.tensor_copy(maskCj[:, j, :], maskC[:, bass.ds(b, 1), :].rearrange("p o k -> p (o k)"))
                    nc.gpsimd.tensor_copy(cols[:, j, :], mods[:, l, :, bass.ds(b, 1)].rearrange("p c o -> p (c o)"))
                else:
                    pool.wait_ge(added.sem, added.before(l, i, j + 1))
                    nc.gpsimd.tensor_copy(anc[:, j, :], anchor[:, :, bass.ds(b, 1)].rearrange("p c o -> p (c o)"))
                    nc.gpsimd.tensor_copy(ranc[:, j:j + 1], ranchor[:, bass.ds(b, 1)])
                    nc.gpsimd.tensor_copy(kT[:, j, :, 0:SC], kcT[:, :, bass.ds(b * SC, SC)])
                src = ctxnT if l == 2 else ctxT
                nc.gpsimd.tensor_copy(cs[:, j, :, 0:SC], src[:, :, bass.ds(b * SC, SC)]).then_inc(picked.sem, 1)

            def turn(l, i, more):
                for j in range(PAIR):
                    pick(l, i, j)
                for k in range(2, 2 * NLN[l]):
                    inverse(l, i, k)
                if more:
                    for k in range(PAIR):
                        inverse(l, i + 1, k)

            for l in range(4):
                for k in range(PAIR):
                    inverse(l, 0, k)
                pool.wait_ge(s_pre_empty, KEYS_IN[l] + (l == 3))
                if l == 3:
                    pool.wait_ge(s_mask, 1)
                with pool.Fori(0, TURNS - 1) as i:
                    turn(l, i, True)
                turn(l, TURNS - 1, False)
                if l < 3:
                    layer_done(pool, l + 1)

        @block.tensor
        def _(pe):
            uses = [0]

            def pre_bank():
                u = uses[0]
                uses[0] += 1
                if 1 <= u - 2 <= ROWS_IN[2]:
                    pe.wait_ge(s_rows, u - 2)
                elif u >= 2:
                    pe.wait_ge(s_pre_empty, max(1, u - 1 - ROWS_IN[2]))
                return pj[u % 2]

            def mm(dst, pairs):
                for n, (x, y) in enumerate(pairs):
                    last = nc.tensor.matmul(dst, x, y, start=(n == 0), stop=(n == len(pairs) - 1))
                return last

            pe.wait_ge(s_in, 16 * PRE_LOADS)
            pe.wait_ge(s_const, 2)
            b_ = pre_bank()
            for c in range(CT):
                nc.tensor.transpose(b_[:, c * B:(c + 1) * B], crow[:, c * P:(c + 1) * P], ident[0:B, 0:B])
            pe.wait_ge(s_pre_act, 1)
            for c in range(CT):
                nc.tensor.transpose(b_[:, (2 + c) * B:(3 + c) * B], srow[:, c * P:(c + 1) * P], ident[0:B, 0:B])
            nc.tensor.transpose(b_[:, P:P + NROW], hT[0:NROW, 0, 0, 0:P], ident[0:NROW, 0:NROW]).then_inc(s_pre_full, 1)
            pe.wait_ge(s_pre_empty, 1)
            for l in range(3):
                pe.wait_ge(s_ada[l], 16)
                cc = cT if l == 0 else scT
                for n in range(0, ADA_N[l], 512):
                    w = min(512, ADA_N[l] - n)
                    b_ = pre_bank()
                    mm(b_[0:B, 0:w], [(cc[:, k, :], WA[str(l)][:, k, n:n + w]) for k in range(CT)]).then_inc(s_pre_full, 1)
            for l in range(3):
                pe.wait_ge(s_rows, ROWS_IN[l])
                b_ = pre_bank()
                rows = mod_rows(KM, l)
                at = 0
                for m in MOD[l]:
                    if m is None:
                        continue
                    for chunk in m[0:2]:
                        for c in range(CT):
                            last = nc.tensor.transpose(b_[:, at:at + B], rows[:, chunk * D + c * P:chunk * D + (c + 1) * P], ident[0:B, 0:B])
                            at += B
                last.then_inc(s_pre_full, 1)
            for norm in range(2):
                ctx_tok = stage[0:SC, 0:B * D].rearrange("p (b d) -> p b d", b=B)
                if norm:
                    pe.wait_ge(s_pre_dve, PRE_DVE_CTX)
                for b0 in range(0, B, 3):
                    b_ = pre_bank()
                    for b in range(b0, min(b0 + 3, B)):
                        for c in range(CT):
                            at = (c * 3 + b - b0) * SC
                            last = nc.tensor.transpose(b_[:, at:at + SC], ctx_tok[:, b, c * P:(c + 1) * P], ident[0:SC, 0:SC])
                    last.then_inc(s_pre_full, 1)
            pe.drain().then_inc(s_phase, 1)
            pe.wait_ge(s_phase, 5)

            def context_keys(l):
                src = ctxnT if l == 2 else ctxT
                for c in range(CT):
                    for n in range(0, B * SC, 512):
                        w = min(512, B * SC - n)
                        b_ = pre_bank()
                        mm(b_[:, 0:w], [(W[l]["ck"][:, k, c * P:(c + 1) * P], src[:, k, n:n + w]) for k in range(CT)]).then_inc(s_pre_full, 1)

            def to_channels(l, i, j, n):
                pe.wait_ge(xh_ready.sem, xh_ready.of(l, i, 2 * n + j + 1))
                b_ = wait_free(pe, l, i, f"T{n}", j)
                for t in range(QT):
                    for c in range(CT):
                        last = nc.tensor.transpose(b_[:, c * S + t * P:c * S + (t + 1) * P], xh[:, j, t, c * P:(c + 1) * P], ident[:, :])
                last.then_inc(full.sem, 1)

            def channels_out(l, i, name, j, w, at, rhs, *needs, ks=CT):
                b_ = wait_free(pe, l, i, name, j, *needs)
                for c in range(2):
                    last = mm(b_[:, c * S:(c + 1) * S], [(w[:, k, at + c * P:at + (c + 1) * P], rhs(k)) for k in range(ks)])
                last.then_inc(full.sem, 1)

            def tokens_out(l, i, name, j, w, at, lhs, *needs, ks=CT, late=None):
                b_ = wait_free(pe, l, i, name, j, *needs)
                for t in range(QT):
                    for k in range(ks):
                        if late and t == 0 and k == ks - 2:
                            wait_taken(pe, l, i, late, j)
                        last = nc.tensor.matmul(b_[:, t * D:(t + 1) * D], lhs(k)[:, t * P:(t + 1) * P], w[:, k, at:at + D], start=(k == 0), stop=(k == ks - 1))
                last.then_inc(full.sem, 1)

            def use(l, i, name, j):
                w = W[l]
                x = lambda k: hT[:, j, k, :]
                o = lambda k: oT[:, j, k, :]
                if name == "VC":
                    pe.wait_ge(picked.sem, picked.of(l, i, j + 1))
                    b_ = wait_free(pe, l, i, "VC", j)
                    mm(b_[0:SCP, 0:D], [(cs[:, j, k, :], w["cv"][:, k, :]) for k in range(CT)]).then_inc(full.sem, 1)
                elif name in ("O", "OC"):
                    cross = name == "OC"
                    pe.wait_ge(normed.sem, normed.of(l, i, 2 * cross + j + 1))
                    tokens_out(l, i, name, j, w["co" if cross else "so"], 0, o)
                elif name in ("T1", "T2"):
                    to_channels(l, i, j, int(name[1]))
                elif name == "QC":
                    channels_out(l, i, "QC", j, w["cq"], 0, x, "T1")
                elif name == "MO":
                    hid = hidden(j, l)
                    last = HT_N - 1 if l == 1 else HT_N // 2 - 1
                    tokens_out(l, i, "MO", j, w["m2"], 0, lambda k: hid[:, k, :], f"M{last - (2 if l == 1 else 1)}", ks=HT_N, late=f"M{last}")
                elif l == 1:
                    m = int(name[1:])
                    b_ = wait_free(pe, l, i, name, j, "T2")
                    for half in range(2):
                        at = half * HID + m * P
                        last = mm(b_[:, half * S:(half + 1) * S], [(w["m1"][:, k, at:at + P], x(k)) for k in range(CT)])
                    last.then_inc(full.sem, 1)
                else:
                    channels_out(l, i, name, j, w["m1"], 2 * int(name[1:]) * P, x, "T2")

            def attentions(l, i):
                e = ends(l)
                for step in range(NG[l] + SUM_LAG):
                    if step < NG[l]:
                        n = step
                        cross, j, qt, h0, hg, kts, width, kp_ = parts(l, n)
                        if n in (0, *e):
                            if l == 0 and not cross:
                                pe.wait_ge(rope_ready.sem, rope_ready.of(l, i, 2 * j + 2))
                            else:
                                wait_taken(pe, l, i, "QC" if cross else "Q", j)
                            pe.wait_ge(keys_in[j].sem, keys_in[j].of(l, i, 256 if cross else 128))
                        wait_group(pe, exped, l, i, n - 2)
                        for x in range(hg):
                            h = h0 + x
                            keys = KM[:, j, h // HPT, h % HPT, 0:SCP] if cross else (
                                KM[:, j, h // HPT, h % HPT, qt * P:(qt + 1) * P] if kts == 1 else KM[:, j, h // HPT, h % HPT, :])
                            last = nc.tensor.matmul(ps[n % 2][:, x * width:(x + 1) * width], qT[:, j, h // HPT, qt * P:(qt + 1) * P], keys, start=True, stop=True)
                        last.then_inc(scored.sem, 1)
                    if 0 <= step - 2 < NG[l]:
                        n = step - 2
                        cross, j, qt, h0, hg, kts, width, kp_ = parts(l, n)
                        if l == 1 and cross:
                            pe.wait_ge(chosen.sem, chosen.of(l, i, n - NSELF[l] + 1))
                        else:
                            wait_group(pe, exped, l, i, n)
                        wait_copied(pe, l, i, n - 2)
                        for x in range(hg):
                            for k in range(kts):
                                at = (x * kts + k) * P
                                keys_ = SC if cross else P
                                last = nc.tensor.transpose(pt[n % 2][0:keys_, at:at + P], probs[:, n % 4, x * width + k * P:x * width + k * P + keys_], ident[:, :])
                        last.then_inc(turned.sem, 1)
                    if step - 2 in e:
                        k = e.index(step - 2)
                        pe.wait_ge(spread.sem, spread.of(l, i, k + 1))
                        for t in range(QT):
                            for c in range(CT):
                                last = nc.tensor.transpose(pn[:, c * S + t * P:c * S + (t + 1) * P], rden[:, t * D + c * P:t * D + (c + 1) * P], ident[:, :])
                        last.then_inc(sums_turned.sem, 1)
                    if 0 <= step - SUM_LAG < NG[l]:
                        n = step - SUM_LAG
                        cross, j, qt, h0, hg, kts, width, kp_ = parts(l, n)
                        if n in (0, *e):
                            k = 2 * cross + j
                            if k:
                                pe.wait_ge(normed.sem, normed.of(l, i, k))
                            else:
                                pe.wait_ge(normed.sem, normed.before(l, i, 4))
                            wait_taken(pe, l, i, "VC" if cross else "V0", j)
                        wait_copied(pe, l, i, n)
                        for x in range(0, hg, 2):
                            h = h0 + x
                            quad, c = h % HPT // 2, h // HPT
                            at = slice(c * S + qt * P, c * S + (qt + 1) * P)
                            for u in range(2):
                                for k in range(kts):
                                    kt = qt if (kts == 1 and not cross) else k
                                    col = ((x + u) * kts + k) * P
                                    last = nc.tensor.matmul(po[32 * quad:32 * quad + 32, at], VP[0:kp_, j, kt, h // 2, u, :], probsT[0:kp_, n % 4, col:col + P],
                                                            start=(u == 0 and k == 0), stop=(u == 1 and k == kts - 1))
                        last.then_inc(summed.sem, 1)
                    for name, j in between(l).get(step, ()):
                        use(l, i, name, j)

            for l in range(3):
                w = W[l]
                pe.wait_ge(s_w[l], LOADED[l])
                context_keys(l)
                pe.wait_ge(s_pre_empty, KEYS_IN[l])
                with pe.Fori(0, TURNS) as i:
                    for j in range(PAIR):
                        to_channels(l, i, j, 0)
                    for j in range(PAIR):
                        x = lambda k: hT[:, j, k, :]
                        channels_out(l, i, "K", j, w["qkv"], D, x, "T0")
                        channels_out(l, i, "Q", j, w["qkv"], 0, x)
                        tokens_out(l, i, "V0", j, w["qkv"], 2 * D, x)
                    attentions(l, i)
                    for name, j in tail(l):
                        use(l, i, name, j)
                layer_done(pe, l + 1)

            l, w = 3, W[3]
            pe.wait_ge(s_w[3], LOADED[3])
            context_keys(3)
            b_ = pre_bank()
            for m in range(M3):
                for k in range(CT):
                    lhs = W3["e1a"][:, m // 4, k, m % 4 * P:(m % 4 + 1) * P] if m < 4 * E_N else W3["g1a"][:, k, (m - 4 * E_N) * P:(m - 4 * E_N + 1) * P]
                    last = nc.tensor.matmul(b_[:, m * B:(m + 1) * B], lhs, cT[:, k, :], start=(k == 0), stop=(k == CT - 1))
            mm(b_[0:E_N, M3 * B:(M3 + 1) * B], [(W3["ra"][:, k, :], cT[:, k, :]) for k in range(CT)]).then_inc(s_pre_full, 1)
            pe.wait_ge(s_pre_empty, KEYS_IN[3] + 1)
            with pe.Fori(0, TURNS) as i:
                for j in range(PAIR):
                    to_channels(l, i, j, 0)
                    pe.wait_ge(picked.sem, picked.of(l, i, j + 1))
                    b_ = wait_free(pe, l, i, "VC", j)
                    mm(b_[0:SCP, 0:D], [(cs[:, j, k, :], w["cv"][:, k, :]) for k in range(CT)]).then_inc(full.sem, 1)
                for j in range(PAIR):
                    channels_out(l, i, "Q", j, w["wq"], 0, lambda k: hT[:, j, k, :], "T0")
                for j in range(PAIR):
                    b_ = wait_free(pe, l, i, "S", j, "Q")
                    for t in range(QT):
                        last = mm(b_[:, t * SC:(t + 1) * SC], [(qT[:, j, k, t * P:(t + 1) * P], kT[:, j, k, 0:SC]) for k in range(CT)])
                    last.then_inc(full.sem, 1)
                for j in range(PAIR):
                    pe.wait_ge(dve3.sem, dve3.of(l, i, 3 + j))
                    b_ = wait_free(pe, l, i, "PT", j)
                    for t in range(QT):
                        last = nc.tensor.transpose(b_[0:SC, t * P:(t + 1) * P], probs[:, j, t * SC:(t + 1) * SC], ident[:, :])
                    last.then_inc(full.sem, 1)
                for j in range(PAIR):
                    b_ = wait_free(pe, l, i, "EV", j, "PT", "VC")
                    for c in range(CT):
                        last = nc.tensor.matmul(b_[:, c * S:(c + 1) * S], V3(VP, j)[:, c * P:(c + 1) * P], probsT[0:SCP, j, 0:S], start=True, stop=True)
                    last.then_inc(full.sem, 1)
                comb = lambda j: (lambda k: hT[:, j, k, :] if k < CT else qT[:, j, k - CT, :])
                for j in range(PAIR):
                    b_ = wait_free(pe, l, i, "RL", j, "EV")
                    mm(b_[0:E_N, 0:S], [(W3["r"][:, k, :], comb(j)(k)) for k in range(4)]).then_inc(full.sem, 1)
                for j in range(PAIR):
                    b_ = wait_free(pe, l, i, "RT", j, "RL")
                    hold(pe)
                    for t in range(QT):
                        last = nc.tensor.transpose(b_[:, t * E_N:(t + 1) * E_N], logT[:, j, t * P:(t + 1) * P], ident[0:E_N, 0:E_N])
                    last.then_inc(full.sem, 1)
                for j in range(PAIR):
                    for m in range(M3 // 2):
                        ws, at = (w["e1"][:, m // 2], m % 2 * 2 * P) if m < 2 * E_N else (w["g1"], 0)
                        channels_out(l, i, f"M{m}", j, ws, at, comb(j), ks=4)
                for j in range(PAIR):
                    hid = hidden(j, l)
                    for e in range(E_N):
                        tokens_out(l, i, f"E{e}", j, w["e2"][:, e], 0, lambda k: hid[:, 4 * e + k, :], f"M{M3 // 2 - 1}", ks=4)
                for j in range(PAIR):
                    hid = hidden(j, l)
                    tokens_out(l, i, "GO", j, w["g2"], 0, lambda k: hid[:, 4 * E_N + k, :])
                for j in range(PAIR):
                    b_ = wait_free(pe, l, i, "RR", j, f"E{E_N - 1}")
                    for t in range(QT):
                        for c in range(CT):
                            last = nc.tensor.transpose(b_[:, c * S + t * P:c * S + (t + 1) * P], xh[:, j, t, c * P:(c + 1) * P], ident[:, :])
                    last.then_inc(full.sem, 1)
                for j in range(PAIR):
                    tokens_out(l, i, "OUT", j, W3["out"], 0, lambda k: hT[:, j, k, :], "RR")

        @block.scalar
        def _(act):
            uses = [0]

            def pre_bank():
                u = uses[0]
                uses[0] += 1
                act.wait_ge(s_pre_full, u + 1)
                return pj[u % 2]

            ident_ = lambda o, x, **kw: nc.scalar.activation(o, x, ACT.Identity, **kw)
            copy_ = lambda o, x: nc.scalar.activation(o, x, ACT.Copy)
            act.wait_ge(s_in, 16 * PRE_LOADS)
            nc.scalar.activation(srow, crow, ACT.Silu).then_inc(s_pre_act, 1)
            b_ = pre_bank()
            copy_(cT[:, :, :].rearrange("p c b -> p (c b)"), b_[:, 0:CT * B])
            copy_(scT[:, :, :].rearrange("p c b -> p (c b)"), b_[:, CT * B:2 * CT * B])
            for n, c in enumerate((VC(1, "b_qkv"), VC(1, "b_q"), VC(2, "b_qkv"), VC(2, "b_qc"))):
                nc.scalar.activation(bq[:, n // 2, n % 2 * 2:n % 2 * 2 + 2], b_[:, P + c:P + c + 2], ACT.Copy, scale=SCALE)
            copy_(vec[:, :], b_[:, P:P + NROW]).then_inc(s_pre_empty, 1)
            uses[0] += sum(NPRE)
            for l in range(3):
                b_ = pre_bank()
                at = 0
                for n, m in enumerate(MOD[l]):
                    if m is None:
                        continue
                    for what in range(2):
                        o = mods[:, l, 4 * n + 2 * what:4 * n + 2 * what + 2, :]
                        src = b_[:, at:at + CT * B].rearrange("p (c b) -> p c b", c=CT)
                        if what == 0:
                            last = copy_(o, src)
                        elif l > 0:
                            last = ident_(o, src, bias=1.0)
                        else:
                            for c in range(CT):
                                wc = vec[:, 2 * n + c:2 * n + c + 1]
                                last = ident_(o[:, c, :], src[:, c, :], bias=wc, scale=wc)
                        at += CT * B
                last.then_inc(s_pre_empty, 1)
            for dst in (ctxT, ctxnT):
                for b0 in range(0, B, 3):
                    nb = min(3, B - b0)
                    b_ = pre_bank()
                    for c in range(CT):
                        last = copy_(dst[:, c, b0 * SC:(b0 + nb) * SC], b_[:, c * 3 * SC:(c * 3 + nb) * SC])
                    last.then_inc(s_pre_empty, 1)
            act.drain().then_inc(s_phase, 1)
            act.wait_ge(s_phase, 5)

            def context_keys(l):
                for c in range(CT):
                    for n in range(0, B * SC, 512):
                        w = min(512, B * SC - n)
                        b_ = pre_bank()
                        o = kcT[:, c, n:n + w]
                        if l in BKC:
                            last = ident_(o, b_[:, 0:w], bias=vec[:, BKC[l] + c:BKC[l] + c + 1])
                        else:
                            last = copy_(o, b_[:, 0:w])
                        last.then_inc(s_pre_empty, 1)

            def channels(l, i, j, n):
                wait_full(act, l, i, f"T{n}", j)
                b_ = bank_of(l, f"T{n}", j)
                for c in range(CT):
                    if l == 3:
                        sc, bi = vec[:, VC(3, "ln_gamma") + c:][:, 0:1], vec[:, VC(3, "ln_beta") + c:][:, 0:1]
                    else:
                        sc, bi = cols[:, j, 4 * n + 2 + c:4 * n + 3 + c], cols[:, j, 4 * n + c:4 * n + c + 1]
                    if l == 2 and n == 1:
                        last = copy_(hT[:, j, c, :], b_[:, c * S:(c + 1) * S])
                    elif l == 1 and n == 0:
                        ident_(hT[:, j, c, 0:S - SHIFT], b_[:, c * S + SHIFT:(c + 1) * S], bias=bi, scale=sc)
                        last = ident_(hT[:, j, c, S - SHIFT:S], b_[:, c * S:c * S + SHIFT], bias=bi, scale=sc)
                    else:
                        last = ident_(hT[:, j, c, :], b_[:, c * S:(c + 1) * S], bias=bi, scale=sc)
                last.then_inc(emptied["A"].sem, 1)

            def queries(l, i, j, cross):
                name = "QC" if cross else "Q"
                wait_full(act, l, i, name, j)
                b_ = bank_of(l, name, j)
                scale = SCALE3 if l == 3 else SCALE
                if l in (1, 2):
                    for c in range(CT):
                        bias = bq[:, l - 1, 2 * cross + c:2 * cross + c + 1]
                        last = ident_(qT[:, j, c, :], b_[:, c * S:(c + 1) * S], bias=bias, scale=scale)
                else:
                    last = nc.scalar.activation(qT[:, j].rearrange("p c s -> p (c s)"), b_[:, :], ACT.Copy, scale=scale)
                last.then_inc(emptied["A"].sem, 1)

            def use(l, i, name, j):
                if name == "VC":
                    values(l, i, j)
                elif name in ("T1", "T2"):
                    channels(l, i, j, int(name[1]))
                elif name == "QC":
                    queries(l, i, j, 1)
                elif name[0] == "M" and name != "MO":
                    hid, m = hidden(j, l), int(name[1:])
                    wait_full(act, l, i, name, j)
                    b_ = bank_of(l, name, j)
                    if l == 1:
                        nc.scalar.activation(hid[:, m, :], b_[:, 0:S], ACT.Silu, bias=vec[:, B1[l] + m:B1[l] + m + 1]).then_inc(silu_done.sem, 1)
                    else:
                        for x in range(2):
                            k = 2 * m + x
                            last = nc.scalar.activation(hid[:, k, :], b_[:, x * S:(x + 1) * S], ACT.Gelu_apprx_tanh, bias=vec[:, B1[l] + k:B1[l] + k + 1])
                        last.then_inc(emptied["A"].sem, 1)

            def attentions(l, i):
                e = ends(l)
                for step in range(NG[l] + SUM_LAG):
                    if 0 <= step - 2 < NG[l] and not by_vector(l, step - 2):
                        n = step - 2
                        kp_ = parts(l, n)[-1]
                        wait_group(act, turned, l, i, n)
                        wait_group(act, summed, l, i, n - 4)
                        copy_(probsT[0:kp_, n % 4, :], pt[n % 2][0:kp_, :]).then_inc(copied[0].sem, 1)
                    if step < NG[l]:
                        n = step
                        cross, j, qt, h0, hg, kts, width, kp_ = parts(l, n)
                        wait_group(act, maxed, l, i, n)
                        wait_group(act, turned, l, i, n - 4)
                        keys_ = SC if cross else width
                        for x in range(hg):
                            acc = {} if l == 1 and cross else {"accum_out": sums[:, j, qt, h0 + x:h0 + x + 1]}
                            last = nc.scalar.activation(probs[:, n % 4, x * width:x * width + keys_], ps[n % 2][:, x * width:x * width + keys_],
                                                        ACT.Exp, bias=nmax[:, n % 4, x:x + 1], **acc)
                        last.then_inc(exped.sem, 1)
                    if step - 2 in e:
                        k = e.index(step - 2) + 1
                        act.wait_ge(sums_turned.sem, sums_turned.of(l, i, k))
                        copy_(rden[:, :], pn[:, :]).then_inc(sums_copied.sem, 1)
                    for name, j in between(l).get(step, ()):
                        use(l, i, name, j)

            def values(l, i, j):
                wait_full(act, l, i, "VC", j)
                b_ = bank_of(l, "VC", j)
                if l == 3:
                    last = copy_(V3(VP, j), b_[0:SCP, 0:D])
                else:
                    last = copy_(padded(VP, j, 0, SCP), b_[0:SCP, 0:D].rearrange("p (h e d) -> p h e d", e=2, d=HD))
                last.then_inc(emptied["A"].sem, 1)

            for l in range(3):
                context_keys(l)
                with act.Fori(0, TURNS) as i:
                    for j in range(PAIR):
                        act.wait_ge(picked.sem, picked.of(l, i, j + 1))
                        channels(l, i, j, 0)
                    for j in range(PAIR):
                        if l == 0:
                            wait_full(act, l, i, "K", j)
                            act.wait_ge(added.sem, added.before(l, i, 5 + j))
                            copy_(kT[:, j].rearrange("p c s -> p (c s)"), bank_of(l, "K", j)[:, :]).then_inc(emptied["A"].sem, 1)
                        queries(l, i, j, 0)
                    attentions(l, i)
                    for name, j in tail(l):
                        use(l, i, name, j)
                layer_done(act, l + 1)

            l = 3
            context_keys(3)
            b_ = pre_bank()
            copy_(anchor[:, :, :].rearrange("p m b -> p (m b)"), b_[:, 0:M3 * B])
            nc.scalar.activation(ranchor[:, 0:B], b_[0:E_N, M3 * B:(M3 + 1) * B], ACT.Identity, bias=rb[:, 0:1]).then_inc(s_pre_empty, 1)
            with act.Fori(0, TURNS) as i:
                for j in range(PAIR):
                    channels(l, i, j, 0)
                    values(l, i, j)
                for j in range(PAIR):
                    queries(l, i, j, 0)
                for j in range(PAIR):
                    act.wait_ge(dve3.sem, dve3.of(l, i, 1 + j))
                    b_ = bank_of(l, "S", j)
                    for t in range(QT):
                        last = nc.scalar.activation(probs[:, j, t * SC:(t + 1) * SC], b_[:, t * SC:(t + 1) * SC], ACT.Exp,
                                                    bias=nmax[:, j, t:t + 1], accum_out=small[:, j, t, 0:1])
                    last.then_inc(emptied["A"].sem, 1)
                for j in range(PAIR):
                    wait_full(act, l, i, "PT", j)
                    copy_(probsT[0:SCP, j, 0:S], bank_of(l, "PT", j)[0:SCP, 0:S]).then_inc(emptied["A"].sem, 1)
                for j in range(PAIR):
                    wait_full(act, l, i, "EV", j)
                    copy_(qT[:, j].rearrange("p c s -> p (c s)"), bank_of(l, "EV", j)[:, :]).then_inc(emptied["A"].sem, 1)
                for j in range(PAIR):
                    act.wait_ge(picked.sem, picked.of(l, i, j + 1))
                    wait_full(act, l, i, "RL", j)
                    ident_(logT[:, j, :], bank_of(l, "RL", j)[0:E_N, 0:S], bias=ranc[:, j:j + 1]).then_inc(emptied["A"].sem, 1)
                for j in range(PAIR):
                    wait_taken(act, l, i, "RT", j)
                    for t in range(QT):
                        last = nc.scalar.activation(rp[:, j, t, :], rp[:, j, t, :], ACT.Exp, accum_out=small[:, j, t, 1:2])
                    last.then_inc(act3.sem, 1)
                for j in range(PAIR):
                    hid = hidden(j, l)
                    for m in range(M3 // 2):
                        wait_full(act, l, i, f"M{m}", j)
                        b_ = bank_of(l, f"M{m}", j)
                        for x in range(2):
                            k = 2 * m + x
                            last = nc.scalar.activation(hid[:, k, :], b_[:, x * S:(x + 1) * S], ACT.Silu, bias=anc[:, j, k:k + 1])
                        last.then_inc(emptied["A"].sem, 1)
                for j in range(PAIR):
                    wait_taken(act, l, i, "GO", j)
                    g = kT[:, j].rearrange("p c s -> p (c s)")
                    nc.scalar.activation(g, g, ACT.Tanh, scale=0.5).then_inc(act3.sem, 1)
                for j in range(PAIR):
                    wait_full(act, l, i, "RR", j)
                    copy_(hT[:, j].rearrange("p c s -> p (c s)"), bank_of(l, "RR", j)[:, :]).then_inc(emptied["A"].sem, 1)

        @block.vector
        def _(dve):
            vector_engine[0] = dve
            links = [0]
            where = [None, None]

            def link(ins):
                links[0] += 1
                ins.then_inc(dve_own.sem, 1)

            def settle():
                l, i = where
                dve.wait_ge(dve_own.sem, dve_own.of(l, i, links[0]))

            uses = [1]
            pre = [0]

            def pre_link(ins, wait=True):
                pre[0] += 1
                ins.then_inc(s_pre_dve, 1)
                if wait:
                    dve.wait_ge(s_pre_dve, pre[0])

            dve.wait_ge(s_in, 16 * PRE_LOADS)
            ctx_tok = stage[0:SC, 0:B * D].rearrange("p (b d) -> p b d", b=B)
            st = rden[0:SC, 32:32 + 6 * B].rearrange("p (b s) -> p b s", b=B)
            mvc = rden[0:SC, 128:128 + 2 * B].rearrange("p (b s) -> p b s", b=B)
            for b in range(B):
                pre_link(nc.vector.bn_stats(st[:, b, :], ctx_tok[:, b, :]), b == B - 1)
            for b in range(B):
                pre_link(nc.vector.bn_aggr(mvc[:, b, :], st[:, b, :]), b == B - 1)
            pre_link(nc.vector.tensor_scalar(rden[0:SC, 8:16], mvc[:, :, 1], EPS[2], None, ALU.add))
            assert pre[0] == PRE_DVE_VAR, pre[0]
            for m, mb in ((maskS, maskSb), (maskC, maskCb)):
                pre_link(nc.vector.tensor_copy(m[:, :, :], mb[:, :, :]))
                pre_link(nc.vector.tensor_scalar(m[:, :, :], m[:, :, :], 1.0, -NEG, ALU.subtract, ALU.mult))
            for l in range(3):
                for n in range(0, ADA_N[l], 512):
                    w = min(512, ADA_N[l] - n)
                    dve.wait_ge(s_pre_full, uses[0] + 1)
                    b_ = pj[uses[0] % 2]
                    uses[0] += 1
                    r = mod_rows(KM, l)[:, n:n + w]
                    nc.vector.tensor_tensor(r, b_[0:B, 0:w], r, ALU.add).then_inc(s_rows, 1)
            dve.wait_ge(s_pre_full, PRE_RAW)
            dve.wait_ge(s_pre_pool, 4)
            for b in range(B):
                pre_link(nc.vector.tensor_scalar(ctx_tok[:, b, :], ctx_tok[:, b, :], mvc[:, b, 0:1], rden[0:SC, 16 + b:17 + b], ALU.subtract, ALU.mult), False)
            assert pre[0] == PRE_DVE_CTX, pre[0]
            dve.drain().then_inc(s_phase, 1)
            dve.wait_ge(s_phase, 5)

            def statistics(l, i, j, n):
                b = i * PAIR + j
                hold(dve)
                for t in range(QT):
                    link(nc.vector.bn_stats(stats[:, j, t, :], X[:, bass.ds(b, 1), t, :].rearrange("p o d -> p (o d)")))
                settle()
                hold(dve)
                for t in range(QT):
                    link(nc.vector.bn_aggr(mv[:, j, t, :], stats[:, j, t, :]))
                settle()
                nc.vector.tensor_scalar(ve[:, j, :], mv[:, j, :, 1], EPS[l], None, ALU.add).then_inc(var_ready.sem, 1)

            def normalise(l, i, j, n):
                b = i * PAIR + j
                dve.wait_ge(rstd_ready.sem, rstd_ready.of(l, i, 2 * n + j + 1))
                for t in range(QT):
                    last = nc.vector.tensor_scalar(xh[:, j, t, :], X[:, bass.ds(b, 1), t, :].rearrange("p o d -> p (o d)"),
                                                   mv[:, j, t, 0:1], rstd[:, j, t:t + 1], ALU.subtract, ALU.mult)
                last.then_inc(xh_ready.sem, 1)

            def residual(l, i, j, n, name):
                b = i * PAIR + j
                wait_full(dve, l, i, name, j)
                b_ = bank_of(l, name, j)[:, :].rearrange("p (t d) -> p t d", t=QT)
                u = kT[:, j].rearrange("p c s -> p (c s)").rearrange("p (t d) -> p t d", t=QT)
                gate = not (l == 2 and n == 1)
                x = X[:, bass.ds(b, 1)].rearrange("p o t d -> p (o t) d")
                row = BROW_AT[l].get(n)
                g = gates[:, j, n, :].unsqueeze(1).to_broadcast([P, QT, D])
                if n == 0:
                    dve.wait_ge(gates_in[j].sem, gates_in[j].of(l, i, 16))
                if row is not None:
                    bb = brow[:, row, :].unsqueeze(1).to_broadcast([P, QT, D])
                    nc.vector.tensor_tensor(u, b_, bb, ALU.add).then_inc(emptied["V"].sem, 1)
                    wait_taken(dve, l, i, name, j)
                    if gate:
                        link(nc.vector.tensor_tensor(u, u, g, ALU.mult))
                        settle()
                else:
                    nc.vector.tensor_tensor(u, b_, g, ALU.mult).then_inc(emptied["V"].sem, 1)
                    wait_taken(dve, l, i, name, j)
                nc.vector.tensor_tensor(x, x, u, ALU.add).then_inc(added.sem, 1)
                dve.wait_ge(added.sem, added.of(l, i, 2 * n + j + 1))

            def rope(l, i, j, name):
                wait_taken(dve, l, i, name, j)
                hold(dve)
                x = name == "Q"
                r = (qT if x else kT)[:, j].rearrange("p c s -> p (c s)")
                swap = stage[:, (2 * j + x) * 512:(2 * j + x + 1) * 512]
                n = 512 // P
                c, s = (m[:, :].unsqueeze(1).to_broadcast([P, n, P]) for m in (cosT, sinT))
                link(nc.vector.stream_shuffle(swap, r, [p ^ (HD // 2) for p in range(32)]))
                settle()
                rv, wv = (m.rearrange("p (n w) -> p n w", w=P) for m in (r, swap))
                link(nc.vector.tensor_tensor(rv, rv, c, ALU.mult))
                link(nc.vector.tensor_tensor(wv, wv, s, ALU.mult))
                settle()
                nc.vector.tensor_tensor(r, r, swap, ALU.add).then_inc(rope_ready.sem, 1)

            def keys(l, i, j):
                wait_full(dve, l, i, "K", j)
                b_ = bank_of(l, "K", j)
                for c in range(CT):
                    last = nc.vector.tensor_scalar(kT[:, j, c, :], b_[:, c * S:(c + 1) * S], vec[:, BK[l] + c:BK[l] + c + 1], None, ALU.add)
                last.then_inc(emptied["V"].sem, 1)

            def values(l, i, j):
                wait_full(dve, l, i, "V0", j)
                b_ = bank_of(l, "V0", j)
                for t in range(QT):
                    last = nc.vector.tensor_copy(padded(VP, j, t, P), b_[:, t * D:(t + 1) * D].rearrange("p (h e d) -> p h e d", e=2, d=HD))
                last.then_inc(emptied["V"].sem, 1)

            def spread_sums(l, i, j, cross):
                wait_group(dve, exped, l, i, ends(l)[2 * cross + j] - 1)
                if l == 1 and cross:
                    dve.wait_ge(chosen.sem, chosen.of(l, i, ends(l)[2 + j] - NSELF[l]))
                link(nc.vector.reciprocal(rsum[:, :, :], sums[:, j, :, :]))
                settle()
                o = rden[:, :].rearrange("p (t h d) -> p t h d", t=QT, h=H)
                nc.vector.tensor_copy(o, rsum[:, :, :].unsqueeze(3).to_broadcast([P, QT, H, HD])).then_inc(spread.sem, 1)

            def heads_out(l, i, j, cross):
                wait_group(dve, summed, l, i, ends(l)[2 * cross + j] - 1)
                o = oT[:, j].rearrange("p c s -> p (c s)")
                bias = BV.get((l, cross))
                dve.wait_ge(sums_copied.sem, sums_copied.of(l, i, 2 * cross + j + 1))
                if l == 1 and not cross:
                    ov = o.rearrange("p (c s) -> p c s", c=CT)
                    pv = po[:, :].rearrange("p (c s) -> p c s", c=CT)
                    rv = rden[:, :].rearrange("p (c s) -> p c s", c=CT)
                    link(nc.vector.tensor_tensor(ov[:, :, SHIFT:S], pv[:, :, 0:S - SHIFT], rv[:, :, 0:S - SHIFT], ALU.mult))
                    last = nc.vector.tensor_tensor(ov[:, :, 0:SHIFT], pv[:, :, S - SHIFT:S], rv[:, :, S - SHIFT:S], ALU.mult)
                else:
                    last = nc.vector.tensor_tensor(o, po[:, :], rden[:, :], ALU.mult)
                if bias is None:
                    last.then_inc(normed.sem, 1)
                    return
                link(last)
                settle()
                for c in range(CT):
                    last = nc.vector.tensor_scalar(oT[:, j, c, :], oT[:, j, c, :], vec[:, bias + c:bias + c + 1], None, ALU.add)
                last.then_inc(normed.sem, 1)

            def maxima(l, i, n):
                cross, j, qt, h0, hg, kts, width, kp_ = parts(l, n)
                wait_group(dve, scored, l, i, n)
                wait_group(dve, exped, l, i, n - 4)
                keys_ = SC if cross else width
                sc = ps[n % 2][:, 0:hg * width].rearrange("p (h k) -> p h k", h=hg)[:, :, 0:keys_]
                if l == 0:
                    hold(dve)
                    for x in range(hg):
                        m = maskCj[:, j, :] if cross else maskS[:, qt, :]
                        link(nc.vector.tensor_tensor_reduce(sc[:, x, :], sc[:, x, :], m, 1.0, NEG, ALU.add, ALU.max, top1[:, n % 4, x:x + 1]))
                    settle()
                    nc.vector.tensor_scalar(nmax[:, n % 4, 0:hg], top1[:, n % 4, 0:hg], -1.0, None, ALU.mult).then_inc(maxed.sem, 1)
                elif l == 1 and cross:
                    hold(dve)
                    for x in range(hg):
                        link(nc.vector.max(top1[:, x, :], sc[:, x, :]))
                    settle()
                    hold(dve)
                    for x in range(hg):
                        link(nc.vector.match_replace(left1[:, x, :], top1[:, x, :], sc[:, x, :], TAKEN))
                    nc.vector.tensor_scalar(nmax[:, n % 4, 0:hg], top1[:, :, 0], -1.0, None, ALU.mult).then_inc(maxed.sem, 1)
                    settle()
                    hold(dve)
                    for x in range(hg):
                        link(nc.vector.max(top2[:, x, :], left1[:, x, :]))
                    settle()
                    hold(dve)
                    for x in range(hg):
                        link(nc.vector.match_replace(left2[:, n % 2, x, :], top2[:, x, :], left1[:, x, :], TAKEN))
                else:
                    nc.vector.tensor_reduce(nmax[:, n % 4, 0:hg], sc, AX_X, ALU.max, negate=True).then_inc(maxed.sem, 1)

            def strike(l, i, n):
                cross, j, qt, h0, hg, kts, width, kp_ = parts(l, n)
                wait_group(dve, exped, l, i, n)
                settle()
                p = probs[:, n % 4, 0:hg * width].rearrange("p (h k) -> p h k", h=hg)[:, :, 0:SC]
                for x in range(hg):
                    last = nc.vector.scalar_tensor_tensor(p[:, x, :], left2[:, n % 2, x, :], TAKEN, p[:, x, :], ALU.is_equal, ALU.mult,
                                                          accum_out=sums[:, j, qt, h0 + x:h0 + x + 1])
                last.then_inc(chosen.sem, 1)

            def attentions(l, i):
                e = ends(l)
                for step in range(NG[l] + SUM_LAG + 1):
                    if step - SUM_LAG in e:
                        k = e.index(step - SUM_LAG)
                        heads_out(l, i, k % 2, k // 2)
                    if step < NG[l]:
                        maxima(l, i, step)
                    if l == 1 and NSELF[l] <= step - 1 < NG[l]:
                        strike(l, i, step - 1)
                    if 0 <= step - 2 < NG[l] and by_vector(l, step - 2):
                        n = step - 2
                        kp_ = parts(l, n)[-1]
                        wait_group(dve, turned, l, i, n)
                        wait_group(dve, summed, l, i, n - 4)
                        nc.vector.tensor_copy(probsT[0:kp_, n % 4, :], pt[n % 2][0:kp_, :]).then_inc(copied[1].sem, 1)
                    if step in e:
                        k = e.index(step)
                        spread_sums(l, i, k % 2, k // 2)
                    for k in range(3):
                        n = k // 2
                        if step == e[k] + OUT_AT + RES_LAG:
                            residual(l, i, k % 2, n, "OC" if n else "O")
                            statistics(l, i, k % 2, n + 1)
                        if step == e[k] + OUT_AT + NORM_LAG:
                            normalise(l, i, k % 2, n + 1)

            def turn(l, i, more):
                    links[0] = FIRST
                    where[:] = [l, i]
                    for j in range(PAIR):
                        if l > 0:
                            keys(l, i, j)
                        else:
                            rope(l, i, j, "K")
                            rope(l, i, j, "Q")
                        values(l, i, j)
                    if l > 0:
                        dve.wait_ge(s_brow, sum(BROW_N[:l + 1]))
                    attentions(l, i)
                    for name, j in tail(l):
                        if name == "OC":
                            residual(l, i, 1, 1, "OC")
                            statistics(l, i, 1, 2)
                            normalise(l, i, 1, 2)
                        elif name == "MO":
                            if l == 0 and j == 0:
                                dve.wait_ge(s_brow, BROW_N[0])
                            residual(l, i, j, 2, "MO")
                            if j == 0 and more:
                                for x in range(PAIR):
                                    statistics(l, i + 1, x, 0)
                                wait_taken(dve, l, i, "T2", PAIR - 1)
                                for x in range(PAIR):
                                    normalise(l, i + 1, x, 0)
                        elif l == 1 and name[0] == "M":
                            hid, m = hidden(j, l), int(name[1:])
                            dve.wait_ge(silu_done.sem, silu_done.of(l, i, j * HT_N + m + 1))
                            b_ = bank_of(l, name, j)
                            c = B1[l] + HT_N + m
                            nc.vector.scalar_tensor_tensor(hid[:, m, :], b_[:, S:2 * S], vec[:, c:c + 1], hid[:, m, :], ALU.add, ALU.mult).then_inc(emptied["V"].sem, 1)

            def first_norm(l):
                links[0] = 0
                where[:] = [l, 0]
                for j in range(PAIR):
                    statistics(l, 0, j, 0)
                for j in range(PAIR):
                    normalise(l, 0, j, 0)
                assert links[0] == FIRST, links[0]

            for l in range(3):
                first_norm(l)
                with dve.Fori(0, TURNS - 1) as i:
                    turn(l, i, True)
                    LINKS[l] = links[0] - FIRST
                turn(l, TURNS - 1, False)
                layer_done(dve, l + 1)

            l = 3
            dve.wait_ge(s_brow, sum(BROW_N))
            dve.wait_ge(s_pre_empty, KEYS_IN[3] + 1)
            bh = vec[:, VC(3, "e_b1"):VC(3, "e_b1") + M3].unsqueeze(2).to_broadcast([P, M3, B])
            nc.vector.tensor_tensor(anchor[:, :, :], anchor[:, :, :], bh, ALU.add).then_inc(s_mask, 1)

            def last_layer(l, i, more):
                links[0] = FIRST
                where[:] = [l, i]
                for j in range(PAIR):
                    wait_full(dve, l, i, "S", j)
                    sc = bank_of(l, "S", j)[:, 0:QT * SC].rearrange("p (t k) -> p t k", t=QT)
                    nc.vector.tensor_reduce(nmax[:, j, 0:QT], sc, AX_X, ALU.max, negate=True).then_inc(dve3.sem, 1)
                for j in range(PAIR):
                    wait_taken(dve, l, i, "S", j)
                    link(nc.vector.reciprocal(small[:, j, :, 0], small[:, j, :, 0]))
                    settle()
                    for t in range(QT):
                        p = probs[:, j, t * SC:(t + 1) * SC]
                        last = nc.vector.tensor_scalar(p, p, small[:, j, t, 0:1], None, ALU.mult)
                    last.then_inc(dve3.sem, 1)
                for j in range(PAIR):
                    wait_full(dve, l, i, "RT", j)
                    b_ = bank_of(l, "RT", j)[:, 0:QT * E_N].rearrange("p (t e) -> p t e", t=QT)
                    link(nc.vector.tensor_reduce(nmax[:, 2 + j, 0:QT], b_, AX_X, ALU.max))
                    settle()
                    nc.vector.tensor_tensor(rp[:, j, :, :], b_, nmax[:, 2 + j, 0:QT].unsqueeze(2).to_broadcast([P, QT, E_N]), ALU.subtract).then_inc(emptied["V"].sem, 1)
                for j in range(PAIR):
                    act3_k = 1 + j
                    dve.wait_ge(act3.sem, act3.of(l, i, act3_k))
                    link(nc.vector.reciprocal(small[:, j, :, 1], small[:, j, :, 1]))
                    settle()
                    link(nc.vector.tensor_tensor(rp[:, j, :, :], rp[:, j, :, :], small[:, j, :, 1:2].to_broadcast([P, QT, E_N]), ALU.mult))
                    settle()
                    for t in range(QT):
                        link(nc.vector.tensor_scalar(xh[:, j, t, :], brow[:, 0, :], rp[:, j, t, 0:1], None, ALU.mult))
                    for e in range(1, E_N):
                        settle()
                        for t in range(QT):
                            link(nc.vector.scalar_tensor_tensor(xh[:, j, t, :], brow[:, e, :], rp[:, j, t, e:e + 1], xh[:, j, t, :], ALU.mult, ALU.add))
                settle()
                for j in range(PAIR):
                    for e in range(E_N):
                        wait_full(dve, l, i, f"E{e}", j)
                        b_ = bank_of(l, f"E{e}", j)
                        for t in range(QT):
                            last = nc.vector.scalar_tensor_tensor(xh[:, j, t, :], b_[:, t * D:(t + 1) * D], rp[:, j, t, e:e + 1], xh[:, j, t, :], ALU.mult, ALU.add)
                        last.then_inc(emptied["V"].sem, 1)
                        wait_taken(dve, l, i, f"E{e}", j)
                for j in range(PAIR):
                    wait_full(dve, l, i, "GO", j)
                    g = kT[:, j].rearrange("p c s -> p (c s)").rearrange("p (t d) -> p t d", t=QT)
                    b_ = bank_of(l, "GO", j)[:, :].rearrange("p (t d) -> p t d", t=QT)
                    nc.vector.tensor_tensor(g, b_, brow[:, 3, :].unsqueeze(1).to_broadcast([P, QT, D]), ALU.add).then_inc(emptied["V"].sem, 1)
                if more:
                    for j in range(PAIR):
                        statistics(l, i + 1, j, 0)
                    for j in range(PAIR):
                        wait_taken(dve, l, i, "RR", j)
                        normalise(l, i + 1, j, 0)
                for j in range(PAIR):
                    b = i * PAIR + j
                    g = kT[:, j].rearrange("p c s -> p (c s)").rearrange("p (t d) -> p t d", t=QT)
                    u = probs[:, j, :].rearrange("p (t d) -> p t d", t=QT)
                    dve.wait_ge(act3.sem, act3.of(l, i, 3 + j))
                    link(nc.vector.tensor_scalar(g, g, 1.0, 0.5, ALU.add, ALU.mult))
                    wait_full(dve, l, i, "OUT", j)
                    b_ = bank_of(l, "OUT", j)[:, :].rearrange("p (t d) -> p t d", t=QT)
                    nc.vector.tensor_tensor(u, b_, brow[:, 4, :].unsqueeze(1).to_broadcast([P, QT, D]), ALU.add).then_inc(emptied["V"].sem, 1)
                    settle()
                    wait_taken(dve, l, i, "OUT", j)
                    link(nc.vector.tensor_tensor(u, u, g, ALU.mult))
                    settle()
                    x = X[:, bass.ds(b, 1)].rearrange("p o t d -> p (o t) d")
                    nc.vector.tensor_tensor(x, x, u, ALU.add).then_inc(added.sem, 1)

            first_norm(3)
            with dve.Fori(0, TURNS - 1) as i:
                last_layer(3, i, True)
                LINKS[3] = links[0] - FIRST
            last_layer(3, TURNS - 1, False)
        assert tuple(LINKS[l] for l in range(4)) == DVE_LINKS, LINKS


def kernel(**inputs):
    import numpy as np
    import concourse.bacc as bacc
    from concourse.bass_utils import run_bass_kernel_spmd as run

    nc = bacc.Bacc("TRN2", target_bir_lowering=False, num_devices=1)
    arrays = {}
    for name, x in inputs.items():
        x = np.ascontiguousarray(x)
        arrays[name] = x.reshape(-1).view(np.int32) if x.dtype == np.bool_ else x
    inv = 1.0 / 10000.0 ** (np.arange(0, HD, 2, dtype=np.float32) / HD)
    freqs = np.outer(np.arange(P, dtype=np.float32), inv)
    emb = np.concatenate([freqs, freqs], axis=-1)
    sign = np.where(np.arange(HD) < HD // 2, -1.0, 1.0).astype(np.float32)
    arrays["rope_cos"] = np.ascontiguousarray(np.tile(np.cos(emb).astype(np.float32).T, (HPT, 1)))
    arrays["rope_sin"] = np.ascontiguousarray(np.tile((np.sin(emb).astype(np.float32) * sign).T, (HPT, 1)))
    aps = {n: nc.dram_tensor(f"in_{n}", x.shape, mybir.dt.from_np(x.dtype), kind="ExternalInput").ap() for n, x in arrays.items()}
    out = nc.dram_tensor("out", (B, S, D), F32, kind="ExternalOutput").ap()
    build(nc, aps, out)
    r = run(nc, [{f"in_{n}": x for n, x in arrays.items()}], core_ids=[0])
    return r.results[0]["out"]
```

```python
from contextlib import ExitStack

import concourse.bass as bass
from concourse import mybir

ALU = mybir.AluOpType
ACT = mybir.ActivationFunctionType
F32 = mybir.dt.float32
U8 = mybir.dt.uint8
I32 = mybir.dt.int32
AX_X = mybir.AxisListType.X

P = 128
B, S, D = 8, 256, 256
SC = 77
SCP = 96
H, HD = 16, 16
CT = D // P
QT = S // P
HPT = P // HD
PAIR = 2
TURNS = B // PAIR
HID = 4 * D
HT_N = HID // P
E_N, RH = 3, 512
M3 = E_N * RH // P + CT
NEG = -3.4028234663852886e38
TAKEN = -3.0e38
SCALE = HD ** -0.5
SCALE3 = D ** -0.5
EPS = (1e-5, 1e-6, 1e-6, 1e-5)
SHIFT = 64
W_EVEN, W_ODD = 8192, 12288

SELF = {0: (2, 2), 1: (4, 1), 2: (2, 2)}
CROSS = (4, 1)


def groups(hg):
    return QT * H // hg


class Mark:

    def __init__(self, sem, per):
        self.sem, self.per, self.credit = sem, per, max(per)

    def base(self, l):
        return self.credit + TURNS * sum(self.per[:l])

    def of(self, l, i, k):
        return i * self.per[l] + (self.base(l) + k)

    def before(self, l, i, k):
        return i * self.per[l] + (self.base(l) - self.per[l] + k)


TURN_LAG, SUM_LAG = 2, 4
SPREAD_AT, VALUES_AT, OUT_AT = 2, SUM_LAG - 1, SUM_LAG
TURN_AT = (((8, 6), (6, 6), (8, 6)), (8, 8, 8))
ROPE_AT = 2
RES_LAG, STAT_LAG, NORM_LAG = 0, 0, 1


def ends(l):
    a, c = NSELF[l] // 2, NCROSS // 2
    return [a, 2 * a, 2 * a + c, 2 * a + 2 * c]


def between(l):
    e = ends(l)
    at = {x + SPREAD_AT: [("DC" if k > 1 else "DS", k % 2)] for k, x in enumerate(e)}
    for j in range(PAIR):
        for d, name in ((VALUES_AT, "VC"), (OUT_AT, "O"), (TURN_AT[0][l][j], "T1"), (TURN_AT[0][l][j] + 1, "QC")):
            at.setdefault(e[j] + d, []).append((name, j))
    for d, name in ((OUT_AT, "OC"), (TURN_AT[1][l], "T2")):
        at.setdefault(e[2] + d, []).append((name, 0))
    return at


def tail(l):
    m = [f"M{x}" for x in range(HT_N if l == 1 else HT_N // 2)]
    first = [(x, 0) for x in m]
    if l == 1:
        first[5:5] = [("T2", 1)]
    else:
        first[4:4] = [("T2", 1)]
    first[1:1] = [("OC", 1)]
    return first + [("MO", 0)] + [(x, 1) for x in m] + [("MO", 1)]


def projection_uses(l):
    both = lambda *names: [(n, j, o) for j in range(PAIR) for n, o in names]
    if l < 3:
        uses = both(("T0", "A"))
        uses += both(("K", "A" if l == 0 else "V"), ("Q", "A"), ("V0", "V"))
        owner = {"DS": "A", "DC": "A", "VC": "A", "O": "V", "T1": "A", "QC": "A", "OC": "V", "T2": "A", "MO": "V"}
        rest = [x for step in sorted(between(l)) for x in between(l)[step]] + tail(l)
        uses += [(n, j, owner.get(n, "V" if l == 1 else "A")) for n, j in rest]
    else:
        uses = both(("T0", "A")) + both(("Q", "A")) + both(("VC", "A"))
        uses += both(("S", "A")) + both(("PT", "A"))
        uses += both(("EV", "A")) + both(("RL", "A")) + both(("RT", "V"))
        uses += both(*[(f"M{m}", "A") for m in range(M3 // 2)])
        uses += both(*[(f"E{e}", "V") for e in range(E_N)])
        uses += both(("GO", "V")) + both(("RR", "A")) + both(("OUT", "V"))
    return uses


NSELF = [PAIR * groups(SELF[l][0]) for l in range(3)]
NCROSS = PAIR * groups(CROSS[0])
NG = [n + NCROSS for n in NSELF] + [0]
USES = [projection_uses(l) for l in range(4)]
INDEX = [{(n, j): k for k, (n, j, _) in enumerate(u)} for u in USES]
ORDER = [[sum(x[2] == u[k][2] for x in u[:k + 1]) for k in range(len(u))] for u in USES]
COUNT = {o: [sum(x[2] == o for x in u) for u in USES] for o in "AV"}
NLN = (3, 3, 3, 1)



def by_vector(l, n):
    return n % 2 == 1 if n < NSELF[l] else l != 1


VECTORS = [("L0_xcond_norm1_w", 2), ("L0_xcond_normc_w", 2), ("L0_xcond_norm2_w", 2), ("L0_xcond_mlp_b1", 8),
           ("L1_xcond_b_qkv", 6), ("L1_xcond_b_q", 2), ("L1_xcond_b_kv", 4), ("L1_xcond_b_m1", 16),
           ("L2_xcond_b_qkv", 6), ("L2_xcond_b_qc", 2), ("L2_xcond_b_kvc", 4), ("L2_xcond_b_mlp1", 8),
           ("L3_xcond_ln_gamma", 2), ("L3_xcond_ln_beta", 2), ("L3_xcond_e_b1", 12), ("L3_xcond_gate_b1", 2)]
ROW, NROW = {}, 0
for _n, _k in VECTORS:
    ROW[_n] = NROW
    NROW += _k

NPRE = [(9 * D + 511) // 512, (9 * D + 511) // 512, (6 * D + 511) // 512]
ROWS_IN = [sum(NPRE[:l + 1]) for l in range(3)]
PRE_MODS = 1 + ROWS_IN[2] + 1 + 3
PRE_RAW = PRE_MODS + 3
PRE_ALL = PRE_RAW + 3
KEY_BANKS = CT * ((B * SC + 511) // 512)
KEYS_IN = [PRE_ALL - ROWS_IN[2] + (l + 1) * KEY_BANKS for l in range(4)]
PRE_LOADS = 1 + len(VECTORS) + 6

FIRST = 4 * PAIR
DVE_LINKS = (168, 290, 32, 32)


def mod_rows(KM, l):
    n = (0, 9 * D, 18 * D, 24 * D)
    return KM[0:B].rearrange("p j c h s -> p (j c h s)")[:, n[l]:n[l + 1]]


def padded(VP, j, t, n):
    return VP[0:n, j, t].rearrange("p h e (u d) -> p h (e u) d", d=HD)[:, :, 0:4:3, :]


def V3(VP, j):
    return VP[0:SCP, j, 0].rearrange("p h e w -> p (h e w)")[:, 0:D]


LINKS = {}
PRE_DVE_VAR = 2 * B + 1
PRE_DVE_CTX = PRE_DVE_VAR + 4 + B


def build(nc, a, out):
    A = lambda l, n: a[f"L{l}_xcond_{n}"]
    with ExitStack() as ctx:
        def sb(name, shape, dt=F32):
            return ctx.enter_context(nc.sbuf_tensor(name, shape, dt))

        def sem(name):
            return ctx.enter_context(nc.semaphore(name))

        X = sb("X", [P, B, QT, D])
        w_even = sb("w_even", [P, W_EVEN])
        w_odd = sb("w_odd", [P, W_ODD])
        KM = sb("KM", [P, PAIR, CT, HPT, S])
        probs = sb("probs", [P, 4, 512])
        probsT = sb("probsT", [P, 4, 512])
        xh = sb("xh", [P, PAIR, QT, D])
        oT = xh
        hT = sb("hT", [P, PAIR, CT, S])
        qT = sb("qT", [P, PAIR, CT, S])
        kT = sb("kT", [P, PAIR, CT, S])
        VP = sb("VP", [P, PAIR, QT, HPT, 2, 32])
        gates = sb("gates", [P, PAIR, 3, D])
        brow = sb("brow", [P, 5, D])
        ctxT = sb("ctxT", [P, CT, B * SC])
        ctxnT = sb("ctxnT", [P, CT, B * SC])
        kcT = sb("kcT", [P, CT, B * SC])
        cs = sb("cs", [P, PAIR, CT, SCP])
        mods = sb("mods", [P, 3, 12, B])
        cols = sb("cols", [P, PAIR, 12])
        vec = sb("vec", [P, NROW])
        bq = sb("bq", [P, 2, 4])
        ident = sb("ident", [P, P])
        cosT = sb("cosT", [P, P])
        sinT = sb("sinT", [P, P])
        maskS = sb("maskS", [P, QT, S])
        maskC = sb("maskC", [P, B, SC])
        maskCj = sb("maskCj", [P, PAIR, SC])
        maskSw = sb("maskSw", [P, QT * S // 4], I32)
        maskCw = sb("maskCw", [P, B * SC // 4], I32)
        maskSb = maskSw[:, :].bitcast(U8).rearrange("p (t k) -> p t k", t=QT)
        maskCb = maskCw[:, :].bitcast(U8).rearrange("p (b k) -> p b k", b=B)
        cT = sb("cT", [P, CT, B])
        scT = sb("scT", [P, CT, B])
        crow = xh[0:B, 0, 0, :]
        srow = xh[0:B, 0, 1, :]
        nmax = sb("nmax", [P, 4, 4])
        top1 = sb("top1", [P, 4, 8])
        top2 = sb("top2", [P, 4, 8])
        left = maskC[:, :, :].rearrange("p (n h) k -> p n h k", n=2)
        rden = sb("rden", [P, CT * S])
        sums = sb("sums", [P, PAIR, QT, H])
        rsum = sb("rsum", [P, QT, H])
        gb = brow[:, 4, :]
        stats = sb("stats", [P, PAIR, QT, 6])
        mv = sb("mv", [P, PAIR, QT, 2])
        ve = sb("ve", [P, PAIR, QT])
        rstd = sb("rstd", [P, PAIR, QT])
        warm = sb("warm", [P, 2])
        mhalf = sb("mhalf", [P, 8])
        anchor = gates[:, 0, 1, 0:M3 * B].rearrange("p (m b) -> p m b", b=B)
        anc = sb("anc", [P, PAIR, M3])
        ranchor = sb("ranchor", [E_N, B + 1])
        ranc = sb("ranc", [E_N, PAIR])
        rb = sb("rb", [E_N, 1])
        logT = gates[0:E_N, :, 0, :]
        rp = sb("rp", [P, PAIR, QT, E_N])
        small = sb("small", [P, PAIR, QT, 2])
        stage = probs[:, :, :].rearrange("p a b -> p (a b)")
        scratch = nc.dram_tensor("gate_rows", [3, B, 3 * D], F32, kind="Internal").ap()

        bank = [ctx.enter_context(nc.psum_tensor(f"bank{n}", [P, 512], F32)) for n in range(8)]
        pj, ps, pt, po = bank[0:2], bank[2:5], bank[5:7], bank[7]

        s_in = sem("inputs_landed")
        s_cond = sem("condition_landed")
        s_bias = sem("modulation_biases_landed")
        s_ada = [sem(f"ada_landed{l}") for l in range(3)]
        s_w = [sem(f"weights_landed{l}") for l in range(4)]
        s_w3 = sem("more_weights_landed3")
        s_brow = sem("bias_rows_landed")
        s_const = sem("constants_made")
        s_anchor = sem("anchor_biased")
        s_phase = sem("engine_done_with_layer")
        s_pre_full = sem("prelude_bank_full")
        s_pre_empty = sem("prelude_bank_emptied_by_scalar")
        s_rows = sem("modulation_rows_bank_emptied_by_vector")
        s_pre_dve = sem("prelude_vector_step")
        s_pre_act = sem("prelude_scalar_step")
        s_pre_pool = sem("prelude_pool_step")
        s_gates_out = sem("gate_rows_stored")
        s_out = sem("outputs_stored")
        s_held = {}
        credited = []

        def mark(name, per):
            m = Mark(sem(name), tuple(per))
            credited.append(m)
            return m

        full = mark("projection_bank_full", [len(u) for u in USES])
        emptied = {"A": mark("bank_emptied_by_scalar", COUNT["A"]), "V": mark("bank_emptied_by_vector", COUNT["V"])}
        var_ready = mark("variance_ready", [2 * n for n in NLN])
        rstd_ready = mark("rstd_ready", [2 * n for n in NLN])
        xh_ready = mark("tokens_normalised", [2 * n for n in NLN])
        rope_ready = mark("rope_done", [4, 0, 0, 0])
        scored = mark("scores_ready", NG)
        maxed = mark("max_ready", NG)
        exped = mark("exp_ready", NG)
        chosen = mark("topk_applied", [0, NCROSS, 0, 0])
        turned = mark("probs_transposed", NG)
        copied = [mark(f"probsT_copied_{n}", [sum(by_vector(l, g) == (n == "vector") for g in range(NG[l])) for l in range(4)]) for n in ("scalar", "vector")]
        spread = mark("denominators_spread", [4, 4, 4, 0])
        summed = mark("values_summed", NG)
        normed = mark("heads_normalised", [4, 4, 4, 0])
        biased = mark("biases_added", [2, 6, 6, 0])
        bias_gated = mark("biases_gated", [2, 6, 4, 0])
        added = mark("residual_added", [6, 6, 6, 2])
        picked = mark("batch_columns_copied", [2, 2, 2, 2])
        gates_in = [mark(f"gates_landed{j}", [16, 16, 16, 0]) for j in range(PAIR)]
        keys_in = [mark(f"masked_keys_landed{j}", [256, 256, 256, 0]) for j in range(PAIR)]
        act3 = mark("layer3_scalar_step", [0, 0, 0, 4])
        silu_done = mark("silu_ready", [0, PAIR * HT_N, 0, 0])
        dve3 = mark("layer3_vector_step", [0, 0, 0, 4])
        dve_own = mark("vector_own_step", DVE_LINKS)

        def region(buf, at, *shape):
            n = 1
            for s in shape:
                n *= s
            v = buf[:, at:at + n]
            if len(shape) == 2:
                v = v.rearrange("p (k n) -> p k n", n=shape[1])
            elif len(shape) == 3:
                v = v.rearrange("p (e k n) -> p e k n", k=shape[1], n=shape[2])
            return v

        def lay(buf, items):
            got, at = {}, 0
            for name, *shape in items:
                n = 1
                for s in shape:
                    n *= s
                got[name] = region(buf, at, *shape)
                at += n
            assert at <= buf.shape[1], (at, buf.shape)
            return got

        common = lambda kv, m1: [("qkv", CT, 3 * D), ("so", CT, D), ("cq", CT, D), *kv, ("co", CT, D), ("m1", CT, m1), ("m2", HT_N, D)]
        W = [lay(w_even, common([("ck", CT, D), ("cv", CT, D)], HID)),
             lay(w_odd, common([("ckv", CT, 2 * D)], 2 * HID)),
             lay(w_even, common([("ckv", CT, 2 * D)], HID)),
             lay(w_odd, [("e1", E_N, 4, RH), ("e2", E_N, 4, D), ("wq", CT, D), ("ck", CT, D), ("cv", CT, D), ("g1", 4, D), ("g2", CT, D)])]
        W3 = lay(w_even, [("out", CT, D), ("e1a", E_N, CT, RH), ("g1a", CT, D), ("r", 4, E_N), ("ra", CT, E_N)])
        ADA_N = (9 * D, 9 * D, 6 * D)
        WA = lay(w_odd, [("0", CT, ADA_N[0]), ("1", CT, ADA_N[1]), ("2", CT, ADA_N[2])])
        for l in (1, 2):
            W[l]["ck"], W[l]["cv"] = W[l]["ckv"][:, :, 0:D], W[l]["ckv"][:, :, D:2 * D]
        kp = lambda w: w.rearrange("(k p) n -> p k n", p=P)
        LOADS = [
            [("qkv", "qkv_W"), ("so", "attn_out_W"), ("cq", "cq_W"), ("ck", "ck_W"), ("cv", "cv_W"), ("co", "co_W"), ("m1", "mlp_W1"), ("m2", "mlp_W2")],
            [("qkv", "w_qkv"), ("so", "w_so"), ("cq", "w_q"), ("ckv", "w_kv"), ("co", "w_co"), ("m1", "w_m1"), ("m2", "w_m2")],
            [("qkv", "W_qkv"), ("so", "W_proj"), ("cq", "W_qc"), ("ckv", "W_kvc"), ("co", "W_cproj"), ("m1", "W_mlp1"), ("m2", "W_mlp2")],
        ]
        LOADED = [16 * len(x) for x in LOADS] + [16 * 11]
        BROWS = [["mlp_b2"], ["b_so", "b_co", "b_m2"], ["b_proj", "b_cproj", "b_mlp2"], ["e_b2", "gate_b2", "out_b"]]
        BROW_AT = [{2: 0}, {0: 0, 1: 1, 2: 2}, {0: 0, 1: 1, 2: 2}]
        BROW_N = [16 * len(x) for x in BROWS]
        VC = lambda l, name: ROW[f"L{l}_xcond_{name}"]
        BK = {1: VC(1, "b_qkv") + 2, 2: VC(2, "b_qkv") + 2}
        BV = {(1, 0): VC(1, "b_qkv") + 4, (2, 0): VC(2, "b_qkv") + 4, (1, 1): VC(1, "b_kv") + 2, (2, 1): VC(2, "b_kvc") + 2}
        BKC = {1: VC(1, "b_kv"), 2: VC(2, "b_kvc")}
        B1 = {0: VC(0, "mlp_b1"), 1: VC(1, "b_m1"), 2: VC(2, "b_mlp1")}
        MOD = {0: [(0, 1, 2), (3, 4, 5), (6, 7, 8)], 1: [(0, 1, 2), (3, 4, 5), (6, 7, 8)], 2: [(0, 1, 2), None, (3, 4, 5)]}

        def wait_full(eng, l, i, name, j):
            eng.wait_ge(full.sem, full.of(l, i, INDEX[l][name, j] + 1))

        def wait_taken(eng, l, i, name, j):
            k = INDEX[l][name, j]
            m = emptied[USES[l][k][2]]
            eng.wait_ge(m.sem, m.of(l, i, ORDER[l][k]))

        def wait_free(eng, l, i, name, j, *needs):
            k = INDEX[l][name, j]
            last = k - 2 if k >= 2 else max(x for x in range(len(USES[l])) if x % 2 == k % 2)
            owner = USES[l][last][2]
            least = {owner: ORDER[l][last] - (0 if k >= 2 else emptied[owner].per[l])}
            for n in needs:
                x = INDEX[l][n, j]
                owner = USES[l][x][2]
                least[owner] = max(ORDER[l][x], least.get(owner, ORDER[l][x]))
            for owner, k_ in least.items():
                eng.wait_ge(emptied[owner].sem, emptied[owner].of(l, i, k_))
            return pj[k % 2]

        def bank_of(l, name, j):
            return pj[INDEX[l][name, j] % 2]

        def wait_group(eng, m, l, i, n):
            if n >= 0:
                eng.wait_ge(m.sem, m.of(l, i, n + 1))
            else:
                eng.wait_ge(m.sem, m.before(l, i, m.per[l] + n + 1))

        def wait_copied(eng, l, i, n):
            g = n % NG[l]
            m = copied[by_vector(l, g)]
            k = sum(by_vector(l, x) == by_vector(l, g) for x in range(g + 1))
            eng.wait_ge(m.sem, m.of(l, i, k) if n >= 0 else m.before(l, i, k))

        def gated(l, n):
            return not (l == 2 and n == 1)

        def bias_event(l, n, j):
            rows = sorted(BROW_AT[l])
            return rows.index(n) * PAIR + j + 1 if n in rows else 0

        def hold(eng):
            eng.sem_inc(s_held[eng], 1)

        def parts(l, n):
            cross = n >= NSELF[l]
            hg, kts = CROSS if cross else SELF[l]
            g, per = n - NSELF[l] * cross, H // hg
            return cross, g // (QT * per), g // per % QT, g % per * hg, hg, kts, SC if cross else kts * P, SCP if cross else P

        def layer_done(eng, l):
            eng.drain().then_inc(s_phase, 1)
            eng.wait_ge(s_phase, 5 * (l + 1))

        def hidden(j, l):
            if l == 3:
                return KM[:, j].rearrange("p c h s -> p (c h) s")
            buf = probs if j == 0 else probsT
            return buf[:, :, :].rearrange("p a (b s) -> p (a b) s", s=S)

        block = ctx.enter_context(nc.Block())

        @block.sync
        def _(sp):
            sp.dma_start(crow, a["cond_1024"]).then_inc(s_cond, 16)
            for l, n in enumerate(("adaLN_b", "b_ada", "b_mod")):
                sp.dma_start(mod_rows(KM, l), A(l, n).rearrange("(o n) -> o n", o=1).to_broadcast([B, ADA_N[l]])).then_inc(s_bias, 16)
            sp.dma_start(WA["0"], kp(A(0, "adaLN_W"))).then_inc(s_ada[0], 16)
            ctx_tok = stage[0:SC, 0:B * D].rearrange("p (b d) -> p b d", b=B)
            sp.dma_start(ctx_tok, a["ctx_1024"].rearrange("b s d -> s b d")).then_inc(s_in, 16)
            vst = hT[:, 0, 0, 0:P]
            for n, k in VECTORS:
                r = ROW[n]
                v = a[n]
                if len(v.shape) == 2:
                    v = v.rearrange("e n -> (e n)")
                sp.dma_start(vst[r:r + k, :], v.rearrange("(k p) -> k p", p=P)).then_inc(s_in, 16)
            for l, n in ((1, "w_ada"), (2, "W_mod")):
                sp.dma_start(WA[str(l)], kp(A(l, n))).then_inc(s_ada[l], 16)
                if l == 1:
                    sp.dma_start(X[:, :, :, :].rearrange("p b t d -> p (b t) d"), a["x"].rearrange("b (t p) d -> p (b t) d", p=P)).then_inc(s_in, 16)
                    sp.dma_start(maskSw[:, :].rearrange("p (t k) -> p t k", t=QT), a["mask_SxS_bk0"].rearrange("(t p k) -> p t k", p=P, t=QT)).then_inc(s_in, 16)
                    sp.dma_start(maskCw[:, :], a["mask_BxS2_bf1"].rearrange("(o k) -> o k", o=1).to_broadcast([P, B * SC // 4])).then_inc(s_in, 16)
                    sp.dma_start(cosT[:, :], a["rope_cos"]).then_inc(s_in, 16)
                    sp.dma_start(sinT[:, :], a["rope_sin"]).then_inc(s_in, 16)
                    sp.dma_start(rb[:, :], A(3, "router_b").rearrange("(e o) -> e o", o=1)).then_inc(s_in, 16)
            for name, src in LOADS[0]:
                sp.dma_start(W[0][name], kp(A(0, src))).then_inc(s_w[0], 16)
            for l in range(3):
                sp.wait_ge(s_rows, ROWS_IN[l])
                for n, m in enumerate(MOD[l]):
                    g = (m or MOD[l][0])[2]
                    sp.dma_start(scratch[l, :, n * D:(n + 1) * D], mod_rows(KM, l)[:, g * D:(g + 1) * D]).then_inc(s_gates_out, 16)
            sp.wait_ge(s_gates_out, 16 * 9)
            sp.drain().then_inc(s_phase, 1)
            sp.wait_ge(s_phase, 5)
            for l in range(4):
                r = 0
                for n in BROWS[l]:
                    v = A(l, n)
                    if n == "e_b2":
                        sp.dma_start(brow[:, 0:E_N, :], v.rearrange("(o e) n -> o e n", o=1).to_broadcast([P, E_N, D])).then_inc(s_brow, 16)
                        r += E_N
                    else:
                        sp.dma_start(brow[:, r, :], v.rearrange("(o n) -> o n", o=1).to_broadcast([P, D])).then_inc(s_brow, 16)
                        r += 1
                if l == 3:
                    for e in range(E_N):
                        sp.dma_start(W3["e1a"][:, e], A(3, "e_w1")[e, 4 * P:6 * P, :].rearrange("(k p) n -> p k n", p=P)).then_inc(s_w3, 16)
                    sp.dma_start(W3["g1a"], kp(A(3, "gate_w1")[4 * P:6 * P, :])).then_inc(s_w3, 16)
                    sp.dma_start(W3["r"], kp(A(3, "router_W")[0:4 * P, :])).then_inc(s_w3, 16)
                    sp.dma_start(W3["ra"], kp(A(3, "router_W")[4 * P:6 * P, :])).then_inc(s_w3, 16)
                    sp.dma_start(W3["out"], kp(A(3, "out_w"))).then_inc(s_w3, 16)
                elif l == 2:
                    for n, src in (("ck", "Wk"), ("cv", "Wv"), ("wq", "Wq"), ("g2", "gate_w2")):
                        sp.dma_start(W[3][n], kp(A(3, src))).then_inc(s_w[3], 16)
                    sp.dma_start(W[3]["g1"], kp(A(3, "gate_w1")[0:4 * P, :])).then_inc(s_w[3], 16)
                    for e in range(E_N):
                        sp.dma_start(W[3]["e1"][:, e], kp(A(3, "e_w1")[e, 0:4 * P, :])).then_inc(s_w[3], 16)
                        sp.dma_start(W[3]["e2"][:, e], kp(A(3, "e_w2")[e])).then_inc(s_w[3], 16)
                else:
                    for name, src in LOADS[l + 1]:
                        sp.dma_start(W[l + 1][name], kp(A(l + 1, src))).then_inc(s_w[l + 1], 16)
                if l == 3:
                    with sp.Fori(0, TURNS) as i:
                        for j in range(PAIR):
                            sp.wait_ge(added.sem, added.of(3, i, j + 1))
                            sp.dma_start(out[bass.ds(i * PAIR + j, 1)].rearrange("o (t p) d -> p (o t) d", p=P),
                                         X[:, bass.ds(i * PAIR + j, 1)].rearrange("p o t d -> p (o t) d")).then_inc(s_out, 16)
                    sp.wait_ge(s_out, 16 * B)
                else:
                    sp.wait_ge(s_pre_empty, KEYS_IN[l])
                    with sp.Fori(0, TURNS) as i:
                        for j in range(PAIR):
                            if l == 0:
                                sp.wait_ge(rope_ready.sem, rope_ready.of(l, i, 2 * j + 1))
                            else:
                                wait_taken(sp, l, i, "K", j)
                            for h in range(HPT):
                                sp.dma_start(KM[HD * h:HD * (h + 1), j, :, h, :], kT[HD * h:HD * (h + 1), j, :, :]).then_inc(keys_in[j].sem, 16)
                        for j in range(PAIR):
                            sp.wait_ge(added.sem, added.before(l, i, 5 + j))
                            sp.dma_start(gates[:, j].rearrange("p g d -> p (g d)"),
                                         scratch[l, bass.ds(i * PAIR + j, 1), :].to_broadcast([P, 3 * D])).then_inc(gates_in[j].sem, 16)
                        for j in range(PAIR):
                            wait_group(sp, scored, l, i, (j + 1) * NSELF[l] // 2 - 1)
                            for h in range(HPT):
                                sp.dma_start(KM[HD * h:HD * (h + 1), j, :, h, 0:SC],
                                             kcT[HD * h:HD * (h + 1), :, bass.ds((i * PAIR + j) * SC, SC)]).then_inc(keys_in[j].sem, 16)
                if l < 3:
                    layer_done(sp, l + 1)

        @block.gpsimd
        def _(pool):
            s_held[pool] = sem("pool_held")
            for m in credited:
                pool.sem_inc(m.sem, m.credit)
            nc.gpsimd.memset(ident[:, :], 0.0).then_inc(s_pre_pool, 1)
            pool.wait_ge(s_pre_pool, 1)
            nc.gpsimd.affine_select(out=ident[:, :], in_=ident[:, :], compare_op=ALU.not_equal, fill=1.0,
                                    base=0, pattern=[[-1, P]], channel_multiplier=1).then_inc(s_const, 1)
            nc.gpsimd.memset(mods[:, :, :, :].rearrange("p l c b -> p (l c b)"), 0.0).then_inc(s_const, 1)
            nc.gpsimd.memset(cs[:, :, :, :].rearrange("p j c k -> p (j c k)"), 0.0).then_inc(s_pre_pool, 1)
            nc.gpsimd.memset(warm[:, :], 0.0).then_inc(s_pre_pool, 1)
            nc.gpsimd.memset(mhalf[:, :], -0.5).then_inc(s_pre_pool, 1)
            nc.gpsimd.memset(VP[:, :].rearrange("p j t h e w -> p (j t h e w)"), 0.0).then_inc(s_const, 1)
            pool.wait_ge(s_pre_pool, 4)
            pool.wait_ge(s_pre_dve, PRE_DVE_VAR)
            nc.gpsimd.tensor_tensor(rden[0:SC, 16:24], rden[0:SC, 8:16], mhalf[0:SC, :], ALU.pow).then_inc(s_pre_pool, 1)
            pool.wait_ge(s_pre_full, PRE_MODS)
            pool.wait_ge(s_gates_out, 16 * 9)
            for j in range(PAIR):
                nc.gpsimd.memset(KM[:, j].rearrange("p c h s -> p (c h s)"), 0.0).then_inc(s_const, 1)
            pool.drain().then_inc(s_phase, 1)
            pool.wait_ge(s_phase, 5)
            def inverse(l, i, k):
                pool.wait_ge(var_ready.sem, var_ready.of(l, i, k + 1))
                nc.gpsimd.tensor_tensor(rstd[:, k % 2, :], ve[:, k % 2, :], mhalf[:, 0:QT], ALU.pow).then_inc(rstd_ready.sem, 1)

            def pick(l, i, j):
                b = i * PAIR + j
                if l < 3:
                    last = emptied["A"]
                    k = INDEX[l]["T2", j]
                    pool.wait_ge(last.sem, last.before(l, i, ORDER[l][k]))
                    if l == 0:
                        nc.gpsimd.tensor_copy(maskCj[:, j, :], maskC[:, bass.ds(b, 1), :].rearrange("p o k -> p (o k)"))
                    nc.gpsimd.tensor_copy(cols[:, j, :], mods[:, l, :, bass.ds(b, 1)].rearrange("p c o -> p (c o)"))
                else:
                    pool.wait_ge(added.sem, added.before(l, i, j + 1))
                    nc.gpsimd.tensor_copy(anc[:, j, :], anchor[:, :, bass.ds(b, 1)].rearrange("p c o -> p (c o)"))
                    nc.gpsimd.tensor_copy(ranc[:, j:j + 1], ranchor[:, bass.ds(b, 1)])
                    nc.gpsimd.tensor_copy(kT[:, j, :, 0:SC], kcT[:, :, bass.ds(b * SC, SC)])
                src = ctxnT if l == 2 else ctxT
                nc.gpsimd.tensor_copy(cs[:, j, :, 0:SC], src[:, :, bass.ds(b * SC, SC)]).then_inc(picked.sem, 1)

            def add_bias(l, i, n, j):
                if not bias_event(l, n, j):
                    return
                pool.wait_ge(xh_ready.sem, xh_ready.of(l, i, 2 * n + j + 1))
                if n == min(BROW_AT[l]):
                    pool.wait_ge(gates_in[j].sem, gates_in[j].of(l, i, 16))
                x = X[:, bass.ds(i * PAIR + j, 1)].rearrange("p o t d -> p (o t) d")
                bias = brow[:, BROW_AT[l][n], :]
                if gated(l, n):
                    k = 1 + j + PAIR * [m for m in sorted(BROW_AT[l]) if gated(l, m)].index(n)
                    nc.gpsimd.tensor_tensor(gb, gates[:, j, n, :], bias, ALU.mult).then_inc(bias_gated.sem, 1)
                    pool.wait_ge(bias_gated.sem, bias_gated.of(l, i, k))
                    bias = gb
                hold(pool)
                nc.gpsimd.tensor_tensor(x, x, bias.unsqueeze(1).to_broadcast([P, QT, D]), ALU.add).then_inc(biased.sem, 1)
                pool.wait_ge(biased.sem, biased.of(l, i, bias_event(l, n, j)))

            def turn(l, i, more):
                for j in range(PAIR):
                    pick(l, i, j)
                for k in range(2, 2 * NLN[l]):
                    if k % 2 == 0:
                        for j in range(PAIR):
                            add_bias(l, i, k // 2 - 1, j)
                    inverse(l, i, k)
                if l < 3:
                    for j in range(PAIR):
                        add_bias(l, i, 2, j)
                if more:
                    for k in range(PAIR):
                        inverse(l, i + 1, k)

            for l in range(4):
                for k in range(PAIR):
                    inverse(l, 0, k)
                pool.wait_ge(s_pre_empty, KEYS_IN[l] + (l == 3))
                if l == 3:
                    pool.wait_ge(s_anchor, 1)
                else:
                    pool.wait_ge(s_brow, sum(BROW_N[:l + 1]))
                with pool.Fori(0, TURNS - 1) as i:
                    turn(l, i, True)
                turn(l, TURNS - 1, False)
                if l < 3:
                    layer_done(pool, l + 1)

        @block.tensor
        def _(pe):
            s_held[pe] = sem("tensor_held")
            uses = [0]

            def pre_bank():
                u = uses[0]
                uses[0] += 1
                if 1 <= u - 2 <= ROWS_IN[2]:
                    pe.wait_ge(s_rows, u - 2)
                elif u >= 2:
                    pe.wait_ge(s_pre_empty, max(1, u - 1 - ROWS_IN[2]))
                return pj[u % 2]

            def mm(dst, pairs):
                for n, (x, y) in enumerate(pairs):
                    last = nc.tensor.matmul(dst, x, y, start=(n == 0), stop=(n == len(pairs) - 1))
                return last

            pe.wait_ge(s_cond, 16)
            pe.wait_ge(s_const, 2)
            b_ = pre_bank()
            for c in range(CT):
                nc.tensor.transpose(b_[:, c * B:(c + 1) * B], crow[:, c * P:(c + 1) * P], ident[0:B, 0:B])
            pe.wait_ge(s_pre_act, 1)
            for c in range(CT):
                last = nc.tensor.transpose(b_[:, (2 + c) * B:(3 + c) * B], srow[:, c * P:(c + 1) * P], ident[0:B, 0:B])
            last.then_inc(s_pre_full, 1)
            pe.wait_ge(s_pre_empty, 1)
            for l in range(3):
                pe.wait_ge(s_ada[l], 16)
                cc = cT if l == 0 else scT
                for n in range(0, ADA_N[l], 512):
                    w = min(512, ADA_N[l] - n)
                    b_ = pre_bank()
                    mm(b_[0:B, 0:w], [(cc[:, k, :], WA[str(l)][:, k, n:n + w]) for k in range(CT)]).then_inc(s_pre_full, 1)
            pe.wait_ge(s_in, 16 * PRE_LOADS)
            b_ = pre_bank()
            nc.tensor.transpose(b_[:, 0:NROW], hT[0:NROW, 0, 0, 0:P], ident[0:NROW, 0:NROW]).then_inc(s_pre_full, 1)
            for l in range(3):
                pe.wait_ge(s_rows, ROWS_IN[l])
                b_ = pre_bank()
                rows = mod_rows(KM, l)
                at = 0
                for m in MOD[l]:
                    if m is None:
                        continue
                    for chunk in m[0:2]:
                        for c in range(CT):
                            last = nc.tensor.transpose(b_[:, at:at + B], rows[:, chunk * D + c * P:chunk * D + (c + 1) * P], ident[0:B, 0:B])
                            at += B
                last.then_inc(s_pre_full, 1)
            for norm in range(2):
                ctx_tok = stage[0:SC, 0:B * D].rearrange("p (b d) -> p b d", b=B)
                if norm:
                    pe.wait_ge(s_pre_dve, PRE_DVE_CTX)
                for b0 in range(0, B, 3):
                    b_ = pre_bank()
                    for b in range(b0, min(b0 + 3, B)):
                        for c in range(CT):
                            at = (c * 3 + b - b0) * SC
                            last = nc.tensor.transpose(b_[:, at:at + SC], ctx_tok[:, b, c * P:(c + 1) * P], ident[0:SC, 0:SC])
                    last.then_inc(s_pre_full, 1)
            pe.drain().then_inc(s_phase, 1)
            pe.wait_ge(s_phase, 5)

            def context_keys(l):
                src = ctxnT if l == 2 else ctxT
                for c in range(CT):
                    for n in range(0, B * SC, 512):
                        w = min(512, B * SC - n)
                        b_ = pre_bank()
                        mm(b_[:, 0:w], [(W[l]["ck"][:, k, c * P:(c + 1) * P], src[:, k, n:n + w]) for k in range(CT)]).then_inc(s_pre_full, 1)

            def to_channels(l, i, j, n):
                pe.wait_ge(xh_ready.sem, xh_ready.of(l, i, 2 * n + j + 1))
                b_ = wait_free(pe, l, i, f"T{n}", j)
                for t in range(QT):
                    for c in range(CT):
                        last = nc.tensor.transpose(b_[:, c * S + t * P:c * S + (t + 1) * P], xh[:, j, t, c * P:(c + 1) * P], ident[:, :])
                last.then_inc(full.sem, 1)

            def channels_out(l, i, name, j, w, at, rhs, *needs, ks=CT):
                b_ = wait_free(pe, l, i, name, j, *needs)
                for c in range(2):
                    last = mm(b_[:, c * S:(c + 1) * S], [(w[:, k, at + c * P:at + (c + 1) * P], rhs(k)) for k in range(ks)])
                last.then_inc(full.sem, 1)

            def tokens_out(l, i, name, j, w, at, lhs, *needs, ks=CT, late=None):
                b_ = wait_free(pe, l, i, name, j, *needs)
                for t in range(QT):
                    for k in range(ks):
                        if late and t == 0 and k == ks - 2:
                            wait_taken(pe, l, i, late, j)
                        last = nc.tensor.matmul(b_[:, t * D:(t + 1) * D], lhs(k)[:, t * P:(t + 1) * P], w[:, k, at:at + D], start=(k == 0), stop=(k == ks - 1))
                last.then_inc(full.sem, 1)

            def use(l, i, name, j):
                w = W[l]
                x = lambda k: hT[:, j, k, :]
                o = lambda k: oT[:, j, k, :]
                if name in ("DS", "DC"):
                    pe.wait_ge(spread.sem, spread.of(l, i, 2 * (name == "DC") + j + 1))
                    b_ = wait_free(pe, l, i, name, j)
                    for t in range(QT):
                        for c in range(CT):
                            last = nc.tensor.transpose(b_[:, c * S + t * P:c * S + (t + 1) * P], rden[:, t * D + c * P:t * D + (c + 1) * P], ident[:, :])
                    last.then_inc(full.sem, 1)
                elif name == "VC":
                    pe.wait_ge(picked.sem, picked.of(l, i, j + 1))
                    b_ = wait_free(pe, l, i, "VC", j)
                    mm(b_[0:SCP, 0:D], [(cs[:, j, k, :], w["cv"][:, k, :]) for k in range(CT)]).then_inc(full.sem, 1)
                elif name in ("O", "OC"):
                    cross = name == "OC"
                    pe.wait_ge(normed.sem, normed.of(l, i, 2 * cross + j + 1))
                    tokens_out(l, i, name, j, w["co" if cross else "so"], 0, o)
                elif name in ("T1", "T2"):
                    to_channels(l, i, j, int(name[1]))
                elif name == "QC":
                    channels_out(l, i, "QC", j, w["cq"], 0, x, "T1")
                elif name == "MO":
                    hid = hidden(j, l)
                    last = HT_N - 1 if l == 1 else HT_N // 2 - 1
                    tokens_out(l, i, "MO", j, w["m2"], 0, lambda k: hid[:, k, :], f"M{last - (2 if l == 1 else 1)}", ks=HT_N, late=f"M{last}")
                elif l == 1:
                    m = int(name[1:])
                    b_ = wait_free(pe, l, i, name, j, "T2")
                    for half in range(2):
                        at = half * HID + m * P
                        last = mm(b_[:, half * S:(half + 1) * S], [(w["m1"][:, k, at:at + P], x(k)) for k in range(CT)])
                    last.then_inc(full.sem, 1)
                else:
                    channels_out(l, i, name, j, w["m1"], 2 * int(name[1:]) * P, x, "T2")

            def attentions(l, i):
                e = ends(l)
                for step in range(NG[l] + SUM_LAG):
                    if step < NG[l]:
                        n = step
                        cross, j, qt, h0, hg, kts, width, kp_ = parts(l, n)
                        if n in (0, *e):
                            if l == 0 and not cross:
                                pe.wait_ge(rope_ready.sem, rope_ready.of(l, i, 2 * j + 2))
                            else:
                                wait_taken(pe, l, i, "QC" if cross else "Q", j)
                            pe.wait_ge(keys_in[j].sem, keys_in[j].of(l, i, 256 if cross else 128))
                        wait_group(pe, exped, l, i, n - 3 if n >= 3 else -1)
                        c, k0 = h0 // HPT, qt * P if kts == 1 and not cross else 0
                        nc.tensor.matmul(ps[n % 3][:, 0:hg * width].rearrange("p (h k) -> p h k", h=hg), qT[:, j, c, qt * P:(qt + 1) * P],
                                         KM[:, j, c, h0 % HPT:h0 % HPT + hg, k0:k0 + width], start=True, stop=True).then_inc(scored.sem, 1)
                    if 0 <= step - TURN_LAG < NG[l]:
                        n = step - TURN_LAG
                        cross, j, qt, h0, hg, kts, width, kp_ = parts(l, n)
                        if l == 1 and cross:
                            pe.wait_ge(chosen.sem, chosen.of(l, i, n - NSELF[l] + 1))
                        else:
                            wait_group(pe, exped, l, i, n)
                        wait_copied(pe, l, i, n - 2)
                        for x in range(hg):
                            for k in range(kts):
                                at = (x * kts + k) * P
                                keys_ = SC if cross else P
                                last = nc.tensor.transpose(pt[n % 2][0:keys_, at:at + P], probs[:, n % 4, x * width + k * P:x * width + k * P + keys_], ident[:, :])
                        last.then_inc(turned.sem, 1)
                    if 0 <= step - SUM_LAG < NG[l]:
                        n = step - SUM_LAG
                        cross, j, qt, h0, hg, kts, width, kp_ = parts(l, n)
                        if n in (0, *e):
                            k = 2 * cross + j
                            if k:
                                pe.wait_ge(normed.sem, normed.of(l, i, k))
                            else:
                                pe.wait_ge(normed.sem, normed.before(l, i, 4))
                            wait_taken(pe, l, i, "VC" if cross else "V0", j)
                        wait_copied(pe, l, i, n)
                        for x in range(0, hg, 2):
                            h = h0 + x
                            quad, c = h % HPT // 2, h // HPT
                            at = slice(c * S + qt * P, c * S + (qt + 1) * P)
                            for u in range(2):
                                for k in range(kts):
                                    kt = qt if (kts == 1 and not cross) else k
                                    col = ((x + u) * kts + k) * P
                                    last = nc.tensor.matmul(po[32 * quad:32 * quad + 32, at], VP[0:kp_, j, kt, h // 2, u, :], probsT[0:kp_, n % 4, col:col + P],
                                                            start=(u == 0 and k == 0), stop=(u == 1 and k == kts - 1))
                        last.then_inc(summed.sem, 1)
                    for name, j in between(l).get(step, ()):
                        use(l, i, name, j)

            for l in range(3):
                w = W[l]
                pe.wait_ge(s_w[l], LOADED[l])
                context_keys(l)
                pe.wait_ge(s_pre_empty, KEYS_IN[l])
                with pe.Fori(0, TURNS) as i:
                    for j in range(PAIR):
                        to_channels(l, i, j, 0)
                    for j in range(PAIR):
                        x = lambda k: hT[:, j, k, :]
                        channels_out(l, i, "K", j, w["qkv"], D, x, "T0")
                        channels_out(l, i, "Q", j, w["qkv"], 0, x)
                        tokens_out(l, i, "V0", j, w["qkv"], 2 * D, x)
                    attentions(l, i)
                    for name, j in tail(l):
                        use(l, i, name, j)
                layer_done(pe, l + 1)

            l, w = 3, W[3]
            pe.wait_ge(s_w[3], LOADED[3])
            context_keys(3)
            pe.wait_ge(s_w3, 16 * 7)
            b_ = pre_bank()
            for m in range(M3):
                for k in range(CT):
                    lhs = W3["e1a"][:, m // 4, k, m % 4 * P:(m % 4 + 1) * P] if m < 4 * E_N else W3["g1a"][:, k, (m - 4 * E_N) * P:(m - 4 * E_N + 1) * P]
                    last = nc.tensor.matmul(b_[:, m * B:(m + 1) * B], lhs, cT[:, k, :], start=(k == 0), stop=(k == CT - 1))
            mm(b_[0:E_N, M3 * B:(M3 + 1) * B], [(W3["ra"][:, k, :], cT[:, k, :]) for k in range(CT)]).then_inc(s_pre_full, 1)
            pe.wait_ge(s_pre_empty, KEYS_IN[3] + 1)
            with pe.Fori(0, TURNS) as i:
                for j in range(PAIR):
                    to_channels(l, i, j, 0)
                for j in range(PAIR):
                    channels_out(l, i, "Q", j, w["wq"], 0, lambda k: hT[:, j, k, :], "T0")
                for j in range(PAIR):
                    pe.wait_ge(picked.sem, picked.of(l, i, j + 1))
                    b_ = wait_free(pe, l, i, "VC", j)
                    mm(b_[0:SCP, 0:D], [(cs[:, j, k, :], w["cv"][:, k, :]) for k in range(CT)]).then_inc(full.sem, 1)
                for j in range(PAIR):
                    b_ = wait_free(pe, l, i, "S", j, "Q")
                    for t in range(QT):
                        last = mm(b_[:, t * SC:(t + 1) * SC], [(qT[:, j, k, t * P:(t + 1) * P], kT[:, j, k, 0:SC]) for k in range(CT)])
                    last.then_inc(full.sem, 1)
                for j in range(PAIR):
                    pe.wait_ge(dve3.sem, dve3.of(l, i, 3 + j))
                    b_ = wait_free(pe, l, i, "PT", j)
                    for t in range(QT):
                        last = nc.tensor.transpose(b_[0:SC, t * P:(t + 1) * P], probs[:, j, t * SC:(t + 1) * SC], ident[:, :])
                    last.then_inc(full.sem, 1)
                for j in range(PAIR):
                    b_ = wait_free(pe, l, i, "EV", j, "PT", "VC")
                    for c in range(CT):
                        last = nc.tensor.matmul(b_[:, c * S:(c + 1) * S], V3(VP, j)[:, c * P:(c + 1) * P], probsT[0:SCP, j, 0:S], start=True, stop=True)
                    last.then_inc(full.sem, 1)
                comb = lambda j: (lambda k: hT[:, j, k, :] if k < CT else qT[:, j, k - CT, :])
                for j in range(PAIR):
                    b_ = wait_free(pe, l, i, "RL", j, "EV")
                    mm(b_[0:E_N, 0:S], [(W3["r"][:, k, :], comb(j)(k)) for k in range(4)]).then_inc(full.sem, 1)
                for j in range(PAIR):
                    b_ = wait_free(pe, l, i, "RT", j, "RL")
                    hold(pe)
                    for t in range(QT):
                        last = nc.tensor.transpose(b_[:, t * E_N:(t + 1) * E_N], logT[:, j, t * P:(t + 1) * P], ident[0:E_N, 0:E_N])
                    last.then_inc(full.sem, 1)
                for j in range(PAIR):
                    for m in range(M3 // 2):
                        ws, at = (w["e1"][:, m // 2], m % 2 * 2 * P) if m < 2 * E_N else (w["g1"], 0)
                        channels_out(l, i, f"M{m}", j, ws, at, comb(j), ks=4)
                for j in range(PAIR):
                    hid = hidden(j, l)
                    for e in range(E_N):
                        tokens_out(l, i, f"E{e}", j, w["e2"][:, e], 0, lambda k: hid[:, 4 * e + k, :], f"M{M3 // 2 - 1}", ks=4)
                for j in range(PAIR):
                    hid = hidden(j, l)
                    tokens_out(l, i, "GO", j, w["g2"], 0, lambda k: hid[:, 4 * E_N + k, :])
                for j in range(PAIR):
                    b_ = wait_free(pe, l, i, "RR", j, f"E{E_N - 1}")
                    for t in range(QT):
                        for c in range(CT):
                            last = nc.tensor.transpose(b_[:, c * S + t * P:c * S + (t + 1) * P], xh[:, j, t, c * P:(c + 1) * P], ident[:, :])
                    last.then_inc(full.sem, 1)
                for j in range(PAIR):
                    tokens_out(l, i, "OUT", j, W3["out"], 0, lambda k: hT[:, j, k, :], "RR")

        @block.scalar
        def _(act):
            uses = [0]

            def pre_bank():
                u = uses[0]
                uses[0] += 1
                act.wait_ge(s_pre_full, u + 1)
                return pj[u % 2]

            ident_ = lambda o, x, **kw: nc.scalar.activation(o, x, ACT.Identity, **kw)
            copy_ = lambda o, x: nc.scalar.activation(o, x, ACT.Copy)
            act.wait_ge(s_cond, 16)
            nc.scalar.activation(srow, crow, ACT.Silu).then_inc(s_pre_act, 1)
            b_ = pre_bank()
            copy_(cT[:, :, :].rearrange("p c b -> p (c b)"), b_[:, 0:CT * B])
            copy_(scT[:, :, :].rearrange("p c b -> p (c b)"), b_[:, CT * B:2 * CT * B]).then_inc(s_pre_empty, 1)
            uses[0] += sum(NPRE)
            b_ = pre_bank()
            for n, c in enumerate((VC(1, "b_qkv"), VC(1, "b_q"), VC(2, "b_qkv"), VC(2, "b_qc"))):
                nc.scalar.activation(bq[:, n // 2, n % 2 * 2:n % 2 * 2 + 2], b_[:, c:c + 2], ACT.Copy, scale=SCALE)
            copy_(vec[:, :], b_[:, 0:NROW]).then_inc(s_pre_empty, 1)
            act.wait_ge(s_pre_empty, 2)
            for l in range(3):
                b_ = pre_bank()
                at = 0
                for n, m in enumerate(MOD[l]):
                    if m is None:
                        continue
                    for what in range(2):
                        o = mods[:, l, 4 * n + 2 * what:4 * n + 2 * what + 2, :]
                        src = b_[:, at:at + CT * B].rearrange("p (c b) -> p c b", c=CT)
                        if what == 0:
                            last = copy_(o, src)
                        elif l > 0:
                            last = ident_(o, src, bias=1.0)
                        else:
                            for c in range(CT):
                                wc = vec[:, 2 * n + c:2 * n + c + 1]
                                last = ident_(o[:, c, :], src[:, c, :], bias=wc, scale=wc)
                        at += CT * B
                last.then_inc(s_pre_empty, 1)
            for dst in (ctxT, ctxnT):
                for b0 in range(0, B, 3):
                    nb = min(3, B - b0)
                    b_ = pre_bank()
                    for c in range(CT):
                        last = copy_(dst[:, c, b0 * SC:(b0 + nb) * SC], b_[:, c * 3 * SC:(c * 3 + nb) * SC])
                    last.then_inc(s_pre_empty, 1)
            act.drain().then_inc(s_phase, 1)
            act.wait_ge(s_phase, 5)

            def context_keys(l):
                for c in range(CT):
                    for n in range(0, B * SC, 512):
                        w = min(512, B * SC - n)
                        b_ = pre_bank()
                        o = kcT[:, c, n:n + w]
                        if l in BKC:
                            last = ident_(o, b_[:, 0:w], bias=vec[:, BKC[l] + c:BKC[l] + c + 1])
                        else:
                            last = copy_(o, b_[:, 0:w])
                        last.then_inc(s_pre_empty, 1)

            def channels(l, i, j, n):
                wait_full(act, l, i, f"T{n}", j)
                b_ = bank_of(l, f"T{n}", j)
                for c in range(CT):
                    if l == 3:
                        sc, bi = vec[:, VC(3, "ln_gamma") + c:][:, 0:1], vec[:, VC(3, "ln_beta") + c:][:, 0:1]
                    else:
                        sc, bi = cols[:, j, 4 * n + 2 + c:4 * n + 3 + c], cols[:, j, 4 * n + c:4 * n + c + 1]
                    if l == 2 and n == 1:
                        last = copy_(hT[:, j, c, :], b_[:, c * S:(c + 1) * S])
                    elif l == 1 and n == 0:
                        ident_(hT[:, j, c, 0:S - SHIFT], b_[:, c * S + SHIFT:(c + 1) * S], bias=bi, scale=sc)
                        last = ident_(hT[:, j, c, S - SHIFT:S], b_[:, c * S:c * S + SHIFT], bias=bi, scale=sc)
                    else:
                        last = ident_(hT[:, j, c, :], b_[:, c * S:(c + 1) * S], bias=bi, scale=sc)
                last.then_inc(emptied["A"].sem, 1)

            def queries(l, i, j, cross):
                name = "QC" if cross else "Q"
                wait_full(act, l, i, name, j)
                b_ = bank_of(l, name, j)
                scale = SCALE3 if l == 3 else SCALE
                if l in (1, 2):
                    for c in range(CT):
                        bias = bq[:, l - 1, 2 * cross + c:2 * cross + c + 1]
                        last = ident_(qT[:, j, c, :], b_[:, c * S:(c + 1) * S], bias=bias, scale=scale)
                else:
                    last = nc.scalar.activation(qT[:, j].rearrange("p c s -> p (c s)"), b_[:, :], ACT.Copy, scale=scale)
                last.then_inc(emptied["A"].sem, 1)

            def use(l, i, name, j):
                if name in ("DS", "DC"):
                    wait_full(act, l, i, name, j)
                    copy_(rden[:, :], bank_of(l, name, j)[:, :]).then_inc(emptied["A"].sem, 1)
                elif name == "VC":
                    values(l, i, j)
                elif name in ("T1", "T2"):
                    channels(l, i, j, int(name[1]))
                elif name == "QC":
                    queries(l, i, j, 1)
                elif name[0] == "M" and name != "MO":
                    hid, m = hidden(j, l), int(name[1:])
                    wait_full(act, l, i, name, j)
                    b_ = bank_of(l, name, j)
                    if l == 1:
                        nc.scalar.activation(hid[:, m, :], b_[:, 0:S], ACT.Silu, bias=vec[:, B1[l] + m:B1[l] + m + 1]).then_inc(silu_done.sem, 1)
                    else:
                        for x in range(2):
                            k = 2 * m + x
                            last = nc.scalar.activation(hid[:, k, :], b_[:, x * S:(x + 1) * S], ACT.Gelu_apprx_tanh, bias=vec[:, B1[l] + k:B1[l] + k + 1])
                        last.then_inc(emptied["A"].sem, 1)

            def attentions(l, i):
                for step in range(NG[l] + SUM_LAG):
                    if 0 <= step - TURN_LAG < NG[l] and not by_vector(l, step - TURN_LAG):
                        n = step - TURN_LAG
                        kp_ = parts(l, n)[-1]
                        wait_group(act, turned, l, i, n)
                        wait_group(act, summed, l, i, n - 4)
                        copy_(probsT[0:kp_, n % 4, :], pt[n % 2][0:kp_, :]).then_inc(copied[0].sem, 1)
                    if step < NG[l]:
                        n = step
                        cross, j, qt, h0, hg, kts, width, kp_ = parts(l, n)
                        wait_group(act, maxed, l, i, n)
                        wait_group(act, turned, l, i, n - 4)
                        keys_ = SC if cross else width
                        for x in range(hg):
                            acc = {} if l == 1 and cross else {"accum_out": sums[:, j, qt, h0 + x:h0 + x + 1]}
                            last = nc.scalar.activation(probs[:, n % 4, x * width:x * width + keys_], ps[n % 3][:, x * width:x * width + keys_],
                                                        ACT.Exp, bias=nmax[:, n % 4, x:x + 1], **acc)
                        last.then_inc(exped.sem, 1)
                        if n == NG[l] - 1:
                            nc.scalar.activation(warm[:, 1:2], warm[:, 0:1], ACT.Silu if l == 1 else ACT.Gelu_apprx_tanh)
                    for name, j in between(l).get(step, ()):
                        use(l, i, name, j)

            def values(l, i, j):
                wait_full(act, l, i, "VC", j)
                b_ = bank_of(l, "VC", j)
                if l == 3:
                    last = copy_(V3(VP, j), b_[0:SCP, 0:D])
                else:
                    last = copy_(padded(VP, j, 0, SCP), b_[0:SCP, 0:D].rearrange("p (h e d) -> p h e d", e=2, d=HD))
                last.then_inc(emptied["A"].sem, 1)

            for l in range(3):
                context_keys(l)
                with act.Fori(0, TURNS) as i:
                    for j in range(PAIR):
                        act.wait_ge(picked.sem, picked.of(l, i, j + 1))
                        channels(l, i, j, 0)
                    for j in range(PAIR):
                        if l == 0:
                            wait_full(act, l, i, "K", j)
                            act.wait_ge(added.sem, added.before(l, i, 5 + j))
                            copy_(kT[:, j].rearrange("p c s -> p (c s)"), bank_of(l, "K", j)[:, :]).then_inc(emptied["A"].sem, 1)
                        queries(l, i, j, 0)
                    attentions(l, i)
                    for name, j in tail(l):
                        use(l, i, name, j)
                    nc.scalar.activation(warm[:, 1:2], warm[:, 0:1], ACT.Exp)
                layer_done(act, l + 1)

            l = 3
            context_keys(3)
            b_ = pre_bank()
            copy_(anchor[:, :, :].rearrange("p m b -> p (m b)"), b_[:, 0:M3 * B])
            nc.scalar.activation(ranchor[:, 0:B], b_[0:E_N, M3 * B:(M3 + 1) * B], ACT.Identity, bias=rb[:, 0:1]).then_inc(s_pre_empty, 1)
            with act.Fori(0, TURNS) as i:
                for j in range(PAIR):
                    channels(l, i, j, 0)
                for j in range(PAIR):
                    queries(l, i, j, 0)
                for j in range(PAIR):
                    values(l, i, j)
                for j in range(PAIR):
                    act.wait_ge(dve3.sem, dve3.of(l, i, 1 + j))
                    b_ = bank_of(l, "S", j)
                    for t in range(QT):
                        last = nc.scalar.activation(probs[:, j, t * SC:(t + 1) * SC], b_[:, t * SC:(t + 1) * SC], ACT.Exp,
                                                    bias=nmax[:, j, t:t + 1], accum_out=small[:, j, t, 0:1])
                    last.then_inc(emptied["A"].sem, 1)
                for j in range(PAIR):
                    wait_full(act, l, i, "PT", j)
                    copy_(probsT[0:SCP, j, 0:S], bank_of(l, "PT", j)[0:SCP, 0:S]).then_inc(emptied["A"].sem, 1)
                for j in range(PAIR):
                    wait_full(act, l, i, "EV", j)
                    copy_(qT[:, j].rearrange("p c s -> p (c s)"), bank_of(l, "EV", j)[:, :]).then_inc(emptied["A"].sem, 1)
                for j in range(PAIR):
                    act.wait_ge(picked.sem, picked.of(l, i, j + 1))
                    wait_full(act, l, i, "RL", j)
                    ident_(logT[:, j, :], bank_of(l, "RL", j)[0:E_N, 0:S], bias=ranc[:, j:j + 1]).then_inc(emptied["A"].sem, 1)
                for j in range(PAIR):
                    wait_taken(act, l, i, "RT", j)
                    for t in range(QT):
                        last = nc.scalar.activation(rp[:, j, t, :], rp[:, j, t, :], ACT.Exp, accum_out=small[:, j, t, 1:2])
                    last.then_inc(act3.sem, 1)
                for j in range(PAIR):
                    hid = hidden(j, l)
                    for m in range(M3 // 2):
                        wait_full(act, l, i, f"M{m}", j)
                        b_ = bank_of(l, f"M{m}", j)
                        for x in range(2):
                            k = 2 * m + x
                            last = nc.scalar.activation(hid[:, k, :], b_[:, x * S:(x + 1) * S], ACT.Silu, bias=anc[:, j, k:k + 1])
                        last.then_inc(emptied["A"].sem, 1)
                for j in range(PAIR):
                    wait_taken(act, l, i, "GO", j)
                    g = kT[:, j].rearrange("p c s -> p (c s)")
                    nc.scalar.activation(g, g, ACT.Tanh, scale=0.5).then_inc(act3.sem, 1)
                for j in range(PAIR):
                    wait_full(act, l, i, "RR", j)
                    copy_(hT[:, j].rearrange("p c s -> p (c s)"), bank_of(l, "RR", j)[:, :]).then_inc(emptied["A"].sem, 1)

        @block.vector
        def _(dve):
            s_held[dve] = sem("vector_held")
            links = [0]
            where = [None, None]

            def link(ins):
                links[0] += 1
                ins.then_inc(dve_own.sem, 1)

            def settle(upto=None):
                l, i = where
                dve.wait_ge(dve_own.sem, dve_own.of(l, i, links[0] if upto is None else upto))

            uses = [1]
            pre = [0]

            def pre_link(ins, wait=True):
                pre[0] += 1
                ins.then_inc(s_pre_dve, 1)
                if wait:
                    dve.wait_ge(s_pre_dve, pre[0])

            def add_biases(l):
                for n in range(0, ADA_N[l], 512):
                    w = min(512, ADA_N[l] - n)
                    dve.wait_ge(s_pre_full, uses[0] + 1)
                    b_ = pj[uses[0] % 2]
                    uses[0] += 1
                    r = mod_rows(KM, l)[:, n:n + w]
                    nc.vector.tensor_tensor(r, b_[0:B, 0:w], r, ALU.add).then_inc(s_rows, 1)

            dve.wait_ge(s_bias, 16 * 3)
            add_biases(0)
            dve.wait_ge(s_in, 16 * PRE_LOADS)
            ctx_tok = stage[0:SC, 0:B * D].rearrange("p (b d) -> p b d", b=B)
            st = rden[0:SC, 32:32 + 6 * B].rearrange("p (b s) -> p b s", b=B)
            mvc = rden[0:SC, 128:128 + 2 * B].rearrange("p (b s) -> p b s", b=B)
            for b in range(B):
                pre_link(nc.vector.bn_stats(st[:, b, :], ctx_tok[:, b, :]), b == B - 1)
            for b in range(B):
                pre_link(nc.vector.bn_aggr(mvc[:, b, :], st[:, b, :]), b == B - 1)
            pre_link(nc.vector.tensor_scalar(rden[0:SC, 8:16], mvc[:, :, 1], EPS[2], None, ALU.add))
            assert pre[0] == PRE_DVE_VAR, pre[0]
            for m, mb in ((maskS, maskSb), (maskC, maskCb)):
                pre_link(nc.vector.tensor_copy(m[:, :, :], mb[:, :, :]))
                pre_link(nc.vector.tensor_scalar(m[:, :, :], m[:, :, :], 1.0, -NEG, ALU.subtract, ALU.mult))
            add_biases(1)
            add_biases(2)
            dve.wait_ge(s_pre_full, PRE_RAW)
            dve.wait_ge(s_pre_pool, 5)
            for b in range(B):
                pre_link(nc.vector.tensor_scalar(ctx_tok[:, b, :], ctx_tok[:, b, :], mvc[:, b, 0:1], rden[0:SC, 16 + b:17 + b], ALU.subtract, ALU.mult), False)
            assert pre[0] == PRE_DVE_CTX, pre[0]
            dve.drain().then_inc(s_phase, 1)
            dve.wait_ge(s_phase, 5)

            def statistics(l, i, j, n):
                b = i * PAIR + j
                hold(dve)
                for t in range(QT):
                    link(nc.vector.bn_stats(stats[:, j, t, :], X[:, bass.ds(b, 1), t, :].rearrange("p o d -> p (o d)")))
                settle()
                hold(dve)
                for t in range(QT):
                    link(nc.vector.bn_aggr(mv[:, j, t, :], stats[:, j, t, :]))
                settle()
                nc.vector.tensor_scalar(ve[:, j, :], mv[:, j, :, 1], EPS[l], None, ALU.add).then_inc(var_ready.sem, 1)

            def normalise(l, i, j, n):
                b = i * PAIR + j
                dve.wait_ge(rstd_ready.sem, rstd_ready.of(l, i, 2 * n + j + 1))
                for t in range(QT):
                    last = nc.vector.tensor_scalar(xh[:, j, t, :], X[:, bass.ds(b, 1), t, :].rearrange("p o d -> p (o d)"),
                                                   mv[:, j, t, 0:1], rstd[:, j, t:t + 1], ALU.subtract, ALU.mult)
                last.then_inc(xh_ready.sem, 1)

            def residual(l, i, j, n, name):
                b = i * PAIR + j
                wait_full(dve, l, i, name, j)
                b_ = bank_of(l, name, j)[:, :].rearrange("p (t d) -> p t d", t=QT)
                x = X[:, bass.ds(b, 1)].rearrange("p o t d -> p (o t) d")
                k = bias_event(l, n, j)
                if n == 0:
                    dve.wait_ge(gates_in[j].sem, gates_in[j].of(l, i, 16))
                if gated(l, n):
                    u = kT[:, j].rearrange("p c s -> p (c s)").rearrange("p (t d) -> p t d", t=QT)
                    g = gates[:, j, n, :].unsqueeze(1).to_broadcast([P, QT, D])
                    nc.vector.tensor_tensor(u, b_, g, ALU.mult).then_inc(emptied["V"].sem, 1)
                    wait_taken(dve, l, i, name, j)
                    if k:
                        dve.wait_ge(biased.sem, biased.of(l, i, k))
                    nc.vector.tensor_tensor(x, x, u, ALU.add).then_inc(added.sem, 1)
                    dve.wait_ge(added.sem, added.of(l, i, 2 * n + j + 1))
                else:
                    dve.wait_ge(biased.sem, biased.of(l, i, k))
                    nc.vector.tensor_tensor(x, x, b_, ALU.add).then_inc(emptied["V"].sem, 1)
                    wait_taken(dve, l, i, name, j)
                    dve.sem_inc(added.sem, 1)

            def rope(l, i, j, name, part):
                x = name == "Q"
                r = (qT if x else kT)[:, j].rearrange("p c s -> p (c s)")
                swap = hT[:, 1].rearrange("p c s -> p (c s)") if j else stage[:, x * 512:(x + 1) * 512]
                n = 512 // P
                c, s = (m[:, :].unsqueeze(1).to_broadcast([P, n, P]) for m in (cosT, sinT))
                rv, wv = (m.rearrange("p (n w) -> p n w", w=P) for m in (r, swap))
                if part == 0:
                    wait_taken(dve, l, i, name, j)
                    settle()
                    if x:
                        dve.wait_ge(rope_ready.sem, rope_ready.of(l, i, 2 * j + 1))
                    hold(dve)
                    link(nc.vector.stream_shuffle(swap, r, [p ^ (HD // 2) for p in range(32)]))
                elif part == 1:
                    settle()
                    link(nc.vector.tensor_tensor(rv, rv, c, ALU.mult))
                    link(nc.vector.tensor_tensor(wv, wv, s, ALU.mult))
                else:
                    settle()
                    nc.vector.tensor_tensor(r, r, swap, ALU.add).then_inc(rope_ready.sem, 1)

            def keys(l, i, j):
                wait_full(dve, l, i, "K", j)
                b_ = bank_of(l, "K", j)
                for c in range(CT):
                    last = nc.vector.tensor_scalar(kT[:, j, c, :], b_[:, c * S:(c + 1) * S], vec[:, BK[l] + c:BK[l] + c + 1], None, ALU.add)
                last.then_inc(emptied["V"].sem, 1)

            def values(l, i, j):
                wait_full(dve, l, i, "V0", j)
                b_ = bank_of(l, "V0", j)
                for t in range(QT):
                    last = nc.vector.tensor_copy(padded(VP, j, t, P), b_[:, t * D:(t + 1) * D].rearrange("p (h e d) -> p h e d", e=2, d=HD))
                last.then_inc(emptied["V"].sem, 1)

            def spread_sums(l, i, j, cross):
                wait_group(dve, exped, l, i, ends(l)[2 * cross + j] - 1)
                if l == 1 and cross:
                    dve.wait_ge(chosen.sem, chosen.of(l, i, ends(l)[2 + j] - NSELF[l]))
                link(nc.vector.reciprocal(rsum[:, :, :], sums[:, j, :, :]))
                settle()
                o = rden[:, :].rearrange("p (t h d) -> p t h d", t=QT, h=H)
                nc.vector.tensor_copy(o, rsum[:, :, :].unsqueeze(3).to_broadcast([P, QT, H, HD])).then_inc(spread.sem, 1)

            def heads_out(l, i, j, cross):
                wait_group(dve, summed, l, i, ends(l)[2 * cross + j] - 1)
                o = oT[:, j].rearrange("p c s -> p (c s)")
                bias = BV.get((l, cross))
                wait_taken(dve, l, i, "DC" if cross else "DS", j)
                if l == 1 and not cross:
                    ov = o.rearrange("p (c s) -> p c s", c=CT)
                    pv = po[:, :].rearrange("p (c s) -> p c s", c=CT)
                    rv = rden[:, :].rearrange("p (c s) -> p c s", c=CT)
                    link(nc.vector.tensor_tensor(ov[:, :, SHIFT:S], pv[:, :, 0:S - SHIFT], rv[:, :, 0:S - SHIFT], ALU.mult))
                    last = nc.vector.tensor_tensor(ov[:, :, 0:SHIFT], pv[:, :, S - SHIFT:S], rv[:, :, S - SHIFT:S], ALU.mult)
                else:
                    last = nc.vector.tensor_tensor(o, po[:, :], rden[:, :], ALU.mult)
                if bias is None:
                    last.then_inc(normed.sem, 1)
                    return
                link(last)
                settle()
                for c in range(CT):
                    last = nc.vector.tensor_scalar(oT[:, j, c, :], oT[:, j, c, :], vec[:, bias + c:bias + c + 1], None, ALU.add)
                last.then_inc(normed.sem, 1)

            def maxima(l, i, n):
                cross, j, qt, h0, hg, kts, width, kp_ = parts(l, n)
                wait_group(dve, scored, l, i, n)
                wait_group(dve, exped, l, i, n - 4)
                sc = ps[n % 3][:, 0:hg * width].rearrange("p (h k) -> p h k", h=hg)
                if l == 0:
                    hold(dve)
                    for x in range(hg):
                        m = maskCj[:, j, :] if cross else maskS[:, qt, :]
                        link(nc.vector.tensor_tensor_reduce(sc[:, x, :], sc[:, x, :], m, 1.0, NEG, ALU.add, ALU.max, top1[:, n % 4, x:x + 1]))
                    settle()
                    nc.vector.tensor_scalar(nmax[:, n % 4, 0:hg], top1[:, n % 4, 0:hg], -1.0, None, ALU.mult).then_inc(maxed.sem, 1)
                else:
                    nc.vector.tensor_reduce(nmax[:, n % 4, 0:hg], sc, AX_X, ALU.max, negate=True).then_inc(maxed.sem, 1)

            def top_k(l, i, n):
                before = links[0]
                first, second = NSELF[l] <= n < NG[l], NSELF[l] <= n - 1 < NG[l]
                heads = range(CROSS[0])
                if first:
                    cross, j, qt, h0, hg, kts, width, kp_ = parts(l, n)
                    wait_group(dve, scored, l, i, n)
                    wait_group(dve, exped, l, i, n - 4)
                    sc = ps[n % 3][:, 0:hg * width].rearrange("p (h k) -> p h k", h=hg)
                    hold(dve)
                    for x in heads:
                        link(nc.vector.max(top1[:, x, :], sc[:, x, :]))
                    largest = links[0]
                if second:
                    settle(before)
                    hold(dve)
                    for x in heads:
                        link(nc.vector.max(top2[:, x, :], left[:, (n - 1) % 2, x, :]))
                    largest2 = links[0]
                if first:
                    settle(largest)
                    k = n - 2 - NSELF[l] + 1
                    dve.wait_ge(chosen.sem, chosen.of(l, i, k) if k > 0 else chosen.before(l, i, NCROSS + k))
                    hold(dve)
                    for x in heads:
                        link(nc.vector.match_replace(left[:, n % 2, x, :], top1[:, x, :], sc[:, x, :], TAKEN))
                    nc.vector.tensor_scalar(nmax[:, n % 4, 0:CROSS[0]], top1[:, :, 0], -1.0, None, ALU.mult).then_inc(maxed.sem, 1)
                if second:
                    settle(largest2)
                    hold(dve)
                    for x in heads:
                        link(nc.vector.match_replace(left[:, (n - 1) % 2, x, :], top2[:, x, :], left[:, (n - 1) % 2, x, :], TAKEN))
                    strike(l, i, n - 1)

            def strike(l, i, n):
                cross, j, qt, h0, hg, kts, width, kp_ = parts(l, n)
                wait_group(dve, exped, l, i, n)
                settle()
                p = probs[:, n % 4, 0:hg * width].rearrange("p (h k) -> p h k", h=hg)
                for x in range(hg):
                    last = nc.vector.scalar_tensor_tensor(p[:, x, :], left[:, n % 2, x, :], TAKEN, p[:, x, :], ALU.is_equal, ALU.mult,
                                                          accum_out=sums[:, j, qt, h0 + x:h0 + x + 1])
                last.then_inc(chosen.sem, 1)

            def attentions(l, i):
                e = ends(l)
                for step in range(NG[l] + SUM_LAG + 1):
                    if step - SUM_LAG in e:
                        k = e.index(step - SUM_LAG)
                        heads_out(l, i, k % 2, k // 2)
                    if l == 1 and step >= NSELF[l]:
                        top_k(l, i, step)
                    elif step < NG[l]:
                        maxima(l, i, step)
                    if 0 <= step - TURN_LAG < NG[l] and by_vector(l, step - TURN_LAG):
                        n = step - TURN_LAG
                        kp_ = parts(l, n)[-1]
                        wait_group(dve, turned, l, i, n)
                        wait_group(dve, summed, l, i, n - 4)
                        nc.vector.tensor_copy(probsT[0:kp_, n % 4, :], pt[n % 2][0:kp_, :]).then_inc(copied[1].sem, 1)
                    if l == 0 and 0 <= step - ROPE_AT < 6:
                        rope(l, i, 1, "KQ"[(step - ROPE_AT) // 3], (step - ROPE_AT) % 3)
                    if step in e:
                        k = e.index(step)
                        spread_sums(l, i, k % 2, k // 2)
                    for k in range(3):
                        n = k // 2
                        if step == e[k] + OUT_AT + RES_LAG:
                            residual(l, i, k % 2, n, "OC" if n else "O")
                        if step == e[k] + OUT_AT + STAT_LAG:
                            statistics(l, i, k % 2, n + 1)
                        if step == e[k] + OUT_AT + NORM_LAG:
                            normalise(l, i, k % 2, n + 1)

            def next_norm(l, i, piece):
                if piece < 2:
                    statistics(l, i, piece, 0)
                else:
                    wait_taken(dve, l, i - 1, "T2", PAIR - 1)
                    normalise(l, i, piece - 2, 0)

            def turn(l, i, more):
                links[0] = FIRST
                where[:] = [l, i]
                for j in range(PAIR):
                    if l > 0:
                        keys(l, i, j)
                    elif j == 0:
                        for part in range(3):
                            rope(l, i, 0, "K", part)
                    values(l, i, j)
                    if l == 0 and j == 0:
                        for part in range(3):
                            rope(l, i, 0, "Q", part)
                attentions(l, i)
                for name, j in tail(l):
                    if name == "OC":
                        residual(l, i, 1, 1, "OC")
                        statistics(l, i, 1, 2)
                        normalise(l, i, 1, 2)
                    elif name == "MO":
                        residual(l, i, j, 2, "MO")
                        if l != 1 and j == 0 and more:
                            for piece in range(4):
                                next_norm(l, i + 1, piece)
                    elif l == 1 and name[0] == "M":
                        hid, m = hidden(j, l), int(name[1:])
                        dve.wait_ge(silu_done.sem, silu_done.of(l, i, j * HT_N + m + 1))
                        b_ = bank_of(l, name, j)
                        c = B1[l] + HT_N + m
                        nc.vector.scalar_tensor_tensor(hid[:, m, :], b_[:, S:2 * S], vec[:, c:c + 1], hid[:, m, :], ALU.add, ALU.mult).then_inc(emptied["V"].sem, 1)
                        if j == 1 and more and m < 4:
                            next_norm(l, i + 1, m)

            def first_norm(l):
                links[0] = 0
                where[:] = [l, 0]
                for j in range(PAIR):
                    statistics(l, 0, j, 0)
                for j in range(PAIR):
                    normalise(l, 0, j, 0)
                assert links[0] == FIRST, links[0]

            for l in range(3):
                first_norm(l)
                with dve.Fori(0, TURNS - 1) as i:
                    turn(l, i, True)
                    LINKS[l] = links[0] - FIRST
                turn(l, TURNS - 1, False)
                layer_done(dve, l + 1)

            l = 3
            dve.wait_ge(s_brow, sum(BROW_N))
            dve.wait_ge(s_pre_empty, KEYS_IN[3] + 1)
            bh = vec[:, VC(3, "e_b1"):VC(3, "e_b1") + M3].unsqueeze(2).to_broadcast([P, M3, B])
            nc.vector.tensor_tensor(anchor[:, :, :], anchor[:, :, :], bh, ALU.add).then_inc(s_anchor, 1)

            def last_layer(l, i, more):
                links[0] = FIRST
                where[:] = [l, i]
                for j in range(PAIR):
                    wait_full(dve, l, i, "S", j)
                    sc = bank_of(l, "S", j)[:, 0:QT * SC].rearrange("p (t k) -> p t k", t=QT)
                    nc.vector.tensor_reduce(nmax[:, j, 0:QT], sc, AX_X, ALU.max, negate=True).then_inc(dve3.sem, 1)
                for j in range(PAIR):
                    wait_taken(dve, l, i, "S", j)
                    link(nc.vector.reciprocal(small[:, j, :, 0], small[:, j, :, 0]))
                    settle()
                    for t in range(QT):
                        p = probs[:, j, t * SC:(t + 1) * SC]
                        last = nc.vector.tensor_scalar(p, p, small[:, j, t, 0:1], None, ALU.mult)
                    last.then_inc(dve3.sem, 1)
                for j in range(PAIR):
                    wait_full(dve, l, i, "RT", j)
                    b_ = bank_of(l, "RT", j)[:, 0:QT * E_N].rearrange("p (t e) -> p t e", t=QT)
                    link(nc.vector.tensor_reduce(nmax[:, 2 + j, 0:QT], b_, AX_X, ALU.max))
                    settle()
                    nc.vector.tensor_tensor(rp[:, j, :, :], b_, nmax[:, 2 + j, 0:QT].unsqueeze(2).to_broadcast([P, QT, E_N]), ALU.subtract).then_inc(emptied["V"].sem, 1)
                for j in range(PAIR):
                    dve.wait_ge(act3.sem, act3.of(l, i, 1 + j))
                    link(nc.vector.reciprocal(small[:, j, :, 1], small[:, j, :, 1]))
                    settle()
                    link(nc.vector.tensor_tensor(rp[:, j, :, :], rp[:, j, :, :], small[:, j, :, 1:2].to_broadcast([P, QT, E_N]), ALU.mult))
                    settle()
                    for t in range(QT):
                        link(nc.vector.tensor_scalar(xh[:, j, t, :], brow[:, 0, :], rp[:, j, t, 0:1], None, ALU.mult))
                    for e in range(1, E_N):
                        settle()
                        for t in range(QT):
                            link(nc.vector.scalar_tensor_tensor(xh[:, j, t, :], brow[:, e, :], rp[:, j, t, e:e + 1], xh[:, j, t, :], ALU.mult, ALU.add))
                settle()
                for j in range(PAIR):
                    for e in range(E_N):
                        wait_full(dve, l, i, f"E{e}", j)
                        b_ = bank_of(l, f"E{e}", j)
                        for t in range(QT):
                            last = nc.vector.scalar_tensor_tensor(xh[:, j, t, :], b_[:, t * D:(t + 1) * D], rp[:, j, t, e:e + 1], xh[:, j, t, :], ALU.mult, ALU.add)
                        last.then_inc(emptied["V"].sem, 1)
                        wait_taken(dve, l, i, f"E{e}", j)
                for j in range(PAIR):
                    wait_full(dve, l, i, "GO", j)
                    g = kT[:, j].rearrange("p c s -> p (c s)").rearrange("p (t d) -> p t d", t=QT)
                    b_ = bank_of(l, "GO", j)[:, :].rearrange("p (t d) -> p t d", t=QT)
                    nc.vector.tensor_tensor(g, b_, brow[:, 3, :].unsqueeze(1).to_broadcast([P, QT, D]), ALU.add).then_inc(emptied["V"].sem, 1)
                if more:
                    for j in range(PAIR):
                        statistics(l, i + 1, j, 0)
                    for j in range(PAIR):
                        wait_taken(dve, l, i, "RR", j)
                        normalise(l, i + 1, j, 0)
                for j in range(PAIR):
                    b = i * PAIR + j
                    g = kT[:, j].rearrange("p c s -> p (c s)").rearrange("p (t d) -> p t d", t=QT)
                    u = probs[:, j, :].rearrange("p (t d) -> p t d", t=QT)
                    dve.wait_ge(act3.sem, act3.of(l, i, 3 + j))
                    link(nc.vector.tensor_scalar(g, g, 1.0, 0.5, ALU.add, ALU.mult))
                    wait_full(dve, l, i, "OUT", j)
                    b_ = bank_of(l, "OUT", j)[:, :].rearrange("p (t d) -> p t d", t=QT)
                    nc.vector.tensor_tensor(u, b_, brow[:, 4, :].unsqueeze(1).to_broadcast([P, QT, D]), ALU.add).then_inc(emptied["V"].sem, 1)
                    settle()
                    wait_taken(dve, l, i, "OUT", j)
                    link(nc.vector.tensor_tensor(u, u, g, ALU.mult))
                    settle()
                    x = X[:, bass.ds(b, 1)].rearrange("p o t d -> p (o t) d")
                    nc.vector.tensor_tensor(x, x, u, ALU.add).then_inc(added.sem, 1)

            first_norm(3)
            with dve.Fori(0, TURNS - 1) as i:
                last_layer(3, i, True)
                LINKS[3] = links[0] - FIRST
            last_layer(3, TURNS - 1, False)
        assert tuple(LINKS[l] for l in range(4)) == DVE_LINKS, LINKS


def kernel(**inputs):
    import numpy as np
    import concourse.bacc as bacc
    from concourse.bass_utils import run_bass_kernel_spmd as run

    nc = bacc.Bacc("TRN2", target_bir_lowering=False, num_devices=1)
    arrays = {}
    for name, x in inputs.items():
        x = np.ascontiguousarray(x)
        arrays[name] = x.reshape(-1).view(np.int32) if x.dtype == np.bool_ else x
    inv = 1.0 / 10000.0 ** (np.arange(0, HD, 2, dtype=np.float32) / HD)
    freqs = np.outer(np.arange(P, dtype=np.float32), inv)
    emb = np.concatenate([freqs, freqs], axis=-1)
    sign = np.where(np.arange(HD) < HD // 2, -1.0, 1.0).astype(np.float32)
    arrays["rope_cos"] = np.ascontiguousarray(np.tile(np.cos(emb).astype(np.float32).T, (HPT, 1)))
    arrays["rope_sin"] = np.ascontiguousarray(np.tile((np.sin(emb).astype(np.float32) * sign).T, (HPT, 1)))
    aps = {n: nc.dram_tensor(f"in_{n}", x.shape, mybir.dt.from_np(x.dtype), kind="ExternalInput").ap() for n, x in arrays.items()}
    out = nc.dram_tensor("out", (B, S, D), F32, kind="ExternalOutput").ap()
    build(nc, aps, out)
    r = run(nc, [{f"in_{n}": x for n, x in arrays.items()}], core_ids=[0])
    return r.results[0]["out"]
```
